# Optimizing a Trainium2 kernel written in Bass

```python
import numpy as np
import jax
import jax.numpy as jnp

def _softmax(x, axis=-1):
    return jax.nn.softmax(x, axis=axis)

def _gelu(x):
    return jax.nn.gelu(x, approximate=True)

def _silu(x):
    return jax.nn.silu(x)

def _sigmoid(x):
    return jax.nn.sigmoid(x)

def _layernorm(x, axis=-1, eps=1e-05):
    m = jnp.mean(x, axis=axis, keepdims=True)
    v = jnp.var(x, axis=axis, keepdims=True)
    return (x - m) / jnp.sqrt(v + eps)

def _scatter_add(tgt, idx, src, axis=0):
    return tgt.at[idx].add(src)

def _segment_sum(src, seg, n):
    return jax.ops.segment_sum(src, seg, n)
kernel_name = 'mk_gnn_preln_d4_gnn_r8_2d5fc3'

def setup_inputs(seed: int=0):
    np.random.seed(seed)
    _w = jnp.asarray

    def _rec_inputs():
        import jax
        import jax.numpy as jnp
        _gk = jax.random.key(seed)
        x = -0.0005121 + 1.001 * jax.random.normal(jax.random.fold_in(_gk, 1), (6250, 64), jnp.float32)
        src = jax.random.randint(jax.random.fold_in(_gk, 2), (200000,), 0, 6250, jnp.int32)
        dst = jax.random.randint(jax.random.fold_in(_gk, 3), (200000,), 0, 6250, jnp.int32)
        _o = jnp.argsort(dst, stable=True)
        src = src[_o]
        dst = dst[_o]
        edge_attr_32 = -8.62073e-06 + 0.999901 * jax.random.normal(jax.random.fold_in(_gk, 12), (200000, 32), jnp.float32)
        return (x, src, dst, edge_attr_32)
    x, src, dst, edge_attr_32 = _rec_inputs()

    def _L0_gnn_setup():
        import jax, jax.numpy as jnp
        import numpy as np
        N_NODES = 6250

        def gcn_conv(x, src, dst, W, b):
            n = x.shape[0]
            ones = jnp.ones(src.shape[0], dtype=x.dtype)
            deg_out = jax.ops.segment_sum(ones, src, num_segments=n)
            deg_in = jax.ops.segment_sum(ones, dst, num_segments=n)
            norm_out = jnp.clip(deg_out, 1.0, None) ** (-0.5)
            norm_in = jnp.clip(deg_in, 1.0, None) ** (-0.5)
            h = x * norm_out[:, None]
            msgs = h[src]
            agg = jax.ops.segment_sum(msgs, dst, num_segments=n)
            agg = agg * norm_in[:, None]
            return agg @ W + b
        key = jax.random.key(seed)
        k1, k2, k3, k4, k5, k6, k7 = jax.random.split(key, 7)
        in_f, hid_f, out_f = (64, 64, 64)
        E = 100000
        x = jax.random.normal(k1, (N_NODES, in_f), dtype=jnp.float32)
        src = jax.random.randint(k2, (E,), 0, N_NODES)
        dst = jax.random.randint(k3, (E,), 0, N_NODES)
        s1 = 1.0 / np.sqrt(in_f)
        s2 = 1.0 / np.sqrt(hid_f)
        W1 = jax.random.uniform(k4, (in_f, hid_f), jnp.float32, -s1, s1)
        b1 = jnp.zeros((hid_f,), jnp.float32)
        W2 = jax.random.uniform(k5, (hid_f, out_f), jnp.float32, -s2, s2)
        b2 = jnp.zeros((out_f,), jnp.float32)
        return {'x': x, 'src': src, 'dst': dst, 'W1': W1, 'b1': b1, 'W2': W2, 'b2': b2}
    _L0_gnn_all = _L0_gnn_setup()
    _L0_gnn_in = {k: v for k, v in _L0_gnn_all.items() if k in ('W1', 'b1', 'W2', 'b2')}
    del _L0_gnn_all

    def _L1_gnn_setup():
        import jax, jax.numpy as jnp
        import numpy as np
        N_NODES = 6250
        N_EDGES = 150000
        D_FEAT = 64
        EMBED = 64
        H = 1
        HEAD_DIM = EMBED // H

        def mish(x):
            return x * jnp.tanh(jax.nn.softplus(x))
        key = jax.random.key(seed)
        ks = jax.random.split(key, 12)
        nodes = jax.random.normal(ks[0], (N_NODES, D_FEAT), dtype=jnp.float32)
        senders = jax.random.randint(ks[1], (N_EDGES,), 0, N_NODES, dtype=jnp.int32)
        receivers = jax.random.randint(ks[2], (N_EDGES,), 0, N_NODES, dtype=jnp.int32)
        s = 0.05
        We_k = jax.random.normal(ks[3], (D_FEAT, H, HEAD_DIM), dtype=jnp.float32) * s
        We_b = jnp.zeros((H, HEAD_DIM), dtype=jnp.float32)
        Ws_k = jax.random.normal(ks[4], (HEAD_DIM, EMBED), dtype=jnp.float32) * s
        Ws_b = jnp.zeros((EMBED,), dtype=jnp.float32)
        Wr_k = jax.random.normal(ks[5], (D_FEAT, H, HEAD_DIM), dtype=jnp.float32) * s
        Wr_b = jnp.zeros((H, HEAD_DIM), dtype=jnp.float32)
        Wa_k = jax.random.normal(ks[6], (EMBED, 1), dtype=jnp.float32) * s
        Wa_b = jnp.zeros((1,), dtype=jnp.float32)
        return {'nodes': nodes, 'senders': senders, 'receivers': receivers, 'We_k': We_k, 'We_b': We_b, 'Ws_k': Ws_k, 'Ws_b': Ws_b, 'Wr_k': Wr_k, 'Wr_b': Wr_b, 'Wa_k': Wa_k, 'Wa_b': Wa_b}
    _L1_gnn_all = _L1_gnn_setup()
    _L1_gnn_in = {k: v for k, v in _L1_gnn_all.items() if k in ('We_k', 'We_b', 'Ws_k', 'Ws_b', 'Wr_k', 'Wr_b', 'Wa_k', 'Wa_b')}
    del _L1_gnn_all

    def _L2_gnn_setup():
        import jax, jax.numpy as jnp
        import numpy as np
        N_NODES = 12500
        ALPHA = 0.5

        def mean_agg(x, idx_from, idx_to, n):
            s = jax.ops.segment_sum(x[idx_from], idx_to, num_segments=n)
            cnt = jax.ops.segment_sum(jnp.ones((idx_to.shape[0],), x.dtype), idx_to, num_segments=n)
            return s / jnp.maximum(cnt, 1.0)[:, None]

        def dir_sage_conv(x, src, dst, w_self, b_self, w_s2d, b_s2d, w_d2s, b_d2s):
            n = x.shape[0]
            agg_in = mean_agg(x, src, dst, n)
            agg_out = mean_agg(x, dst, src, n)
            return x @ w_self + b_self + (1.0 - ALPHA) * (agg_in @ w_s2d + b_s2d) + ALPHA * (agg_out @ w_d2s + b_d2s)
        key = jax.random.key(seed)
        ks = jax.random.split(key, 16)
        d_in, d_hid, d_out = (64, 64, 64)
        n_edges = 200000
        x = jax.random.normal(ks[0], (N_NODES, d_in), dtype=jnp.float32)
        edge_index = jax.random.randint(ks[1], (2, n_edges), 0, N_NODES, dtype=jnp.int64)

        def lin(k, din, dout):
            s = 1.0 / np.sqrt(din)
            kw, kb = jax.random.split(k)
            return (jax.random.uniform(kw, (din, dout), jnp.float32, -s, s), jax.random.uniform(kb, (dout,), jnp.float32, -s, s))
        w_self1, b_self1 = lin(ks[2], d_in, d_hid)
        w_s2d1, b_s2d1 = lin(ks[3], d_in, d_hid)
        w_d2s1, b_d2s1 = lin(ks[4], d_in, d_hid)
        w_self2, b_self2 = lin(ks[5], d_hid, d_out)
        w_s2d2, b_s2d2 = lin(ks[6], d_hid, d_out)
        w_d2s2, b_d2s2 = lin(ks[7], d_hid, d_out)
        return {'x': x, 'edge_index': edge_index, 'w_self1': w_self1, 'b_self1': b_self1, 'w_s2d1': w_s2d1, 'b_s2d1': b_s2d1, 'w_d2s1': w_d2s1, 'b_d2s1': b_d2s1, 'w_self2': w_self2, 'b_self2': b_self2, 'w_s2d2': w_s2d2, 'b_s2d2': b_s2d2, 'w_d2s2': w_d2s2, 'b_d2s2': b_d2s2}
    _L2_gnn_all = _L2_gnn_setup()
    _L2_gnn_in = {k: v for k, v in _L2_gnn_all.items() if k in ('w_self1', 'b_self1', 'w_s2d1', 'b_s2d1', 'w_d2s1', 'b_d2s1', 'w_self2', 'b_self2', 'w_s2d2', 'b_s2d2', 'w_d2s2', 'b_d2s2')}
    del _L2_gnn_all

    def _L3_gnn_setup():
        import jax, jax.numpy as jnp
        import numpy as np
        N_NODES = 12500
        N_EDGES = 125000
        NODE_DIM = 64
        EDGE_DIM = 32
        EPS = 1e-05
        SLOPE = 0.1

        def _mlp2(v, W1, b1, W2, b2):
            h = jax.nn.leaky_relu(v @ W1 + b1, negative_slope=SLOPE)
            return h @ W2 + b2
        key = jax.random.key(seed)
        ks = jax.random.split(key, 8)
        s = 0.05
        return {'x': jax.random.normal(ks[0], (N_NODES, NODE_DIM), dtype=jnp.float32), 'edge_attr': jax.random.normal(ks[1], (N_EDGES, EDGE_DIM), dtype=jnp.float32), 'W1n': jax.random.normal(ks[2], (NODE_DIM, 2 * NODE_DIM), dtype=jnp.float32) * s, 'b1n': jnp.zeros((2 * NODE_DIM,), dtype=jnp.float32), 'W2n': jax.random.normal(ks[3], (2 * NODE_DIM, NODE_DIM), dtype=jnp.float32) * s, 'b2n': jnp.zeros((NODE_DIM,), dtype=jnp.float32), 'W1e': jax.random.normal(ks[4], (EDGE_DIM, NODE_DIM), dtype=jnp.float32) * s, 'b1e': jnp.zeros((NODE_DIM,), dtype=jnp.float32), 'W2e': jax.random.normal(ks[5], (NODE_DIM, NODE_DIM), dtype=jnp.float32) * s, 'b2e': jnp.zeros((NODE_DIM,), dtype=jnp.float32), 'res_w': jnp.ones((1,), dtype=jnp.float32), 'dp_scale': jnp.ones((1,), dtype=jnp.float32), 'gamma': jnp.ones((NODE_DIM,), dtype=jnp.float32), 'beta': jnp.zeros((NODE_DIM,), dtype=jnp.float32), 'edge_index': jax.random.randint(ks[6], (2, N_EDGES), 0, N_NODES, dtype=jnp.int64) if jax.config.jax_enable_x64 else jax.random.randint(ks[6], (2, N_EDGES), 0, N_NODES, dtype=jnp.int32)}
    _L3_gnn_all = _L3_gnn_setup()
    _L3_gnn_in = {k: v for k, v in _L3_gnn_all.items() if k in ('W1n', 'b1n', 'W2n', 'b2n', 'W1e', 'b1e', 'W2e', 'b2e', 'res_w', 'dp_scale', 'gamma', 'beta')}
    del _L3_gnn_all
    return {'x': x, 'src': src, 'dst': dst, 'edge_attr_32': edge_attr_32, 'L0_gnn_W1': _L0_gnn_in['W1'], 'L0_gnn_b1': _L0_gnn_in['b1'], 'L0_gnn_W2': _L0_gnn_in['W2'], 'L0_gnn_b2': _L0_gnn_in['b2'], 'L1_gnn_We_k': _L1_gnn_in['We_k'], 'L1_gnn_We_b': _L1_gnn_in['We_b'], 'L1_gnn_Ws_k': _L1_gnn_in['Ws_k'], 'L1_gnn_Ws_b': _L1_gnn_in['Ws_b'], 'L1_gnn_Wr_k': _L1_gnn_in['Wr_k'], 'L1_gnn_Wr_b': _L1_gnn_in['Wr_b'], 'L1_gnn_Wa_k': _L1_gnn_in['Wa_k'], 'L1_gnn_Wa_b': _L1_gnn_in['Wa_b'], 'L2_gnn_w_self1': _L2_gnn_in['w_self1'], 'L2_gnn_b_self1': _L2_gnn_in['b_self1'], 'L2_gnn_w_s2d1': _L2_gnn_in['w_s2d1'], 'L2_gnn_b_s2d1': _L2_gnn_in['b_s2d1'], 'L2_gnn_w_d2s1': _L2_gnn_in['w_d2s1'], 'L2_gnn_b_d2s1': _L2_gnn_in['b_d2s1'], 'L2_gnn_w_self2': _L2_gnn_in['w_self2'], 'L2_gnn_b_self2': _L2_gnn_in['b_self2'], 'L2_gnn_w_s2d2': _L2_gnn_in['w_s2d2'], 'L2_gnn_b_s2d2': _L2_gnn_in['b_s2d2'], 'L2_gnn_w_d2s2': _L2_gnn_in['w_d2s2'], 'L2_gnn_b_d2s2': _L2_gnn_in['b_d2s2'], 'L3_gnn_W1n': _L3_gnn_in['W1n'], 'L3_gnn_b1n': _L3_gnn_in['b1n'], 'L3_gnn_W2n': _L3_gnn_in['W2n'], 'L3_gnn_b2n': _L3_gnn_in['b2n'], 'L3_gnn_W1e': _L3_gnn_in['W1e'], 'L3_gnn_b1e': _L3_gnn_in['b1e'], 'L3_gnn_W2e': _L3_gnn_in['W2e'], 'L3_gnn_b2e': _L3_gnn_in['b2e'], 'L3_gnn_res_w': _L3_gnn_in['res_w'], 'L3_gnn_dp_scale': _L3_gnn_in['dp_scale'], 'L3_gnn_gamma': _L3_gnn_in['gamma'], 'L3_gnn_beta': _L3_gnn_in['beta']}

def reference(x, src, dst, edge_attr_32, L0_gnn_W1, L0_gnn_b1, L0_gnn_W2, L0_gnn_b2, L1_gnn_We_k, L1_gnn_We_b, L1_gnn_Ws_k, L1_gnn_Ws_b, L1_gnn_Wr_k, L1_gnn_Wr_b, L1_gnn_Wa_k, L1_gnn_Wa_b, L2_gnn_w_self1, L2_gnn_b_self1, L2_gnn_w_s2d1, L2_gnn_b_s2d1, L2_gnn_w_d2s1, L2_gnn_b_d2s1, L2_gnn_w_self2, L2_gnn_b_self2, L2_gnn_w_s2d2, L2_gnn_b_s2d2, L2_gnn_w_d2s2, L2_gnn_b_d2s2, L3_gnn_W1n, L3_gnn_b1n, L3_gnn_W2n, L3_gnn_b2n, L3_gnn_W1e, L3_gnn_b1e, L3_gnn_W2e, L3_gnn_b2e, L3_gnn_res_w, L3_gnn_dp_scale, L3_gnn_gamma, L3_gnn_beta):
    import jax
    import jax.numpy as jnp

    def _L0_gnn_ref(x, src, dst, W1, b1, W2, b2):
        import jax, jax.numpy as jnp
        import numpy as np
        N_NODES = 6250

        def gcn_conv(x, src, dst, W, b):
            n = x.shape[0]
            ones = jnp.ones(src.shape[0], dtype=x.dtype)
            deg_out = jax.ops.segment_sum(ones, src, num_segments=n)
            deg_in = jax.ops.segment_sum(ones, dst, num_segments=n)
            norm_out = jnp.clip(deg_out, 1.0, None) ** (-0.5)
            norm_in = jnp.clip(deg_in, 1.0, None) ** (-0.5)
            h = x * norm_out[:, None]
            msgs = h[src]
            agg = jax.ops.segment_sum(msgs, dst, num_segments=n)
            agg = agg * norm_in[:, None]
            return agg @ W + b
        h = jax.nn.relu(gcn_conv(x, src, dst, W1, b1))
        h = gcn_conv(h, src, dst, W2, b2)
        return h

    def _L1_gnn_ref(nodes, senders, receivers, We_k, We_b, Ws_k, Ws_b, Wr_k, Wr_b, Wa_k, Wa_b):
        import jax, jax.numpy as jnp
        import numpy as np
        N_NODES = 6250
        N_EDGES = 150000
        D_FEAT = 64
        EMBED = 64
        H = 1
        HEAD_DIM = EMBED // H

        def mish(x):
            return x * jnp.tanh(jax.nn.softplus(x))
        n = nodes.shape[0]
        sent = nodes[senders]
        edges = jnp.einsum('ef,fhd->ehd', sent, We_k) + We_b
        recv = nodes[receivers]
        s_att = jnp.einsum('ehd,dm->ehm', edges, Ws_k) + Ws_b
        r_att = jnp.einsum('ef,fhd->ehd', recv, Wr_k) + Wr_b
        x = mish(s_att + r_att)
        logits = jnp.einsum('ehm,mo->eho', x, Wa_k) + Wa_b
        seg_max = jax.ops.segment_max(logits, receivers, num_segments=n)
        seg_max = jnp.where(jnp.isfinite(seg_max), seg_max, 0.0)
        unnorm = jnp.exp(logits - seg_max[receivers])
        denom = jax.ops.segment_sum(unnorm, receivers, num_segments=n)
        weights = unnorm / denom[receivers]
        msg = (weights * edges).reshape(edges.shape[0], H * HEAD_DIM)
        out_nodes = jax.ops.segment_sum(msg, receivers, num_segments=n)
        return out_nodes

    def _L2_gnn_ref(x, edge_index, w_self1, b_self1, w_s2d1, b_s2d1, w_d2s1, b_d2s1, w_self2, b_self2, w_s2d2, b_s2d2, w_d2s2, b_d2s2):
        import jax, jax.numpy as jnp
        import numpy as np
        N_NODES = 12500
        ALPHA = 0.5

        def mean_agg(x, idx_from, idx_to, n):
            s = jax.ops.segment_sum(x[idx_from], idx_to, num_segments=n)
            cnt = jax.ops.segment_sum(jnp.ones((idx_to.shape[0],), x.dtype), idx_to, num_segments=n)
            return s / jnp.maximum(cnt, 1.0)[:, None]

        def dir_sage_conv(x, src, dst, w_self, b_self, w_s2d, b_s2d, w_d2s, b_d2s):
            n = x.shape[0]
            agg_in = mean_agg(x, src, dst, n)
            agg_out = mean_agg(x, dst, src, n)
            return x @ w_self + b_self + (1.0 - ALPHA) * (agg_in @ w_s2d + b_s2d) + ALPHA * (agg_out @ w_d2s + b_d2s)
        src, dst = (edge_index[0], edge_index[1])
        h = dir_sage_conv(x, src, dst, w_self1, b_self1, w_s2d1, b_s2d1, w_d2s1, b_d2s1)
        h = jax.nn.relu(h)
        out = dir_sage_conv(h, src, dst, w_self2, b_self2, w_s2d2, b_s2d2, w_d2s2, b_d2s2)
        return out

    def _L3_gnn_ref(x, edge_attr, W1n, b1n, W2n, b2n, W1e, b1e, W2e, b2e, res_w, dp_scale, gamma, beta, edge_index):
        import jax, jax.numpy as jnp
        import numpy as np
        N_NODES = 12500
        N_EDGES = 125000
        NODE_DIM = 64
        EDGE_DIM = 32
        EPS = 1e-05
        SLOPE = 0.1

        def _mlp2(v, W1, b1, W2, b2):
            h = jax.nn.leaky_relu(v @ W1 + b1, negative_slope=SLOPE)
            return h @ W2 + b2
        num_nodes = x.shape[0]
        x_t = _mlp2(x, W1n, b1n, W2n, b2n)
        e_t = _mlp2(edge_attr, W1e, b1e, W2e, b2e)
        src, dst = (edge_index[0], edge_index[1])
        msgs = x_t[src] * e_t * dp_scale
        aggregated = jax.ops.segment_sum(msgs, dst, num_segments=num_nodes)
        out = x + aggregated * res_w
        mu = jnp.mean(out, axis=-1, keepdims=True)
        var = jnp.mean(jnp.square(out - mu), axis=-1, keepdims=True)
        return (out - mu) * jax.lax.rsqrt(var + EPS) * gamma + beta
    edge_index = jnp.stack([src, dst])
    h = jnp.maximum(_layernorm(x, axis=-1), 0.0)
    x = x + _L0_gnn_ref(h, src, dst, L0_gnn_W1, L0_gnn_b1, L0_gnn_W2, L0_gnn_b2)
    h = jnp.maximum(_layernorm(x, axis=-1), 0.0)
    x = x + _L1_gnn_ref(h, src, dst, L1_gnn_We_k, L1_gnn_We_b, L1_gnn_Ws_k, L1_gnn_Ws_b, L1_gnn_Wr_k, L1_gnn_Wr_b, L1_gnn_Wa_k, L1_gnn_Wa_b)
    h = jnp.maximum(_layernorm(x, axis=-1), 0.0)
    x = x + _L2_gnn_ref(h, edge_index, L2_gnn_w_self1, L2_gnn_b_self1, L2_gnn_w_s2d1, L2_gnn_b_s2d1, L2_gnn_w_d2s1, L2_gnn_b_d2s1, L2_gnn_w_self2, L2_gnn_b_self2, L2_gnn_w_s2d2, L2_gnn_b_s2d2, L2_gnn_w_d2s2, L2_gnn_b_d2s2)
    h = jnp.maximum(_layernorm(x, axis=-1), 0.0)
    x = x + _L3_gnn_ref(h, edge_attr_32, L3_gnn_W1n, L3_gnn_b1n, L3_gnn_W2n, L3_gnn_b2n, L3_gnn_W1e, L3_gnn_b1e, L3_gnn_W2e, L3_gnn_b2e, L3_gnn_res_w, L3_gnn_dp_scale, L3_gnn_gamma, L3_gnn_beta, edge_index)
    return x

_drawn_inputs = setup_inputs


def setup_inputs(seed=0):
    import zlib

    import numpy as np

    out = dict(_drawn_inputs(seed))
    spreads = {'L0_gnn_b1': (0.0, 0.1),
     'L0_gnn_b2': (0.0, 0.1),
     'L1_gnn_We_b': (0.0, 0.1),
     'L1_gnn_Ws_b': (0.0, 0.8),
     'L1_gnn_Wr_b': (0.0, 0.8),
     'L3_gnn_b1n': (0.0, 0.1),
     'L3_gnn_b2n': (0.0, 0.1),
     'L3_gnn_b1e': (0.0, 0.1),
     'L3_gnn_b2e': (0.0, 0.1),
     'L3_gnn_gamma': (1.0, 0.2),
     'L3_gnn_beta': (0.0, 0.1)}
    factors = {'L1_gnn_Ws_k': 8.0,
     'L1_gnn_Wr_k': 8.0,
     'L1_gnn_Wa_k': 8.0,
     'L2_gnn_b_s2d1': 3.816,
     'L2_gnn_b_d2s1': 3.614}
    for name, (base, spread) in spreads.items():
        noise = np.random.default_rng([zlib.crc32(name.encode()), seed]).standard_normal(out[name].shape)
        drawn = base * np.exp(spread * noise) if base else spread * noise
        out[name] = jnp.asarray(drawn.astype(out[name].dtype))
    for name, factor in factors.items():
        out[name] = (out[name] * factor).astype(out[name].dtype)
    return out
```

```python
from contextlib import ExitStack

import concourse.bass as bass
from concourse import mybir

ALU = mybir.AluOpType
ACT = mybir.ActivationFunctionType
AX_X = mybir.AxisListType.X
F32 = mybir.dt.float32
BF16 = mybir.dt.bfloat16
I32 = mybir.dt.int32

P = 128
N_NODES, D, E_EDGES, DE = 6250, 64, 200000, 32
NT = 49
NP = NT * P
NB = 7
NBLK = NT // NB
BW = NB * P
HW = BW // 2
GT = 8
GE = GT * P
G = -(-E_EDGES // GE)
EP = G * GE
T = G * GT
GH = G // 2
SHIFT = 13
PITCH = 1 << SHIFT
TAG = 0x40000000
LESS = 2048.0
EPS = 1e-5
BIG = 1e30
assert NP >= N_NODES and G % 2 == 0 and GE + NP <= PITCH and LESS > GE


class Steps:

    def __init__(self, eng, sem, base=0, turn=0, per=0):
        self.eng, self.sem, self.base, self.turn, self.per, self.n = eng, sem, base, turn, per, 0

    def did(self, instruction, by=1):
        instruction.then_inc(self.sem, by)
        self.n += by

    def wait(self):
        self.eng.wait_ge(self.sem, self.turn * self.per + self.base + self.n)

    def link(self, instruction):
        self.did(instruction)
        self.wait()


def prefetch_row(dram, row, width):
    return dram.rearrange("(a n) -> a n", a=1)[:, bass.ds(row, width)].to_broadcast([P, width])


def build_program(nc, a, out, dbg):
    top = ExitStack()

    passing = {"scope": ExitStack(), "numbers": []}

    def sem(name, keep=False):
        if keep:
            return top.enter_context(nc.semaphore(name))
        handle = passing["scope"].enter_context(nc.semaphore(name))
        passing["numbers"].append(handle)
        return handle

    def end_phase():
        numbers = sorted(h.num for h in passing["numbers"])
        while numbers:
            n = 1
            while n < len(numbers) and numbers[n] == numbers[0] + n:
                n += 1
            nc.gpsimd.sem_clear(range(numbers[0], numbers[0] + n))
            numbers = numbers[n:]
        nc.all_engine_barrier()
        passing["scope"].close()
        passing["scope"], passing["numbers"] = ExitStack(), []

    def dram(name, shape, dt):
        return nc.dram_tensor(name, shape, dt).ap()

    key_d = dram("key_d", (EP,), I32)
    dstf_d = dram("dstf_d", (EP + 2,), F32)
    adj_d = dram("adj_d", (NP * PITCH, 1), BF16)
    adjT_d = dram("adjT_d", (NP, NP), BF16)
    adj_rows = adj_d.rearrange("(d s) o -> d (s o)", s=PITCH)
    send_d = dram("send_d", (NP, 2 * D), F32)
    recv_d = dram("recv_d", (NP, D), F32)
    recvz_d = dram("recvz_d", (EP + NP, D), F32)
    emb_d = dram("emb_d", (G, P, GT * D), F32)
    part_d = dram("part_d", (EP, D), F32)
    xt_d = dram("xt_d", (NP, D), F32)
    lin_d = dram("lin_d", (EP,), F32)
    wgt_d = dram("wgt_d", (EP,), F32)

    def keep(name, shape, dt):
        return top.enter_context(nc.sbuf_tensor(name, shape, dt))

    x_sb = keep("x_sb", [P, NT, D], F32)
    y_sb = keep("y_sb", [P, NT, D], F32)
    h_sb = keep("h_sb", [P, NT, D], F32)
    t_sb = keep("t_sb", [P, NT, D], F32)
    h3 = keep("h3", [P, NT, 3 * D], BF16)
    src_c = keep("src_c", [P, T], I32)
    dst_c = keep("dst_c", [P, T], F32)
    ident = keep("ident", [P, P], F32)
    identb = keep("identb", [P, P], BF16)
    deg_in = keep("deg_in", [P, NT], F32)
    deg_out = keep("deg_out", [P, NT], F32)
    norm_in = keep("norm_in", [P, NT], F32)
    norm_out = keep("norm_out", [P, NT], F32)
    half_in = keep("half_in", [P, NT], F32)
    half_out = keep("half_out", [P, NT], F32)
    end_row = keep("end_row", [P, NT], I32)
    start_row = keep("start_row", [P, NT], I32)
    own_end = keep("own_end", [P, NT], F32)
    first_id = keep("first_id", [P, 2, GT], I32)
    last_id = keep("last_id", [P, 2, GT], F32)

    with ExitStack() as c:
        def sb(name, shape, dt):
            return c.enter_context(nc.sbuf_tensor(name, shape, dt))
        dst_ci = sb("dst_ci", [P, T], I32)
        lin_s = sb("lin_s", [P, T], I32)
        lin_t = sb("lin_t", [P, T], I32)
        key_l = sb("key_l", [P, T], I32)
        key_k = sb("key_k", [P, T], I32)
        dstf_l = sb("dstf_l", [P, T], F32)
        minus1 = sb("minus1", [P, 2], F32)
        zero_b = sb("zero_b", [P, NP], BF16)
        firsts = sb("firsts", [P, 2, GT], F32)
        ld, st, zr, vs, ids, st2 = (sem(n) for n in ("p_load", "p_store", "p_zeroed", "p_dve", "p_ident", "p_bounds"))
        with nc.Block() as block:
            @block.sync
            def _(sp):
                sp.dma_start(lin_s[:], a["src_lin"]).then_inc(ld, 16)
                sp.dma_start(lin_t[:], a["dst_lin"]).then_inc(ld, 16)
                sp.dma_start(src_c[:], a["src_col"]).then_inc(ld, 16)
                sp.dma_start(dst_ci[:], a["dst_col"]).then_inc(ld, 16)
                sp.dma_start(x_sb[:], a["x"].rearrange("(t p) d -> p t d", p=P)).then_inc(ld, 16)
                sp.wait_ge(vs, 6)
                sp.dma_start(key_d.rearrange("(p j) -> p j", p=P), key_l[:]).then_inc(st, 16)
                sp.dma_start(dstf_d[1:EP + 1].rearrange("(p j) -> p j", p=P), dstf_l[:]).then_inc(st, 16)
                sp.dma_start(dstf_d[0:1].rearrange("(a j) -> a j", a=1), minus1[0:1, 0:1]).then_inc(st, 16)
                sp.dma_start(dstf_d[EP + 1:EP + 2].rearrange("(a j) -> a j", a=1), minus1[0:1, 1:2]).then_inc(st, 16)
                sp.wait_ge(st, 64)
                ends = dstf_d[1:EP + 1].rearrange("(h g k p) -> g h k p", h=2, k=GT, p=P)
                with nc.allow_non_contiguous_dma(reason="one number of each tile"):
                    for h in range(2):
                        sp.dma_start(firsts[0:GH, h, :], ends[:, h, :, 0]).then_inc(st2, 16)
                        sp.dma_start(last_id[0:GH, h, :], ends[:, h, :, P - 1]).then_inc(st2, 16)
                sp.wait_ge(st2, 64)
                sp.wait_ge(ld, 80)

            @block.scalar
            def _(act):
                act.wait_ge(vs, 1)
                with act.Fori(0, NT) as i:
                    act.dma_start(adj_rows[bass.ds(i * P, P), 0:NP], zero_b[:]).then_inc(zr, 16)
                act.dma_start(adj_rows[0:1, NP:NP + GE], zero_b[0:1, 0:GE]).then_inc(zr, 16)
                act.wait_ge(zr, 16 * (NT + 1))

            @block.gpsimd
            def _(pool):
                nc.gpsimd.memset(ident[:], 0.0).then_inc(ids, 1)
                pool.wait_ge(ids, 1)
                nc.gpsimd.affine_select(out=ident[:], in_=ident[:], compare_op=ALU.not_equal, fill=1.0, base=0,
                                        pattern=[[-1, P]], channel_multiplier=1).then_inc(ids, 1)

            @block.vector
            def _(dve):
                s = Steps(dve, vs)
                s.did(nc.vector.memset(zero_b[:], 0.0))
                s.did(nc.vector.memset(minus1[:], -1.0))
                dve.wait_ge(ld, 80)
                s.link(nc.vector.tensor_scalar(key_k[:], lin_t[:], SHIFT, TAG, ALU.logical_shift_left, ALU.bitwise_or))
                s.did(nc.vector.tensor_tensor(key_l[:], key_k[:], lin_s[:], ALU.bitwise_or))
                s.did(nc.vector.tensor_copy(dstf_l[:], lin_t[:]))
                s.did(nc.vector.tensor_copy(dst_c[:], dst_ci[:]))
                dve.wait_ge(ids, 2)
                s.did(nc.vector.tensor_copy(identb[:], ident[:]))
                dve.wait_ge(st2, 64)
                s.did(nc.vector.tensor_copy(first_id[0:GH], firsts[0:GH]))

    end_phase()
    with ExitStack() as c:
        def sb(name, shape, dt):
            return c.enter_context(nc.sbuf_tensor(name, shape, dt))
        key_row = sb("key_row", [P, 2, GE], I32)
        key_c = sb("key_c", [P, T], I32)
        key_ck = sb("key_ck", [P, T], I32)
        dst_k = sb("dst_k", [P, T], I32)
        earlier = sb("earlier", [P, 2 * GE - P], F32)
        junk = sb("junk", [P, GT, GE], BF16)
        tally = sb("tally", [P, 2, GT], F32)
        again = sb("again", [P, 2, GT], I32)
        slot = sb("slot", [P, 2, GT], I32)
        count = sb("count", [P, 2, GT], BF16)
        dump = sb("dump", [P, 2, GT], I32)
        zero_f = sb("zero_f", [P, 8 * GT * D], F32)
        ld0, vs0 = sem("b_load0"), sem("b_dve0")
        rows = [sem("b_row0"), sem("b_row1")]
        pool0, zr2 = sem("b_pool0"), sem("b_zeroed")
        vs1, landed, ready = sem("b_dve"), sem("b_landed", keep=True), sem("b_ready")
        with nc.Block() as block:
            @block.sync
            def _(sp):
                sp.dma_start(dst_k[:], a["dst_col"]).then_inc(ld0, 16)
                for b in range(2):
                    sp.dma_start(key_row[:, b, :], prefetch_row(key_d, b * GE, GE)).then_inc(rows[b], 16)
                with sp.Fori(1, G // 2) as i:
                    for b in range(2):
                        sp.wait_ge(ready, i * 2 + (b - 1))
                        sp.dma_start(key_row[:, b, :], prefetch_row(key_d, (i * 2 + b) * GE, GE)).then_inc(rows[b], 16)
                for b in range(2):
                    sp.wait_ge(rows[b], 16 * (G // 2))

            @block.scalar
            def _(act):
                act.wait_ge(vs0, 4)
                zrows = (EP + NP) // P
                zv = recvz_d.rearrange("(p r) d -> p (r d)", p=P)
                step = 8 * GT
                n = 0
                for r in range(0, zrows, step):
                    w = min(step, zrows - r)
                    act.dma_start(zv[:, r * D:(r + w) * D], zero_f[:, 0:w * D]).then_inc(zr2, 16)
                    n += 1
                act.wait_ge(zr2, 16 * n)

            @block.vector
            def _(dve):
                s = Steps(dve, vs0)
                dve.wait_ge(ld0, 16)
                s.link(nc.vector.tensor_scalar(key_ck[:], dst_k[:], SHIFT, TAG, ALU.logical_shift_left, ALU.bitwise_or))
                s.did(nc.vector.tensor_tensor(key_c[:], key_ck[:], src_c[:], ALU.bitwise_or))
                s.did(nc.vector.memset(earlier[:], 1.0))
                s.link(nc.vector.memset(zero_f[:], 0.0))
                dve.wait_ge(pool0, 2)
                def turn(i, first):
                    t = Steps(dve, vs1, turn=i, per=5 * 2)
                    for b in range(2):
                        dve.wait_ge(rows[b], i * 16 + 16)
                        for k in range(GT):
                            col = bass.ds((i * 2 + b) * GT + k, 1)
                            w = earlier[:, GE - P - k * P:2 * GE - P - k * P]
                            last = nc.vector.scalar_tensor_tensor(
                                out=junk[:, k, :], in0=key_row[:, b, :].bitcast(F32), scalar=key_c[:, col].bitcast(F32),
                                in1=w, op0=ALU.is_equal, op1=ALU.mult, accum_out=tally[:, b, k:k + 1])
                        t.link(last)
                        t.did(nc.vector.tensor_scalar(again[:, b, :], tally[:, b, :], LESS, None, ALU.is_ge))
                        if not first:
                            dve.wait_ge(landed, (i * 2 + (b - 1)) * 16 * GT)
                        t.did(nc.vector.tensor_copy(count[:, b, :], tally[:, b, :]))
                        t.link(nc.vector.tensor_scalar(slot[:, b, :], key_c[:, bass.ds((i * 2 + b) * GT, GT)], TAG - 1, None,
                                                       ALU.bitwise_and))
                        dve.nop(nofuse=True)
                        t.did(nc.vector.copy_predicated(slot[:, b, :], again[:, b, :], dump[:, b, :]))
                        t.wait()
                        dve.sem_inc(ready, 1)

                turn(0, True)
                with dve.Fori(1, G // 2) as i:
                    turn(i, False)

            @block.gpsimd
            def _(pool):
                pool.wait_ge(vs0, 3)
                nc.gpsimd.affine_select(out=earlier[:], in_=earlier[:], compare_op=ALU.is_ge, fill=1.0 + LESS,
                                        base=-(GE - P), pattern=[[1, 2 * GE - P]],
                                        channel_multiplier=-1).then_inc(pool0, 1)
                nc.gpsimd.iota(dump[:], pattern=[[0, 2], [P, GT]], base=NP, channel_multiplier=1).then_inc(pool0, 1)
                def turn(i, first):
                    for b in range(2):
                        pool.wait_ge(ready, i * 2 + (b + 1))
                        pool.nop(nofuse=True)
                        if not (first and b == 0):
                            pool.wait_ge(landed, (i * 2 + b) * 16 * GT)
                            pool.nop(nofuse=True)
                        for k in range(GT):
                            nc.gpsimd.indirect_dma_start(
                                adj_d, bass.IndirectOffsetOnAxis(ap=slot[:, b, k:k + 1], axis=0),
                                count[:, b, k:k + 1], None, compute_op=ALU.add).then_inc(landed, 16)

                turn(0, True)
                with pool.Fori(1, G // 2) as i:
                    turn(i, False)
                pool.wait_ge(landed, 16 * GT * G)
    if dbg and dbg["stop"] == "build":
        return finish_debug(nc, top, sem, dbg, {"adj": adj_rows[:, 0:NP]})


    end_phase()
    with ExitStack() as c:
        def sb(name, shape, dt):
            return c.enter_context(nc.sbuf_tensor(name, shape, dt))
        R_IN = 3
        blk = sb("blk", [P, R_IN, NB, BW], BF16)
        blkT = sb("blkT", [P, R_IN, NB, BW], BF16)
        in_part = sb("in_part", [P, NT, NBLK], F32)
        out_part = sb("out_part", [P, NT, NBLK], F32)
        psT = [c.enter_context(nc.psum_tensor(f"psT{j}", [P, BW], BF16)) for j in range(NB)]
        loaded = [sem(f"t_load{q}") for q in range(R_IN)]
        stored = [sem(f"t_store{q}") for q in range(R_IN)]
        turned, moved, summed, degs = sem("t_turned"), sem("t_moved"), sem("t_summed"), sem("t_degs")
        uses = [len(range(q, NBLK, R_IN)) for q in range(R_IN)]

        def before(C, i):
            return i * NBLK + C - R_IN + 1 if C >= R_IN else i * NBLK - NBLK + max(range(C % R_IN, NBLK, R_IN)) + 1

        with nc.Block() as block:
            @block.sync
            def _(sp):
                def turn(i, first):
                    for C in range(NBLK):
                        if not (first and C < R_IN):
                            sp.wait_ge(turned, before(C, i) * NB)
                            sp.wait_ge(summed, before(C, i))
                        sp.dma_start(blk[:, C % R_IN], adj_rows[bass.ds(i * BW, BW), C * BW:(C + 1) * BW]
                                     .rearrange("(t p) s -> p t s", p=P)).then_inc(loaded[C % R_IN], 16)
                turn(0, True)
                with sp.Fori(1, NBLK) as i:
                    turn(i, False)

            @block.tensor
            def _(pe):
                def turn(i, first):
                    for C in range(NBLK):
                        pe.wait_ge(loaded[C % R_IN], i * (16 * uses[C % R_IN]) + 16 * (C // R_IN + 1))
                        for j in range(NB):
                            if not (first and C == 0):
                                pe.wait_ge(moved, i * (NBLK * NB) + ((C - 1) * NB + j + 1))
                            for t in range(NB):
                                mm = nc.tensor.transpose(psT[j][:, t * P:(t + 1) * P],
                                                         blk[:, C % R_IN, t, j * P:(j + 1) * P], identb[:])
                            mm.then_inc(turned, 1)
                turn(0, True)
                with pe.Fori(1, NBLK) as i:
                    turn(i, False)

            @block.scalar
            def _(act):
                def turn(i, first):
                    for C in range(NBLK):
                        if not (first and C < R_IN):
                            prev = (C - R_IN) // R_IN + 1 if C >= R_IN else 0
                            act.wait_ge(stored[C % R_IN], i * (16 * uses[C % R_IN]) + 16 * prev)
                        for j in range(NB):
                            act.wait_ge(turned, i * (NBLK * NB) + (C * NB + j + 1))
                            nc.scalar.activation(blkT[:, C % R_IN, j, :], psT[j][:], ACT.Copy,
                                                 accum_out=out_part[:, C * NB + j, bass.ds(i, 1)]).then_inc(moved, 1)
                        act.wait_ge(moved, i * (NBLK * NB) + ((C + 1) * NB))
                        act.dma_start(adjT_d[C * BW:(C + 1) * BW, bass.ds(i * BW, BW)].rearrange("(t p) s -> p t s", p=P),
                                      blkT[:, C % R_IN]).then_inc(stored[C % R_IN], 16)
                turn(0, True)
                with act.Fori(1, NBLK) as i:
                    turn(i, False)
                for q in range(R_IN):
                    act.wait_ge(stored[q], 16 * uses[q] * NBLK)

            @block.vector
            def _(dve):
                with dve.Fori(0, NBLK) as i:
                    for C in range(NBLK):
                        dve.wait_ge(loaded[C % R_IN], i * (16 * uses[C % R_IN]) + 16 * (C // R_IN + 1))
                        nc.vector.tensor_reduce(in_part[:, bass.ds(i * NB, NB), C], blk[:, C % R_IN], AX_X,
                                                ALU.add).then_inc(summed, 1)
                dve.wait_ge(summed, NBLK * NBLK)
                dve.wait_ge(moved, NBLK * NBLK * NB)
                nc.vector.tensor_reduce(deg_in[:], in_part[:], AX_X, ALU.add).then_inc(degs, 1)
                nc.vector.tensor_reduce(deg_out[:], out_part[:], AX_X, ALU.add).then_inc(degs, 1)

    end_phase()
    with ExitStack() as c:
        def sb(name, shape, dt):
            return c.enter_context(nc.sbuf_tensor(name, shape, dt))
        upto = sb("upto", [P, P], F32)
        ones = sb("ones", [P, P], F32)
        tot = sb("tot", [P, NT], F32)
        cum_t = sb("cum_t", [P, NT], F32)
        cum = sb("cum", [P, NT], F32)
        first = sb("first", [P, NT], F32)
        ei = sb("ei", [P, 2, NT], I32)
        ew = sb("ew", [P, 3, 2, NT], I32)
        cl = sb("cl", [P, 2, NT], F32)
        rt = sb("rt", [P, 2, NT], F32)
        no_edge = sb("no_edge", [P, NT], I32)
        spare = sb("spare", [P, NT], I32)
        low = sb("low", [P, NT], F32)
        alive = sb("alive", [P, NT], F32)
        ps_in = c.enter_context(nc.psum_tensor("ps_in", [P, NT], F32))
        ps_tot = c.enter_context(nc.psum_tensor("ps_tot", [P, NT], F32))
        vs, pl, mm_s, rooted = sem("n_dve"), sem("n_pool"), sem("n_pe"), sem("n_root")
        with nc.Block() as block:
            @block.gpsimd
            def _(pool):
                nc.gpsimd.memset(upto[:], 1.0).then_inc(pl, 1)
                nc.gpsimd.iota(spare[:], pattern=[[P, NT]], base=EP, channel_multiplier=1).then_inc(pl, 1)
                pool.wait_ge(pl, 2)
                nc.gpsimd.affine_select(out=upto[:], in_=upto[:], compare_op=ALU.is_ge, fill=0.0, base=0,
                                        pattern=[[1, P]], channel_multiplier=-1).then_inc(pl, 1)

            @block.tensor
            def _(pe):
                pe.wait_ge(pl, 3)
                pe.wait_ge(vs, 1)
                nc.tensor.matmul(ps_in[:], upto[:], deg_in[:], start=True, stop=True)
                nc.tensor.matmul(ps_tot[:], ones[:], deg_in[:], start=True, stop=True).then_inc(mm_s, 1)

            @block.scalar
            def _(act):
                act.wait_ge(vs, 3)
                nc.scalar.sqrt(rt[:], cl[:]).then_inc(rooted, 1)

            @block.vector
            def _(dve):
                s = Steps(dve, vs)
                s.did(nc.vector.memset(ones[:], 1.0))
                s.did(nc.vector.tensor_scalar_max(cl[:, 0, :], deg_in[:], 1.0))
                s.did(nc.vector.tensor_scalar_max(cl[:, 1, :], deg_out[:], 1.0))
                dve.wait_ge(rooted, 1)
                s.did(nc.vector.reciprocal(norm_in[:], rt[:, 0, :]))
                s.did(nc.vector.reciprocal(norm_out[:], rt[:, 1, :]))
                s.did(nc.vector.reciprocal(half_in[:], cl[:, 0, :]))
                s.link(nc.vector.reciprocal(half_out[:], cl[:, 1, :]))
                s.did(nc.vector.tensor_scalar_mul(half_in[:], half_in[:], 0.5))
                s.did(nc.vector.tensor_scalar_mul(half_out[:], half_out[:], 0.5))
                dve.wait_ge(mm_s, 1)
                s.link(nc.vector.tensor_copy(tot[:], ps_tot[:]))
                s.link(nc.vector.tensor_tensor_scan(cum_t[:], ones[:, 0:NT], tot[:], 0.0, ALU.mult, ALU.add))
                s.link(nc.vector.tensor_sub(cum_t[:], cum_t[:], tot[:]))
                s.link(nc.vector.tensor_add(cum[:], cum_t[:], ps_in[:]))
                s.link(nc.vector.tensor_sub(first[:], cum[:], deg_in[:]))
                s.did(nc.vector.tensor_copy(ei[:, 1, :], first[:]))
                s.link(nc.vector.tensor_scalar(cum[:], cum[:], -1.0, 0.0, ALU.add, ALU.max))
                s.link(nc.vector.tensor_copy(ei[:, 0, :], cum[:]))
                s.did(nc.vector.tensor_scalar(ew[:, 0], ei[:], -GE, None, ALU.bitwise_and))
                s.did(nc.vector.tensor_scalar(ew[:, 1], ei[:], P - 1, 3, ALU.bitwise_and, ALU.logical_shift_left))
                s.link(nc.vector.tensor_scalar(ew[:, 2], ei[:], 7, GT - 1, ALU.logical_shift_right, ALU.bitwise_and))
                s.link(nc.vector.tensor_tensor(ew[:, 0], ew[:, 0], ew[:, 1], ALU.bitwise_or))
                s.did(nc.vector.tensor_tensor(end_row[:], ew[:, 0, 0], ew[:, 2, 0], ALU.bitwise_or))
                s.did(nc.vector.tensor_tensor(start_row[:], ew[:, 0, 1], ew[:, 2, 1], ALU.bitwise_or))
                s.link(nc.vector.tensor_scalar(no_edge[:], deg_in[:], 0.0, None, ALU.is_equal))
                s.did(nc.vector.copy_predicated(start_row[:], no_edge[:], spare[:]))
                s.link(nc.vector.tensor_scalar(ei[:, 1, :], ei[:, 0, :], P - 1, None, ALU.bitwise_and))
                s.link(nc.vector.tensor_scalar(low[:], ei[:, 1, :], float(P - 1), None, ALU.not_equal))
                s.link(nc.vector.tensor_scalar(alive[:], deg_in[:], 0.0, None, ALU.is_gt))
                s.link(nc.vector.tensor_mul(own_end[:], low[:], alive[:]))
    if dbg and dbg["stop"] == "deg":
        return finish_debug(nc, top, sem, dbg, {"adjT": adjT_d, "deg_in": deg_in[:], "deg_out": deg_out[:], "norm_in": norm_in[:],
            "end_row": end_row[:], "start_row": start_row[:], "own_end": own_end[:], "first_id": first_id[0:98], "last_id": last_id[0:98]})


    end_phase()
    def each(row):
        return row.unsqueeze(2).to_broadcast([P, NT, D])

    def along(vector):
        return vector.unsqueeze(1).to_broadcast([P, NT, D])

    def row_of(name, width=D):
        return a[name].rearrange("(a n) -> a n", a=1).to_broadcast([P, width])

    def split(s):
        for part in range(3):
            src = h_sb if part == 0 else t_sb
            s.link(nc.vector.tensor_copy(h3[:, :, part * D:(part + 1) * D], src[:]))
            if part < 2:
                s.link(nc.vector.tensor_sub(t_sb[:], src[:], h3[:, :, part * D:(part + 1) * D]))

    def norm_phase(tag, scale, with_split):
        with ExitStack() as c:
            mean = c.enter_context(nc.sbuf_tensor(f"mean{tag}", [P, NT], F32))
            var = c.enter_context(nc.sbuf_tensor(f"var{tag}", [P, NT], F32))
            std = c.enter_context(nc.sbuf_tensor(f"std{tag}", [P, NT], F32))
            rstd = c.enter_context(nc.sbuf_tensor(f"rstd{tag}", [P, NT], F32))
            vs, rooted = sem(f"ln_dve{tag}"), sem(f"ln_root{tag}")
            with nc.Block() as block:
                @block.scalar
                def _(act):
                    act.wait_ge(vs, 6)
                    nc.scalar.sqrt(std[:], var[:]).then_inc(rooted, 1)

                @block.vector
                def _(dve):
                    s = Steps(dve, vs)
                    s.link(nc.vector.tensor_reduce(mean[:], x_sb[:], AX_X, ALU.add))
                    s.link(nc.vector.tensor_scalar_mul(mean[:], mean[:], 1.0 / D))
                    s.link(nc.vector.tensor_sub(h_sb[:], x_sb[:], each(mean[:])))
                    s.link(nc.vector.tensor_mul(t_sb[:], h_sb[:], h_sb[:]))
                    s.link(nc.vector.tensor_reduce(var[:], t_sb[:], AX_X, ALU.add))
                    s.link(nc.vector.tensor_scalar(var[:], var[:], 1.0 / D, EPS, ALU.mult, ALU.add))
                    dve.wait_ge(rooted, 1)
                    s.link(nc.vector.reciprocal(rstd[:], std[:]))
                    if scale is not None:
                        s.link(nc.vector.tensor_mul(rstd[:], rstd[:], scale[:]))
                    s.link(nc.vector.tensor_scalar_max(h_sb[:], h_sb[:], 0.0))
                    s.link(nc.vector.tensor_mul(h_sb[:], h_sb[:], each(rstd[:])))
                    if with_split:
                        split(s)
        end_phase()

    sw_load = [sem(f"s_load{q}", keep=True) for q in range(4)]
    sw_used, sw_high, sw_low, sw_made, sw_taken, sw_w, sw_chain = (
        sem(n, keep=True) for n in ("s_used", "s_high", "s_low", "s_made", "s_taken", "s_weights", "s_chain"))
    sweeps = [0]

    def sweep(matrix, weight, scale, accumulate):
        n = sweeps[0]
        sweeps[0] += 1
        RING = 4
        uses = [len(range(q, NBLK, RING)) for q in range(RING)]
        tb = n * NBLK
        with ExitStack() as c:
            ring = c.enter_context(nc.sbuf_tensor(f"ring{n}", [P, RING, NB, BW], BF16))
            high = c.enter_context(nc.sbuf_tensor(f"high{n}", [P, 2, HW], F32))
            low = c.enter_context(nc.sbuf_tensor(f"low{n}", [D, 2, HW], F32))
            w2 = c.enter_context(nc.sbuf_tensor(f"w2_{n}", [P, D], F32))
            tmp = c.enter_context(nc.sbuf_tensor(f"swt{n}", [P, NB, D], F32))
            ps_h = c.enter_context(nc.psum_tensor(f"ps_h{n}", [P, 2, 512], F32))
            ps_l = c.enter_context(nc.psum_tensor(f"ps_l{n}", [P, 2, 512], F32))
            ps_y = c.enter_context(nc.psum_tensor(f"ps_y{n}", [P, NB, D], F32))
            hv = high[:].rearrange("p a b -> p (a b)")
            lv = low[:].rearrange("p a b -> p (a b)")

            def before(kb, i):
                held = kb - RING if kb >= RING else max(range(kb % RING, NBLK, RING)) - NBLK
                return i * NBLK + (tb * NBLK + held + 1)

            with nc.Block() as block:
                @block.sync
                def _(sp):
                    sp.dma_start(w2[0:D, :], a[weight]).then_inc(sw_w, 16)
                    sp.dma_start(w2[D:P, :], a[weight]).then_inc(sw_w, 16)

                    def turn(i, first):
                        for kb in range(NBLK):
                            if not (first and kb < RING):
                                sp.wait_ge(sw_used, before(kb, i))
                            sp.dma_start(ring[:, kb % RING], matrix[kb * BW:(kb + 1) * BW, bass.ds(i * BW, BW)]
                                         .rearrange("(t p) s -> p t s", p=P)).then_inc(sw_load[kb % RING], 16)
                    turn(0, True)
                    with sp.Fori(1, NBLK) as i:
                        turn(i, False)

                @block.tensor
                def _(pe):
                    pe.wait_ge(sw_w, 32 * (n + 1))
                    with pe.Fori(0, NBLK) as i:
                        pe.wait_ge(sw_high, i + (tb + 1))
                        pe.wait_ge(sw_low, i + (tb + 1))
                        for kb in range(NBLK):
                            q = kb % RING
                            pe.wait_ge(sw_load[q], i * (16 * uses[q]) + 16 * (tb * uses[q] + kb // RING + 1))
                            for t in range(NB):
                                k = kb * NB + t
                                for half in range(2):
                                    cols = ring[:, q, t, half * HW:(half + 1) * HW]
                                    nc.tensor.matmul(ps_h[:, half, 0:HW], h3[:, k, 0:P], cols, start=k == 0, stop=k == NT - 1)
                                for half in range(2):
                                    cols = ring[:, q, t, half * HW:(half + 1) * HW]
                                    mm = nc.tensor.matmul(ps_l[0:D, half, 0:HW], h3[:, k, P:P + D], cols, start=k == 0,
                                                          stop=k == NT - 1)
                            mm.then_inc(sw_used, 1)
                        pe.wait_ge(sw_high, i + (tb + 2))
                        pe.wait_ge(sw_low, i + (tb + 2))
                        pe.wait_ge(sw_taken, i + (tb + 1))
                        for j in range(NB):
                            nc.tensor.matmul(ps_y[:, j, :], hv[:, j * P:(j + 1) * P], w2[:], start=True, stop=False)
                            mm = nc.tensor.matmul(ps_y[:, j, :], lv[:, j * P:(j + 1) * P], w2[0:D, :], start=False, stop=True)
                        mm.then_inc(sw_made, 1)

                @block.scalar
                def _(act):
                    if n == 0:
                        act.sem_inc(sw_low, 1)
                    with act.Fori(0, NBLK) as i:
                        act.wait_ge(sw_used, i * NBLK + (tb * NBLK + NBLK))
                        nc.scalar.copy(low[:], ps_l[0:D, :, 0:HW]).then_inc(sw_low, 1)

                @block.vector
                def _(dve):
                    if n == 0:
                        dve.sem_inc(sw_high, 1)
                        dve.sem_inc(sw_taken, 1)
                    with dve.Fori(0, NBLK) as i:
                        dve.wait_ge(sw_used, i * NBLK + (tb * NBLK + NBLK))
                        nc.vector.tensor_copy(high[:], ps_h[:, :, 0:HW]).then_inc(sw_high, 1)
                        dve.wait_ge(sw_made, i + (tb + 1))
                        nodes = bass.ds(i * NB, NB)
                        sc = scale[:, nodes].unsqueeze(2).to_broadcast([P, NB, D])
                        if accumulate:
                            nc.vector.tensor_mul(tmp[:], ps_y[:], sc).then_inc(sw_taken, 1)
                            dve.wait_ge(sw_taken, i + (tb + 2))
                            nc.vector.tensor_add(y_sb[:, nodes, :], y_sb[:, nodes, :], tmp[:]).then_inc(sw_chain, 1)
                        else:
                            nc.vector.tensor_mul(y_sb[:, nodes, :], ps_y[:], sc).then_inc(sw_taken, 1)

    def bias_phase(tag, biases, factors, work):
        with ExitStack() as c:
            rows = c.enter_context(nc.sbuf_tensor(f"rows{tag}", [P, len(biases), D], F32))
            ld, vs = sem(f"bias_load{tag}"), sem(f"bias_dve{tag}")
            with nc.Block() as block:
                @block.sync
                def _(sp):
                    for r, name in enumerate(biases):
                        sp.dma_start(rows[:, r, :], row_of(name)).then_inc(ld, 16)

                @block.vector
                def _(dve):
                    dve.wait_ge(ld, 16 * len(biases))
                    work(Steps(dve, vs), rows)
        end_phase()

    norm_phase("0", norm_out, True)
    sweep(adjT_d, "L0_gnn_W1", norm_in, False)

    def between(s, rows):
        s.link(nc.vector.tensor_add(h_sb[:], y_sb[:], along(rows[:, 0, :])))
        s.link(nc.vector.tensor_scalar_max(h_sb[:], h_sb[:], 0.0))
        s.link(nc.vector.tensor_mul(h_sb[:], h_sb[:], each(norm_out[:])))
        split(s)
    bias_phase("0a", ["L0_gnn_b1"], None, between)
    sweep(adjT_d, "L0_gnn_W2", norm_in, False)

    def close0(s, rows):
        s.link(nc.vector.tensor_add(x_sb[:], x_sb[:], y_sb[:]))
        s.link(nc.vector.tensor_add(x_sb[:], x_sb[:], along(rows[:, 0, :])))
    bias_phase("0b", ["L0_gnn_b2"], None, close0)
    if dbg and dbg["stop"] == "L0":
        return finish_debug(nc, top, sem, dbg, {"x": x_sb[:]})


    def node_product(tag, width, fill, local=(), stores=(), hidden=False, prepare=None, extra_bias=None, factor=None):
        per_bank = min(NB, 512 // width)
        banks = -(-NB // per_bank)
        with ExitStack() as c:
            def sb(name, shape, dt=F32):
                return c.enter_context(nc.sbuf_tensor(name + tag, shape, dt))
            wid = P if hidden else width
            wcat = sb("wcat", [D + 1, wid])
            hst = sb("hst", [P, NB, D])
            hT = sb("hT", [D + 1, BW])
            stage = sb("stage", [P, NB, width])
            ps_x = c.enter_context(nc.psum_tensor("ps_x" + tag, [D, 2, 512], F32))
            ps_m = c.enter_context(nc.psum_tensor("ps_m" + tag, [P, banks, 512], F32))
            if hidden:
                w2n = sb("w2n", [P, D])
                b2n = sb("b2n", [P, D])
                dps = sb("dps", [P, 1])
                hid = sb("hid", [P, 2, HW])
                act_h = sb("act_h", [P, 2, HW])
                ps_hid = c.enter_context(nc.psum_tensor("ps_hid" + tag, [P, 2, 512], F32))
            copied, turned, moved, made, taken, stored, wl = (
                sem(f"{n}{tag}") for n in ("np_copied", "np_turned", "np_moved", "np_made", "np_taken", "np_stored", "np_w"))
            hid_made, hid_out, hid_act, prep, chain = (
                sem(f"{n}{tag}") for n in ("np_hid", "np_hidout", "np_hidact", "np_prep", "np_chain"))
            extra = prepare(c) if prepare else None
            loads = [0]
            with nc.Block() as block:
                @block.sync
                def _(sp):
                    loads[0] = 16 * fill(sp, wcat, wl, extra)
                    if hidden:
                        sp.dma_start(w2n[:], a["L3_gnn_W2n"]).then_inc(wl, 16)
                        sp.dma_start(b2n[:], row_of("L3_gnn_b2n")).then_inc(wl, 16)
                        sp.dma_start(dps[:], row_of("L3_gnn_dp_scale", 1)).then_inc(wl, 16)
                        loads[0] += 48

                    def turn(i):
                        sp.wait_ge(taken, i + 1)
                        for cols, rows in stores:
                            sp.dma_start(rows[bass.ds(i * BW, BW), :].rearrange("(t p) d -> p t d", p=P),
                                         stage[:, :, cols]).then_inc(stored, 16)
                    if stores:
                        with sp.Fori(0, NBLK) as i:
                            turn(i)
                        sp.wait_ge(stored, 16 * len(stores) * NBLK)

                @block.tensor
                def _(pe):
                    pe.wait_ge(wl, loads[0])
                    if extra is not None:
                        extra["pe"](pe, prep)

                    def turn(i, first):
                        pe.wait_ge(copied, i + 1)
                        pe.nop(nofuse=True)
                        for j in range(NB):
                            tr = nc.tensor.transpose(ps_x[:, j // 4, (j % 4) * P:(j % 4 + 1) * P], hst[:, j, :], ident[:])
                        tr.then_inc(turned, 1)
                        pe.wait_ge(moved, i * 2 + 2)
                        pe.wait_ge(prep, 2)
                        if hidden:
                            for half in range(2):
                                mm = nc.tensor.matmul(ps_hid[:, half, 0:HW], wcat[:], hT[:, half * HW:(half + 1) * HW],
                                                      start=True, stop=True)
                            mm.then_inc(hid_made, 1)
                            pe.wait_ge(hid_act, i + 1)
                        if not first:
                            pe.wait_ge(taken, i)
                        for j in range(NB):
                            dst = ps_m[:, j // per_bank, (j % per_bank) * width:(j % per_bank + 1) * width]
                            if hidden:
                                lhs, rhs = act_h[:].rearrange("p a b -> p (a b)")[:, j * P:(j + 1) * P], w2n[:]
                            else:
                                lhs, rhs = hT[:, j * P:(j + 1) * P], wcat[:]
                            mm = nc.tensor.matmul(dst, lhs, rhs, start=True, stop=True)
                        mm.then_inc(made, 1)
                    turn(0, True)
                    with pe.Fori(1, NBLK) as i:
                        turn(i, False)

                @block.scalar
                def _(act):
                    def turn(i, first):
                        act.wait_ge(turned, i + 1)
                        if not first:
                            act.wait_ge(made, i)
                        nc.scalar.copy(hT[0:D, 0:512], ps_x[:, 0, :]).then_inc(moved, 1)
                        nc.scalar.copy(hT[0:D, 512:BW], ps_x[:, 1, 0:BW - 512]).then_inc(moved, 1)
                        if hidden:
                            act.wait_ge(hid_made, i + 1)
                            nc.scalar.copy(hid[:], ps_hid[:, :, 0:HW]).then_inc(hid_out, 1)
                    turn(0, True)
                    with act.Fori(1, NBLK) as i:
                        turn(i, False)

                @block.vector
                def _(dve):
                    nc.vector.memset(hT[D:D + 1, :], 1.0).then_inc(prep, 1)
                    if extra is not None:
                        extra["dve"](dve, prep, wl, loads[0])
                    else:
                        dve.sem_inc(prep, 1)
                    dve.wait_ge(wl, loads[0])

                    def turn(i, first):
                        nodes = bass.ds(i * NB, NB)
                        if not first:
                            dve.wait_ge(turned, i)
                        nc.vector.tensor_copy(hst[:], h_sb[:, nodes, :]).then_inc(copied, 1)
                        if hidden:
                            dve.wait_ge(hid_out, i + 1)
                            nc.vector.scalar_tensor_tensor(out=act_h[:], in0=hid[:], scalar=0.1, in1=hid[:], op0=ALU.mult,
                                                           op1=ALU.max).then_inc(hid_act, 1)
                        dve.wait_ge(made, i + 1)
                        if stores and not first:
                            dve.wait_ge(stored, i * (16 * len(stores)))
                        ct = Steps(dve, chain, turn=i, per=banks + (2 if hidden else 0))
                        for b in range(banks):
                            w = min(per_bank, NB - b * per_bank)
                            ct.did(nc.vector.tensor_copy(
                                stage[:, b * per_bank:b * per_bank + w, :],
                                ps_m[:, b, 0:w * width].rearrange("p (j f) -> p j f", j=w)))
                        ct.wait()
                        if hidden:
                            ct.link(nc.vector.tensor_add(stage[:], stage[:], b2n[:].unsqueeze(1).to_broadcast([P, NB, D])))
                            ct.link(nc.vector.tensor_scalar(stage[:], stage[:], dps[:, 0:1], None, ALU.mult))
                        for cols, keep_in in local:
                            nc.vector.tensor_copy(keep_in[:, nodes, :], stage[:, :, cols]).then_inc(sw_chain, 1)
                        dve.nop(nofuse=True)
                        dve.sem_inc(taken, 1)
                    turn(0, True)
                    with dve.Fori(1, NBLK) as i:
                        turn(i, False)
        end_phase()

    def dst_rows(g):
        return dstf_d[1:EP + 1].rearrange("(a n) -> a n", a=1)[:, bass.ds(g * GE, GE)].to_broadcast([P, GE])

    def part_rows(table, g):
        return table[bass.ds(g * GE, GE), :].rearrange("(p k) d -> p (k d)", p=P)

    def collect(tag, finish):
        with ExitStack() as c:
            def sb(name, shape, dt=F32):
                return c.enter_context(nc.sbuf_tensor(name + tag, shape, dt))
            last_row = sb("last_row", [P, 2, GT * D])
            iota_i = sb("iota_i", [P, P], I32)
            iota_f = sb("iota_f", [P, P])
            shifted = sb("shifted", [P, NT, 2 * GT])
            node0 = sb("node0", [P, NT])
            node0_i = sb("node0_i", [P, NT], I32)
            hot = sb("hot", [P, 2, 2 * GT, P])
            ps_c = c.enter_context(nc.psum_tensor("ps_c" + tag, [P, 2, 512], F32))
            got = sem(f"c_got{tag}", keep=True)
            ld, pl, hots, picked, taken, vs, chain = (
                sem(f"{n}{tag}") for n in ("c_load", "c_iota", "c_hot", "c_picked", "c_taken", "c_dve", "c_chain"))
            with nc.Block() as block:
                @block.sync
                def _(sp):
                    view = part_d.rearrange("(h g p k) d -> h g p (k d)", h=2, p=P, k=GT)
                    for h in range(2):
                        sp.dma_start(last_row[0:GH, h, :], view[h, :, P - 1, :]).then_inc(ld, 16)

                @block.gpsimd
                def _(pool):
                    nc.gpsimd.iota(iota_i[:], pattern=[[1, P]], base=0, channel_multiplier=0).then_inc(pl, 1)
                    nc.gpsimd.iota(node0_i[:], pattern=[[P, NT]], base=0, channel_multiplier=0).then_inc(pl, 1)
                    for t in range(NT):
                        nc.gpsimd.indirect_dma_start(y_sb[:, t, :], None, part_d,
                                                     bass.IndirectOffsetOnAxis(ap=end_row[:, t:t + 1], axis=0)).then_inc(got, 16)

                @block.tensor
                def _(pe):
                    pe.wait_ge(ld, 32)

                    def node_tile(t2, i, first):
                        pe.wait_ge(hots, i + 1)
                        if not first:
                            pe.wait_ge(taken, i - 1)
                        for q in range(2 * GT):
                            mm = nc.tensor.matmul(ps_c[:, t2, 0:D], hot[0:GH, t2, q, :],
                                                  last_row[0:GH, q // GT, (q % GT) * D:(q % GT + 1) * D],
                                                  start=q == 0, stop=q == 2 * GT - 1)
                        mm.then_inc(picked, 1)
                    for t2 in range(2):
                        node_tile(t2, t2, True)
                    with pe.Fori(2, NT - 1, 2) as i:
                        for t2 in range(2):
                            node_tile(t2, i + t2, False)
                    node_tile(0, NT - 1, False)

                @block.vector
                def _(dve):
                    s = Steps(dve, vs)
                    dve.wait_ge(pl, 2)
                    s.did(nc.vector.tensor_copy(iota_f[:], iota_i[:]))
                    s.link(nc.vector.tensor_copy(node0[:], node0_i[:]))
                    s.link(nc.vector.tensor_sub(
                        shifted[0:GH], last_id[0:GH].rearrange("p h k -> p (h k)").unsqueeze(1).to_broadcast([GH, NT, 2 * GT]),
                        node0[0:GH, :].unsqueeze(2).to_broadcast([GH, NT, 2 * GT])))
                    dve.wait_ge(got, 16 * NT)
                    s.link(nc.vector.tensor_mul(y_sb[:], y_sb[:], each(own_end[:])))

                    def node_tile(t2, i, first):
                        if not first:
                            dve.wait_ge(picked, i - 1)
                        one = iota_f[0:GH, :].unsqueeze(1).to_broadcast([GH, 2 * GT, P])
                        at = shifted[0:GH, bass.ds(i, 1), :].rearrange("p a q -> p (a q)").unsqueeze(2) \
                            .to_broadcast([GH, 2 * GT, P])
                        nc.vector.tensor_tensor(hot[0:GH, t2], one, at, ALU.is_equal).then_inc(hots, 1)

                    def take(t2, i):
                        dve.wait_ge(picked, i + 1)
                        node = y_sb[:, bass.ds(i, 1), :].rearrange("p a d -> p (a d)")
                        nc.vector.tensor_add(node, node, ps_c[:, t2, 0:D]).then_inc(taken, 1)
                    for t2 in range(2):
                        node_tile(t2, t2, True)
                    with dve.Fori(2, NT - 1, 2) as i:
                        for t2 in range(2):
                            take(t2, i + (t2 - 2))
                            node_tile(t2, i + t2, False)
                    take(0, NT - 3)
                    node_tile(0, NT - 1, False)
                    take(1, NT - 2)
                    take(0, NT - 1)
                    dve.wait_ge(taken, NT)
                    finish(s)
        end_phase()

    norm_phase("1", None, False)

    def l1_prepare(c):
        weT = c.enter_context(nc.sbuf_tensor("weT", [D, D + 1], F32))
        ws = c.enter_context(nc.sbuf_tensor("ws", [D, D], F32))
        wsb = c.enter_context(nc.sbuf_tensor("wsb", [D + 1, D], F32))
        ps_w = c.enter_context(nc.psum_tensor("ps_w", [D + 1, D], F32))
        fused = sem("l1_fused")

        def pe(eng, prep):
            nc.tensor.matmul(ps_w[:], weT[:], ws[:], start=True, stop=True).then_inc(fused, 1)

        def dve(eng, prep, wl, loads):
            eng.wait_ge(wl, loads)
            eng.wait_ge(fused, 1)
            nc.vector.tensor_copy(both["wcat"][:, 0:D], ps_w[:]).then_inc(fused, 1)
            eng.wait_ge(fused, 2)
            nc.vector.tensor_add(both["wcat"][D:D + 1, 0:D], both["wcat"][D:D + 1, 0:D], wsb[D:D + 1, :]).then_inc(prep, 1)
        both = {"pe": pe, "dve": dve, "weT": weT, "ws": ws, "wsb": wsb}
        return both

    def l1_fill(sp, wcat, wl, extra):
        extra["wcat"] = wcat
        for dst, src in ((wcat[0:D, D:2 * D], a["L1_gnn_We_k"].rearrange("f h d -> f (h d)")),
                         (wcat[D:D + 1, D:2 * D], a["L1_gnn_We_b"]),
                         (wcat[0:D, 2 * D:3 * D], a["L1_gnn_Wr_k"].rearrange("f h d -> f (h d)")),
                         (wcat[D:D + 1, 2 * D:3 * D], a["L1_gnn_Wr_b"]),
                         (extra["weT"][:], a["L1_We_T"]),
                         (extra["ws"][:], a["L1_gnn_Ws_k"]),
                         (extra["wsb"][D:D + 1, :], a["L1_gnn_Ws_b"].rearrange("(a n) -> a n", a=1))):
            sp.dma_start(dst, src).then_inc(wl, 16)
        return 7
    node_product("n1", 3 * D, l1_fill, local=[(slice(2 * D, 3 * D), y_sb)],
                 stores=[(slice(0, 2 * D), send_d), (slice(2 * D, 3 * D), recv_d)], prepare=l1_prepare)

    with ExitStack() as c:
        tile_first = c.enter_context(nc.sbuf_tensor("tile_first", [P, 2, GT, D], F32))
        put, got, wrote = sem("z_put", keep=True), sem("z_got", keep=True), sem("z_wrote")
        with nc.Block() as block:
            @block.gpsimd
            def _(pool):
                for h in range(2):
                    for k in range(GT):
                        nc.gpsimd.indirect_dma_start(
                            tile_first[0:GH, h, k, :], None, recv_d,
                            bass.IndirectOffsetOnAxis(ap=first_id[0:GH, h, k:k + 1], axis=0)).then_inc(got, 16)
                for t in range(NT):
                    nc.gpsimd.indirect_dma_start(recvz_d, bass.IndirectOffsetOnAxis(ap=start_row[:, t:t + 1], axis=0),
                                                 y_sb[:, t, :], None).then_inc(put, 16)

            @block.sync
            def _(sp):
                sp.wait_ge(got, 16 * 2 * GT)
                sp.wait_ge(put, 16 * NT)
                view = recvz_d[0:EP, :].rearrange("(h g p k) d -> h g p (k d)", h=2, p=P, k=GT)
                for h in range(2):
                    sp.dma_start(view[h, :, 0, :], tile_first[0:GH, h].rearrange("p k d -> p (k d)")).then_inc(wrote, 16)
                sp.wait_ge(wrote, 32)

    end_phase()
    logit_scope = ExitStack()
    logit = logit_scope.enter_context(nc.sbuf_tensor("logit", [P, T], F32))
    with ExitStack() as c:
        def sb(name, shape, dt=F32):
            return c.enter_context(nc.sbuf_tensor(name, shape, dt))
        idx = sb("e_idx", [P, 2, GT], I32)
        sent = sb("sent", [P, 2, GT, 2 * D])
        drow = sb("drow", [P, 2, GE])
        zrow = sb("zrow", [P, 2, GT * D])
        same = sb("same", [P, 2, GT, P])
        pack = sb("pack", [P, 2, GT * D])
        xs = sb("xs", [P, 2, GT * D])
        xc = sb("xc", [P, 2, GT * D])
        u = sb("u", [P, 2, GT * D])
        tt = sb("tt", [P, 2, GT * D])
        den = sb("den", [P, 2, GT * D])
        qq = sb("qq", [P, 2, GT * D])
        wa = sb("wa", [P, D])
        wab = sb("wab", [P, 1])
        two = sb("two", [P, 1])
        ps_r = c.enter_context(nc.psum_tensor("ps_r", [P, 2, 512], F32))
        wl, fetched, chain = sem("a_w"), sem("a_idx"), sem("a_chain")
        gathered = [sem("a_gat0", keep=True), sem("a_gat1", keep=True)]
        rowed = [sem("a_row0"), sem("a_row1")]
        packed, stored = sem("a_packed"), [sem("a_st0"), sem("a_st1")]
        compared, spread, summed, bent, exped, tted, dened = (
            sem(n) for n in ("a_same", "a_spread", "a_sum", "a_bent", "a_exp", "a_logit", "a_bias"))
        mids, logged, inverted = sem("a_mids"), sem("a_logged"), sem("a_inverted")
        with nc.Block() as block:
            @block.sync
            def _(sp):
                sp.dma_start(wa[:], a["L1_gnn_Wa_k"].rearrange("m o -> o m").to_broadcast([P, D])).then_inc(wl, 16)
                sp.dma_start(wab[:], row_of("L1_gnn_Wa_b", 1)).then_inc(wl, 16)

                def turn(i, first):
                    for b in range(2):
                        if not first:
                            sp.wait_ge(compared, i * 2 + (b - 1))
                            sp.wait_ge(spread, i * 2 + (b - 1))
                        sp.dma_start(drow[:, b, :], dst_rows(i * 2 + b)).then_inc(rowed[b], 16)
                        sp.dma_start(zrow[:, b, :], part_rows(recvz_d, i * 2 + b)).then_inc(rowed[b], 16)
                turn(0, True)
                with sp.Fori(1, G // 2) as i:
                    turn(i, False)

            @block.gpsimd
            def _(pool):
                def turn(i, first):
                    for b in range(2):
                        pool.wait_ge(fetched, i * 2 + (b + 1))
                        pool.nop(nofuse=True)
                        if not first:
                            pool.wait_ge(summed, i * 2 + (b - 1))
                            pool.nop(nofuse=True)
                            pool.wait_ge(packed, i * 2 + (b - 1))
                            pool.nop(nofuse=True)
                        for k in range(GT):
                            nc.gpsimd.indirect_dma_start(
                                sent[:, b, k, :], None, send_d,
                                bass.IndirectOffsetOnAxis(ap=idx[:, b, k:k + 1], axis=0)).then_inc(gathered[b], 16)
                turn(0, True)
                with pool.Fori(1, G // 2) as i:
                    turn(i, False)

            @block.tensor
            def _(pe):
                def turn(i, first):
                    for b in range(2):
                        pe.wait_ge(rowed[b], i * 32 + 32)
                        pe.wait_ge(compared, i * 2 + (b + 1))
                        if not first:
                            pe.wait_ge(summed, i * 2 + (b - 1))
                        for k in range(GT):
                            mm = nc.tensor.matmul(ps_r[:, b, k * D:(k + 1) * D], same[:, b, k, :],
                                                  zrow[:, b, k * D:(k + 1) * D], start=True, stop=True)
                        mm.then_inc(spread, 1)
                turn(0, True)
                with pe.Fori(1, G // 2) as i:
                    turn(i, False)

            @block.scalar
            def _(act):
                nc.scalar.preload_act_table_set("natural_log_exp_and_others")
                act.wait_ge(dened, 1)

                def turn(i, first):
                    for b in range(2):
                        act.wait_ge(gathered[b], i * (16 * GT) + 16 * GT)
                        if not first:
                            act.wait_ge(stored[b], i * 16)
                        nc.scalar.copy(pack[:, b, :].rearrange("p (k d) -> p k d", d=D), sent[:, b, :, D:2 * D]) \
                            .then_inc(packed, 1)
                        act.wait_ge(packed, i * 2 + (b + 1))
                        act.dma_start(emb_d[bass.ds(i * 2 + b, 1)].rearrange("a p f -> p (a f)"), pack[:, b, :]) \
                            .then_inc(stored[b], 16)
                        act.wait_ge(bent, i * 2 + (b + 1))
                        nc.scalar.activation(u[:, b, :], xc[:, b, :], ACT.Exp).then_inc(exped, 1)
                        act.wait_ge(mids, i * 4 + (b * 2 + 1))
                        nc.scalar.activation(den[:, b, :], tt[:, b, :], ACT.Ln, bias=two[:, 0:1]).then_inc(logged, 1)
                        act.wait_ge(logged, i * 2 + (b + 1))
                        nc.scalar.activation(den[:, b, :], den[:, b, :], ACT.Exp, scale=-1.0).then_inc(inverted, 1)
                turn(0, True)
                with act.Fori(1, G // 2) as i:
                    turn(i, False)
                for b in range(2):
                    act.wait_ge(stored[b], 16 * (G // 2))

            @block.vector
            def _(dve):
                nc.vector.memset(two[:], 2.0).then_inc(dened, 1)
                for b in range(2):
                    nc.vector.tensor_copy(idx[:, b, :], src_c[:, b * GT:(b + 1) * GT]).then_inc(fetched, 1)
                dve.wait_ge(wl, 32)

                def front(i, b, first, last):
                    g = i * 2 + b
                    dve.wait_ge(rowed[b], i * 32 + 32)
                    if not first:
                        dve.wait_ge(spread, i * 2 + (b - 1))
                    nc.vector.tensor_tensor(
                        same[:, b], drow[:, b, :].rearrange("p (k e) -> p k e", k=GT),
                        dst_c[:, bass.ds(g * GT, GT)].unsqueeze(2).to_broadcast([P, GT, P]),
                        ALU.is_equal).then_inc(compared, 1)
                    dve.wait_ge(gathered[b], i * (16 * GT) + 16 * GT)
                    dve.wait_ge(spread, i * 2 + (b + 1))
                    nc.vector.tensor_add(xs[:, b, :].rearrange("p (k d) -> p k d", d=D),
                                         ps_r[:, b, :].rearrange("p (k d) -> p k d", d=D),
                                         sent[:, b, :, 0:D]).then_inc(summed, 1)
                    if not last:
                        nc.vector.tensor_copy(idx[:, b, :], src_c[:, bass.ds(g * GT + 2 * GT, GT)]).then_inc(fetched, 1)
                    dve.wait_ge(summed, i * 2 + (b + 1))
                    nc.vector.tensor_scalar_min(xc[:, b, :], xs[:, b, :], 20.0).then_inc(bent, 1)

                def middle(i, b):
                    dve.wait_ge(exped, i * 2 + (b + 1))
                    m = Steps(dve, mids, turn=i, per=4, base=2 * b)
                    m.link(nc.vector.scalar_tensor_tensor(out=tt[:, b, :], in0=u[:, b, :], scalar=2.0, in1=u[:, b, :],
                                                          op0=ALU.add, op1=ALU.mult))
                    m.did(nc.vector.tensor_mul(qq[:, b, :], tt[:, b, :], xs[:, b, :]))

                def back(i, b):
                    dve.wait_ge(inverted, i * 2 + (b + 1))
                    dve.wait_ge(mids, i * 4 + (b * 2 + 2))
                    ct = Steps(dve, chain, turn=i, per=8, base=4 * b)
                    ct.link(nc.vector.scalar_tensor_tensor(out=tt[:, b, :], in0=tt[:, b, :], scalar=2.0, in1=den[:, b, :],
                                                           op0=ALU.add, op1=ALU.mult))
                    ct.link(nc.vector.scalar_tensor_tensor(out=tt[:, b, :], in0=tt[:, b, :], scalar=2.0, in1=den[:, b, :],
                                                           op0=ALU.subtract, op1=ALU.mult))
                    ct.link(nc.vector.tensor_mul(qq[:, b, :], qq[:, b, :], tt[:, b, :]))
                    q3 = qq[:, b, :].rearrange("p (k d) -> p k d", d=D)
                    ct.link(nc.vector.tensor_mul(q3, q3, wa[:].unsqueeze(1).to_broadcast([P, GT, D])))
                    nc.vector.tensor_reduce(logit[:, bass.ds((i * 2 + b) * GT, GT)], q3, AX_X, ALU.add).then_inc(tted, 1)

                def turn(i, first, last):
                    front(i, 0, first, last)
                    if not first:
                        back(i - 1, 1)
                    middle(i, 0)
                    front(i, 1, first, last)
                    back(i, 0)
                    middle(i, 1)
                turn(0, True, False)
                with dve.Fori(1, G // 2 - 1) as i:
                    turn(i, False, False)
                turn(G // 2 - 1, False, True)
                back(G // 2 - 1, 1)
                dve.wait_ge(tted, G)
                nc.vector.tensor_scalar(logit[:], logit[:], -1.0, wab[:, 0:1], ALU.mult, ALU.add).then_inc(dened, 1)
    if dbg and dbg["stop"] == "logit":
        dbg["scope"] = logit_scope
        return finish_debug(nc, top, sem, dbg, {"logit": logit[:], "send": send_d})


    end_phase()
    NTB = -(-T // P)

    def tile_block(c0):
        return min(P, T - c0 * P)

    def lin_rows(table, c0):
        return table.rearrange("(t p) -> t p", p=P)[c0 * P:c0 * P + tile_block(c0), :]

    with ExitStack() as c:
        def sb(name, shape, dt=F32):
            return c.enter_context(nc.sbuf_tensor(name, shape, dt))
        turn_s = sb("turn_s", [P, NTB, P])
        ps_t = [c.enter_context(nc.psum_tensor(f"ps_t{q}", [P, P], F32)) for q in range(2)]
        dl, dp, dn, lin = (sb(n, [P, T]) for n in ("dl", "dp", "dn", "lin"))
        cont, nxt, is_end, gap = (sb(n, [P, T]) for n in ("cont", "nxt", "is_end", "gap"))
        run, ends_v, segmax, expo = (sb(n, [P, T]) for n in ("run", "ends_v", "segmax", "expo"))
        gate = sb("gate", [P, 3])
        row_s = sb("row_s", [1, 2, P])
        carry_r = sb("carry_r", [1, P + 1])
        carry_c = sb("carry_c", [P, 1])
        one = sb("one", [1, 1])
        ps_g = c.enter_context(nc.psum_tensor("ps_g", [1, 2, P], F32))
        ps_c1 = c.enter_context(nc.psum_tensor("ps_c1", [P, 1], F32))
        turned, moved, st, ld, vs, pe_row, pe_col, ex, wst, wld, back_t = (
            sem(n) for n in ("m_turned", "m_moved", "m_store", "m_load", "m_dve", "m_row", "m_col", "m_exp", "m_wst", "m_wld",
                             "m_back"))
        ask_row, ask_col, w_ready = sem("m_askrow"), sem("m_askcol"), sem("m_wready")
        border = [(run[:, T - 1:T], gate[:, 0:1], carry_r[:, 0:P]), (segmax[:, 0:1], gate[:, 2:3], carry_r[:, 1:P + 1]),
                  (run[:, T - 1:T], gate[:, 1:2], carry_r[:, 0:P]), (segmax[:, 0:1], gate[:, 2:3], carry_r[:, 1:P + 1])]
        with nc.Block() as block:
            @block.tensor
            def _(pe):
                for c0 in range(NTB):
                    w = tile_block(c0)
                    if c0 >= 2:
                        pe.wait_ge(moved, c0 - 1)
                    nc.tensor.transpose(ps_t[c0 % 2][0:w, :], logit[:, c0 * P:c0 * P + w], ident[:]).then_inc(turned, 1)
                for n in range(4):
                    pe.wait_ge(ask_row, n + 1)
                    nc.tensor.matmul(ps_g[:, 0, :], border[n][0], ident[:], start=True, stop=True)
                    nc.tensor.matmul(ps_g[:, 1, :], border[n][1], ident[:], start=True, stop=True).then_inc(pe_row, 1)
                    pe.wait_ge(ask_col, n + 1)
                    nc.tensor.matmul(ps_c1[:], border[n][2], one[:], start=True, stop=True).then_inc(pe_col, 1)
                pe.wait_ge(moved, NTB)
                for c0 in range(NTB):
                    w = tile_block(c0)
                    pe.wait_ge(wld, 16 * NTB)
                    if c0 >= 2:
                        pe.wait_ge(back_t, c0 - 1)
                    nc.tensor.transpose(ps_t[c0 % 2][:, 0:w], turn_s[0:w, c0, :], ident[0:w, 0:w]).then_inc(turned, 1)

            @block.sync
            def _(sp):
                for c0 in range(NTB):
                    sp.wait_ge(moved, c0 + 1)
                    sp.dma_start(lin_rows(lin_d, c0), turn_s[0:tile_block(c0), c0, :]).then_inc(st, 16)
                sp.dma_start(dl[:], dstf_d[1:EP + 1].rearrange("(p j) -> p j", p=P)).then_inc(ld, 16)
                sp.dma_start(dp[:], dstf_d[0:EP].rearrange("(p j) -> p j", p=P)).then_inc(ld, 16)
                sp.dma_start(dn[:], dstf_d[2:EP + 2].rearrange("(p j) -> p j", p=P)).then_inc(ld, 16)
                sp.wait_ge(st, 16 * NTB)
                sp.dma_start(lin[:], lin_d.rearrange("(p j) -> p j", p=P)).then_inc(ld, 16)
                sp.wait_ge(w_ready, 1)
                sp.dma_start(wgt_d.rearrange("(p j) -> p j", p=P), run[:]).then_inc(wst, 16)
                sp.wait_ge(wst, 16)
                for c0 in range(NTB):
                    sp.dma_start(turn_s[0:tile_block(c0), c0, :], lin_rows(wgt_d, c0)).then_inc(wld, 16)

            @block.scalar
            def _(act):
                for c0 in range(NTB):
                    act.wait_ge(turned, c0 + 1)
                    w = tile_block(c0)
                    nc.scalar.copy(turn_s[0:w, c0, :], ps_t[c0 % 2][0:w, :]).then_inc(moved, 1)
                act.wait_ge(ex, 1)
                nc.scalar.activation(expo[:], lin[:], ACT.Exp).then_inc(ex, 1)
                for c0 in range(NTB):
                    w = tile_block(c0)
                    act.wait_ge(turned, NTB + c0 + 1)
                    nc.scalar.copy(logit[:, c0 * P:c0 * P + w], ps_t[c0 % 2][:, 0:w]).then_inc(back_t, 1)

            @block.vector
            def _(dve):
                s = Steps(dve, vs)
                s.did(nc.vector.memset(one[:], 1.0))
                dve.wait_ge(ld, 64)
                s.did(nc.vector.tensor_tensor(cont[:], dl[:], dp[:], ALU.is_equal))
                s.link(nc.vector.tensor_tensor(nxt[:], dl[:], dn[:], ALU.is_equal))
                s.did(nc.vector.tensor_scalar(gap[:], cont[:], -1.0, BIG, ALU.add, ALU.mult))
                s.link(nc.vector.tensor_scalar(is_end[:], nxt[:], -1.0, 1.0, ALU.mult, ALU.add))
                s.did(nc.vector.tensor_reduce(gate[:, 0:1], gap[:], AX_X, ALU.min))
                s.did(nc.vector.tensor_reduce(gate[:, 1:2], cont[:], AX_X, ALU.min))
                s.link(nc.vector.tensor_reduce(gate[:, 2:3], nxt[:], AX_X, ALU.min))

                def scan(n, out, g, v, start, op0, op1, reverse):
                    def way(ap):
                        return ap[:, ::-1] if reverse else ap[:]
                    s.link(nc.vector.tensor_tensor_scan(way(out), way(g), way(v), start, op0, op1))
                    dve.sem_inc(ask_row, 1)
                    dve.wait_ge(pe_row, n + 1)
                    s.did(nc.vector.memset(carry_r[:], start))
                    s.link(nc.vector.tensor_copy(row_s[:], ps_g[:]))
                    dst = carry_r[:, P - 1::-1] if reverse else carry_r[:, 1:P + 1]
                    s.link(nc.vector.tensor_tensor_scan(dst, way(row_s[:, 1, :]), way(row_s[:, 0, :]), start, op0, op1))
                    dve.sem_inc(ask_col, 1)
                    dve.wait_ge(pe_col, n + 1)
                    s.link(nc.vector.tensor_copy(carry_c[:], ps_c1[:]))
                    s.link(nc.vector.tensor_tensor_scan(way(out), way(g), way(v), carry_c[:, 0:1], op0, op1))

                scan(0, run, gap, lin, -BIG, ALU.add, ALU.max, False)
                s.link(nc.vector.tensor_mul(ends_v[:], run[:], is_end[:]))
                scan(1, segmax, nxt, ends_v, 0.0, ALU.mult, ALU.add, True)
                s.link(nc.vector.tensor_sub(lin[:], lin[:], segmax[:]))
                dve.sem_inc(ex, 1)
                dve.wait_ge(ex, 2)
                scan(2, run, cont, expo, 0.0, ALU.mult, ALU.add, False)
                s.link(nc.vector.tensor_mul(ends_v[:], run[:], is_end[:]))
                scan(3, segmax, nxt, ends_v, 0.0, ALU.mult, ALU.add, True)
                s.link(nc.vector.reciprocal(segmax[:], segmax[:]))
                s.link(nc.vector.tensor_mul(run[:], expo[:], segmax[:]))
                dve.sem_inc(w_ready, 1)
    if dbg and dbg["stop"] == "soft":
        dbg["scope"] = logit_scope
        return finish_debug(nc, top, sem, dbg, {"logit": logit[:], "send": send_d})

    end_phase()
    RB = 4
    assert G % RB == 0
    with ExitStack() as c:
        def sb(name, shape, dt=F32):
            return c.enter_context(nc.sbuf_tensor(name, shape, dt))
        drow = sb("w_drow", [P, RB, GE])
        emb = sb("w_emb", [P, RB, GT * D])
        same = sb("w_same", [P, RB, GT, P])
        part = sb("w_part", [P, RB, GT * D])
        ps_p = c.enter_context(nc.psum_tensor("ps_p", [P, RB, 512], F32))
        loaded = [sem(f"w_load{b}") for b in range(RB)]
        stored = [sem(f"w_st{b}") for b in range(RB)]
        weighed, summed, moved = sem("w_weighed"), sem("w_summed"), sem("w_moved")

        def turns(eng, turn):
            turn(0, True)
            with eng.Fori(1, G // RB) as i:
                turn(i, False)
        with nc.Block() as block:
            @block.sync
            def _(sp):
                def turn(i, first):
                    for b in range(RB):
                        g = i * RB + b
                        if not first:
                            sp.wait_ge(summed, i * RB + (b + 1 - RB))
                        sp.dma_start(drow[:, b, :], dst_rows(g)).then_inc(loaded[b], 16)
                        sp.dma_start(emb[:, b, :], emb_d[bass.ds(g, 1)].rearrange("a p f -> p (a f)")).then_inc(loaded[b], 16)
                turns(sp, turn)

            @block.vector
            def _(dve):
                def turn(i, first):
                    for b in range(RB):
                        dve.wait_ge(loaded[b], i * 32 + 32)
                        if not first:
                            dve.wait_ge(summed, i * RB + (b + 1 - RB))
                        for k in range(GT):
                            col = bass.ds((i * RB + b) * GT + k, 1)
                            last = nc.vector.tensor_scalar(same[:, b, k, :], drow[:, b, k * P:(k + 1) * P], dst_c[:, col],
                                                           logit[:, col], ALU.is_equal, ALU.mult)
                        last.then_inc(weighed, 1)
                turns(dve, turn)

            @block.tensor
            def _(pe):
                def turn(i, first):
                    for b in range(RB):
                        pe.wait_ge(weighed, i * RB + (b + 1))
                        if not first:
                            pe.wait_ge(moved, i * RB + (b + 1 - RB))
                        for k in range(GT):
                            mm = nc.tensor.matmul(ps_p[:, b, k * D:(k + 1) * D], same[:, b, k, :], emb[:, b, k * D:(k + 1) * D],
                                                  start=True, stop=True)
                        mm.then_inc(summed, 1)
                turns(pe, turn)

            @block.scalar
            def _(act):
                def turn(i, first):
                    for b in range(RB):
                        act.wait_ge(summed, i * RB + (b + 1))
                        if not first:
                            act.wait_ge(stored[b], i * 16)
                        nc.scalar.copy(part[:, b, :], ps_p[:, b, :]).then_inc(moved, 1)
                        act.wait_ge(moved, i * RB + (b + 1))
                        act.dma_start(part_rows(part_d, i * RB + b), part[:, b, :]).then_inc(stored[b], 16)
                turns(act, turn)
                for b in range(RB):
                    act.wait_ge(stored[b], 16 * (G // RB))
    end_phase()
    logit_scope.close()

    def close1(s):
        s.link(nc.vector.tensor_add(x_sb[:], x_sb[:], y_sb[:]))
    collect("c1", close1)
    if dbg and dbg["stop"] == "L1":
        return finish_debug(nc, top, sem, dbg, {"x": x_sb[:]})

    def sage_fill(n):
        def fill(sp, wcat, wl, extra):
            sp.dma_start(wcat[0:D, :], a[f"L2_gnn_w_self{n}"]).then_inc(wl, 16)
            sp.dma_start(wcat[D:D + 1, :], a[f"L2_gnn_b_self{n}"].rearrange("(a n) -> a n", a=1)).then_inc(wl, 16)
            return 2
        return fill

    def sage(n):
        node_product(f"s{n}", D, sage_fill(n), local=[(slice(0, D), y_sb)])
        sweep(adjT_d, f"L2_gnn_w_s2d{n}", half_in, True)
        sweep(adj_rows, f"L2_gnn_w_d2s{n}", half_out, True)

    def half_biases(s, rows):
        s.link(nc.vector.tensor_add(rows[:, 0, :], rows[:, 0, :], rows[:, 1, :]))
        s.link(nc.vector.tensor_scalar_mul(rows[:, 0, :], rows[:, 0, :], 0.5))
        s.link(nc.vector.tensor_add(y_sb[:], y_sb[:], along(rows[:, 0, :])))

    def between2(s, rows):
        half_biases(s, rows)
        s.link(nc.vector.tensor_scalar_max(h_sb[:], y_sb[:], 0.0))
        split(s)

    def close2(s, rows):
        half_biases(s, rows)
        s.link(nc.vector.tensor_add(x_sb[:], x_sb[:], y_sb[:]))
    norm_phase("2", None, True)
    sage(1)
    bias_phase("2a", ["L2_gnn_b_s2d1", "L2_gnn_b_d2s1"], None, between2)
    sage(2)
    bias_phase("2b", ["L2_gnn_b_s2d2", "L2_gnn_b_d2s2"], None, close2)
    if dbg and dbg["stop"] == "L2":
        return finish_debug(nc, top, sem, dbg, {"x": x_sb[:]})

    norm_phase("3", None, False)

    def hidden_fill(sp, wcat, wl, extra):
        sp.dma_start(wcat[0:D, :], a["L3_gnn_W1n"]).then_inc(wl, 16)
        sp.dma_start(wcat[D:D + 1, :], a["L3_gnn_b1n"].rearrange("(a n) -> a n", a=1)).then_inc(wl, 16)
        return 2
    node_product("n3", D, hidden_fill, stores=[(slice(0, D), xt_d)], hidden=True)

    with ExitStack() as c:
        def sb(name, shape, dt=F32):
            return c.enter_context(nc.sbuf_tensor(name, shape, dt))
        idx = sb("g_idx", [P, RB, GT], I32)
        xg = sb("g_xg", [P, RB, GT, D])
        drow = sb("g_drow", [P, RB, GE])
        attr = sb("g_attr", [DE + 1, RB, GE])
        w1 = sb("g_w1", [DE + 1, P])
        w2 = sb("g_w2", [P, D])
        b2 = sb("g_b2", [1, GT, D])
        one_r = sb("g_one", [1, P])
        hid = sb("g_hid", [P, 2, GE])
        same = sb("g_same", [P, RB, GT, P])
        msg = sb("g_msg", [P, RB, GT * D])
        part = sb("g_part", [P, RB, GT * D])
        ps_1 = c.enter_context(nc.psum_tensor("ps_1", [P, 2, 2, 512], F32))
        ps_e = c.enter_context(nc.psum_tensor("ps_e", [P, 2, 512], F32))
        ps_p = c.enter_context(nc.psum_tensor("ps_p3", [P, 2, 512], F32))
        gathered = [sem(f"g_gat{b}", keep=True) for b in range(RB)]
        loaded = [sem(f"g_load{b}") for b in range(RB)]
        stored = [sem(f"g_st{b}") for b in range(RB)]
        wl, prep, fetched, h1, relued, gates, compared, msgs, summed, moved = (
            sem(n) for n in ("g_w", "g_prep", "g_idx_s", "g_h1", "g_relu", "g_gates", "g_same_s", "g_msgs", "g_sum", "g_moved"))
        with nc.Block() as block:
            @block.sync
            def _(sp):
                row = lambda n: a[n].rearrange("(a n) -> a n", a=1)
                for half in range(2):
                    sp.dma_start(w1[0:DE, half * D:(half + 1) * D], a["L3_gnn_W1e"]).then_inc(wl, 16)
                    sp.dma_start(w1[DE:DE + 1, half * D:(half + 1) * D], row("L3_gnn_b1e")).then_inc(wl, 16)
                    sp.dma_start(w2[half * D:(half + 1) * D, :], a["L3_gnn_W2e"]).then_inc(wl, 16)
                for k in range(GT):
                    sp.dma_start(b2[:, k, :], row("L3_gnn_b2e")).then_inc(wl, 16)

                def turn(i, first):
                    for b in range(RB):
                        g = i * RB + b
                        if not first:
                            sp.wait_ge(h1, i * RB + (b + 1 - RB))
                            sp.wait_ge(compared, i * RB + (b + 1 - RB))
                        sp.dma_start(attr[0:DE, b, :], a["attr_T"][:, bass.ds(g * GE, GE)]).then_inc(loaded[b], 16)
                        sp.dma_start(drow[:, b, :], dst_rows(g)).then_inc(loaded[b], 16)
                turns(sp, turn)

            @block.gpsimd
            def _(pool):
                def turn(i, first):
                    for b in range(RB):
                        pool.wait_ge(fetched, i * RB + (b + 1))
                        pool.nop(nofuse=True)
                        if not first:
                            pool.wait_ge(msgs, i * RB + (b + 1 - RB))
                            pool.nop(nofuse=True)
                        for k in range(GT):
                            nc.gpsimd.indirect_dma_start(
                                xg[:, b, k, :], None, xt_d,
                                bass.IndirectOffsetOnAxis(ap=idx[:, b, k:k + 1], axis=0)).then_inc(gathered[b], 16)
                turns(pool, turn)

            @block.tensor
            def _(pe):
                pe.wait_ge(prep, 5)

                def turn(i, first):
                    for b in range(RB):
                        g = i * RB + b
                        pe.wait_ge(loaded[b], i * 32 + 32)
                        if not (first and b < 2):
                            pe.wait_ge(relued, i * RB + (b - 1))
                        for half in range(2):
                            mm = nc.tensor.matmul(ps_1[:, b % 2, half, :], w1[:], attr[:, b, half * 512:(half + 1) * 512],
                                                  start=True, stop=True)
                        mm.then_inc(h1, 1)
                        pe.wait_ge(relued, i * RB + (b + 1))
                        if not (first and b < 2):
                            pe.wait_ge(msgs, i * RB + (b - 1))
                        nc.tensor.matmul(ps_e[:, b % 2, :], one_r[:], b2[:].rearrange("a k d -> a (k d)"), start=True, stop=False)
                        for k in range(GT):
                            mm = nc.tensor.matmul(ps_e[:, b % 2, k * D:(k + 1) * D], hid[:, b % 2, k * P:(k + 1) * P], w2[:],
                                                  start=False, stop=k == GT - 1)
                        mm.then_inc(gates, 1)
                        if not (first and b == 0):
                            sums(i if b else i - 1, (b - 1) % RB, first and b <= 2)

                def sums(i, b, first):
                    pe.wait_ge(msgs, i * RB + (b + 1))
                    pe.wait_ge(compared, i * RB + (b + 1))
                    if not first:
                        pe.wait_ge(moved, i * RB + (b - 1))
                    for k in range(GT):
                        mm = nc.tensor.matmul(ps_p[:, b % 2, k * D:(k + 1) * D], same[:, b, k, :], msg[:, b, k * D:(k + 1) * D],
                                              start=True, stop=True)
                    mm.then_inc(summed, 1)
                turns(pe, turn)
                sums(G // RB - 1, RB - 1, False)

            @block.scalar
            def _(act):
                def store(i, b, first):
                    act.wait_ge(summed, i * RB + (b + 1))
                    if not first:
                        act.wait_ge(stored[b], i * 16)
                    nc.scalar.copy(part[:, b, :], ps_p[:, b % 2, :]).then_inc(moved, 1)
                    act.wait_ge(moved, i * RB + (b + 1))
                    act.dma_start(part_rows(part_d, i * RB + b), part[:, b, :]).then_inc(stored[b], 16)

                def turn(i, first, second=False):
                    for b in range(RB):
                        act.wait_ge(h1, i * RB + (b + 1))
                        if not (first and b < 2):
                            act.wait_ge(gates, i * RB + (b - 1))
                        nc.scalar.activation(hid[:, b % 2, :], ps_1[:, b % 2].rearrange("p a n -> p (a n)"), ACT.Relu) \
                            .then_inc(relued, 1)
                        if b > 0:
                            store(i, b - 1, first)
                        elif not first:
                            store(i - 1, RB - 1, second)
                turn(0, True)
                turn(1, False, True)
                with act.Fori(2, G // RB) as i:
                    turn(i, False)
                store(G // RB - 1, RB - 1, False)
                for b in range(RB):
                    act.wait_ge(stored[b], 16 * (G // RB))

            @block.vector
            def _(dve):
                nc.vector.memset(attr[DE:DE + 1], 1.0).then_inc(prep, 1)
                nc.vector.memset(one_r[:], 1.0).then_inc(prep, 1)
                dve.wait_ge(wl, 16 * (6 + GT))
                nc.vector.tensor_scalar_mul(w1[:, D:P], w1[:, D:P], -1.0).then_inc(prep, 1)
                nc.vector.tensor_scalar_mul(w2[D:P, :], w2[D:P, :], -0.1).then_inc(prep, 1)
                dve.sem_inc(prep, 1)
                for b in range(RB):
                    nc.vector.tensor_copy(idx[:, b, :], src_c[:, b * GT:(b + 1) * GT]).then_inc(fetched, 1)

                def turn(i, first, last=False):
                    for b in range(RB):
                        g = i * RB + b
                        dve.wait_ge(loaded[b], i * 32 + 32)
                        if not first:
                            dve.wait_ge(summed, i * RB + (b + 1 - RB))
                        nc.vector.tensor_tensor(
                            same[:, b], drow[:, b, :].rearrange("p (k e) -> p k e", k=GT),
                            dst_c[:, bass.ds(g * GT, GT)].unsqueeze(2).to_broadcast([P, GT, P]),
                            ALU.is_equal).then_inc(compared, 1)
                        dve.wait_ge(gathered[b], i * (16 * GT) + 16 * GT)
                        dve.wait_ge(gates, i * RB + (b + 1))
                        if not last:
                            nc.vector.tensor_copy(idx[:, b, :], src_c[:, bass.ds((g + RB) * GT, GT)]).then_inc(fetched, 1)
                        nc.vector.tensor_mul(msg[:, b, :], ps_e[:, b % 2, :], xg[:, b].rearrange("p k d -> p (k d)")) \
                            .then_inc(msgs, 1)
                turn(0, True)
                with dve.Fori(1, G // RB - 1) as i:
                    turn(i, False)
                turn(G // RB - 1, False, True)

    end_phase()
    with ExitStack() as c:
        rows = c.enter_context(nc.sbuf_tensor("rows3", [P, 2, D], F32))
        res = c.enter_context(nc.sbuf_tensor("res3", [P, 1], F32))
        mean, var, std, rstd = (c.enter_context(nc.sbuf_tensor(n, [P, NT], F32)) for n in ("mean4", "var4", "std4", "rstd4"))
        wl = sem("f_w", keep=True)
        with nc.Block() as block:
            @block.sync
            def _(sp):
                sp.dma_start(rows[:, 0, :], row_of("L3_gnn_gamma")).then_inc(wl, 16)
                sp.dma_start(rows[:, 1, :], row_of("L3_gnn_beta")).then_inc(wl, 16)
                sp.dma_start(res[:], row_of("L3_gnn_res_w", 1)).then_inc(wl, 16)
                sp.wait_ge(wl, 48)
        def close3(s):
            s.link(nc.vector.scalar_tensor_tensor(out=h_sb[:].rearrange("p t d -> p (t d)"),
                                                  in0=y_sb[:].rearrange("p t d -> p (t d)"), scalar=res[:, 0:1],
                                                  in1=h_sb[:].rearrange("p t d -> p (t d)"), op0=ALU.mult, op1=ALU.add))
            s.link(nc.vector.tensor_reduce(mean[:], h_sb[:], AX_X, ALU.add))
            s.link(nc.vector.tensor_scalar_mul(mean[:], mean[:], 1.0 / D))
            s.link(nc.vector.tensor_sub(h_sb[:], h_sb[:], each(mean[:])))
            s.link(nc.vector.tensor_mul(t_sb[:], h_sb[:], h_sb[:]))
            s.link(nc.vector.tensor_reduce(var[:], t_sb[:], AX_X, ALU.add))
            s.link(nc.vector.tensor_scalar(var[:], var[:], 1.0 / D, EPS, ALU.mult, ALU.add))
        collect("c3", close3)
        done, vs, rooted = sem("f_done"), sem("f_dve"), sem("f_root")
        full = N_NODES // P
        with nc.Block() as block:
            @block.scalar
            def _(act):
                nc.scalar.sqrt(std[:], var[:]).then_inc(rooted, 1)

            @block.vector
            def _(dve):
                s = Steps(dve, vs)
                dve.wait_ge(rooted, 1)
                s.link(nc.vector.reciprocal(rstd[:], std[:]))
                s.link(nc.vector.tensor_mul(h_sb[:], h_sb[:], each(rstd[:])))
                s.link(nc.vector.tensor_mul(h_sb[:], h_sb[:], along(rows[:, 0, :])))
                s.link(nc.vector.tensor_add(h_sb[:], h_sb[:], along(rows[:, 1, :])))
                s.link(nc.vector.tensor_add(x_sb[:], x_sb[:], h_sb[:]))
                dve.sem_inc(done, 1)

            @block.sync
            def _(sp):
                if out is not None:
                    sp.wait_ge(done, 1)
                    sp.dma_start(out[0:full * P, :].rearrange("(t p) d -> p t d", p=P), x_sb[:, 0:full, :]).then_inc(wl, 16)
                    sp.dma_start(out[full * P:N_NODES, :], x_sb[0:N_NODES - full * P, full, :]).then_inc(wl, 16)
                    sp.wait_ge(wl, 48 + 32)
    if dbg and dbg["stop"] == "L3":
        return finish_debug(nc, top, sem, dbg, {"x": x_sb[:]})
    passing["scope"].close()
    top.close()


def finish_debug(nc, top, sem, dbg, what):
    s = sem("dbg", keep=True)
    with nc.Block() as block:
        @block.sync
        def _(sp):
            n = 0
            for name, src in what.items():
                if name in dbg["aps"]:
                    sp.dma_start(dbg["aps"][name], src).then_inc(s, 16)
                    n += 16
            sp.wait_ge(s, n)
    if "scope" in dbg:
        dbg["scope"].close()
    top.close()


def layout(inputs):
    import numpy as np

    arrays = {k: np.ascontiguousarray(v) for k, v in inputs.items() if k.startswith("L")}
    x = np.zeros((NP, D), np.float32)
    x[:N_NODES] = inputs["x"]
    arrays["x"] = x
    pad = np.arange(EP - E_EDGES, dtype=np.int32) % (NP - N_NODES) + N_NODES
    src = np.concatenate([np.asarray(inputs["src"]), pad])
    dst = np.concatenate([np.asarray(inputs["dst"]), np.full(EP - E_EDGES, NP - 1, np.int32)])
    for name, v in (("src", src), ("dst", dst)):
        arrays[f"{name}_lin"] = v.reshape(P, T)
        arrays[f"{name}_col"] = np.ascontiguousarray(v.reshape(T, P).T)
    attr = np.zeros((DE, EP), np.float32)
    attr[:, :E_EDGES] = np.asarray(inputs["edge_attr_32"]).T
    arrays["attr_T"] = attr
    arrays["L1_We_T"] = np.ascontiguousarray(
        np.concatenate([np.asarray(inputs["L1_gnn_We_k"]).reshape(D, D), np.asarray(inputs["L1_gnn_We_b"])]).T)
    return arrays


def kernel(**inputs):
    import concourse.bacc as _bacc
    from concourse.bass_utils import run_bass_kernel_spmd as _run

    nc = _bacc.Bacc("TRN2", target_bir_lowering=False, num_devices=1)
    arrays, aps = {}, {}
    for name, v in layout(inputs).items():
        arrays[f"in_{name}_dram"] = v
        aps[name] = nc.dram_tensor(f"in_{name}_dram", v.shape, mybir.dt.from_np(v.dtype), kind="ExternalInput").ap()
    out = nc.dram_tensor("out_dram", (N_NODES, D), F32, kind="ExternalOutput").ap()
    build_program(nc, aps, out, None)
    r = _run(nc, [arrays], core_ids=[0])
    return r.results[0]["out_dram"]
```

```python
from contextlib import ExitStack

import concourse.bass as bass
from concourse import mybir

ALU = mybir.AluOpType
ACT = mybir.ActivationFunctionType
AX_X = mybir.AxisListType.X
F32 = mybir.dt.float32
BF16 = mybir.dt.bfloat16
I32 = mybir.dt.int32

P = 128
N_NODES, D, E_EDGES, DE = 6250, 64, 200000, 32
NT = 49
NP = NT * P
NB = 7
NBLK = NT // NB
BW = NB * P
SPLIT = (4 * P, (NB - 4) * P)
GT = 8
GE = GT * P
G = -(-E_EDGES // GE)
EP = G * GE
T = G * GT
GH = G // 2
SHIFT = 13
PITCH = 1 << SHIFT
TAG = 0x40000000
LESS = 2048.0
SHORT = 256
EPS = 1e-5
BIG = 1e30
RB = 4
assert G % RB == 0
assert NP >= N_NODES and G % 2 == 0 and GE + NP <= PITCH and LESS > GE


class Steps:

    def __init__(self, eng, sem, base=0, turn=0, per=0):
        self.eng, self.sem, self.base, self.turn, self.per, self.n = eng, sem, base, turn, per, 0

    def did(self, instruction, by=1):
        instruction.then_inc(self.sem, by)
        self.n += by

    def wait(self):
        self.eng.wait_ge(self.sem, self.turn * self.per + self.base + self.n)

    def link(self, instruction):
        self.did(instruction)
        self.wait()


def prefetch_row(dram, row, width):
    return dram.rearrange("(a n) -> a n", a=1)[:, bass.ds(row, width)].to_broadcast([P, width])


def build_program(nc, a, out, dbg):
    top = ExitStack()

    passing = {"scope": ExitStack(), "numbers": []}

    def sem(name, keep=False):
        if keep:
            return top.enter_context(nc.semaphore(name))
        handle = passing["scope"].enter_context(nc.semaphore(name))
        passing["numbers"].append(handle)
        return handle

    def end_phase():
        numbers = sorted(h.num for h in passing["numbers"])
        while numbers:
            n = 1
            while n < len(numbers) and numbers[n] == numbers[0] + n:
                n += 1
            nc.gpsimd.sem_clear(range(numbers[0], numbers[0] + n))
            numbers = numbers[n:]
        nc.all_engine_barrier()
        passing["scope"].close()
        passing["scope"], passing["numbers"] = ExitStack(), []

    def turns(eng, turn):
        turn(0, True)
        with eng.Fori(1, G // RB) as i:
            turn(i, False)

    def dram(name, shape, dt):
        return nc.dram_tensor(name, shape, dt).ap()

    key_d = dram("key_d", (EP,), I32)
    dst2_d = dram("dst2_d", (2, EP), BF16)
    dstf_d = dram("dstf_d", (EP + 2,), F32)
    adj_d = dram("adj_d", (NP * PITCH, 1), BF16)
    adjT_d = dram("adjT_d", (NP, NP), BF16)
    adj_rows = adj_d.rearrange("(d s) o -> d (s o)", s=PITCH)
    send_d = dram("send_d", (NP, 2 * D), F32)
    recv_d = dram("recv_d", (NP, D), F32)
    recvz_d = dram("recvz_d", (EP + NP, D), F32)
    emb_d = dram("emb_d", (G, P, GT * D), F32)
    part_d = dram("part_d", (EP, D), F32)
    gate_d = dram("gate_d", (G, P, GT * D), F32)
    xt_d = dram("xt_d", (NP, D), F32)
    lin_d = dram("lin_d", (EP,), F32)
    wgt_d = dram("wgt_d", (EP,), F32)

    def keep(name, shape, dt):
        return top.enter_context(nc.sbuf_tensor(name, shape, dt))

    x_sb = keep("x_sb", [P, NT, D], F32)
    y_sb = keep("y_sb", [P, NT, D], F32)
    h_sb = keep("h_sb", [P, NT, D], F32)
    t_sb = keep("t_sb", [P, NT, D], F32)
    h3 = keep("h3", [P, NT, 3 * D], BF16)
    src_c = keep("src_c", [P, T], I32)
    dst_c = keep("dst_c", [P, T], F32)
    ident = keep("ident", [P, P], F32)
    identb = keep("identb", [P, P], BF16)
    deg_in = keep("deg_in", [P, NT], F32)
    deg_out = keep("deg_out", [P, NT], F32)
    norm_in = keep("norm_in", [P, NT], F32)
    norm_out = keep("norm_out", [P, NT], F32)
    half_in = keep("half_in", [P, NT], F32)
    half_out = keep("half_out", [P, NT], F32)
    end_row = keep("end_row", [P, NT], I32)
    start_row = keep("start_row", [P, NT], I32)
    own_end = keep("own_end", [P, NT], F32)
    alive = keep("alive", [P, NT], F32)
    carry_row = keep("carry_row", [P, 2, NT], I32)
    carried = keep("carried", [P, 2, NT], F32)
    long_i = keep("long_i", [1, 1], I32)
    first_id = keep("first_id", [P, 2, GT], I32)
    last_id = keep("last_id", [P, 2, GT], F32)

    with ExitStack() as c:
        def sb(name, shape, dt):
            return c.enter_context(nc.sbuf_tensor(name, shape, dt))
        dst_ci = sb("dst_ci", [P, T], I32)
        lin_s = sb("lin_s", [P, T], I32)
        lin_t = sb("lin_t", [P, T], I32)
        key_l = sb("key_l", [P, T], I32)
        key_k = sb("key_k", [P, T], I32)
        dstf_l = sb("dstf_l", [P, T], F32)
        minus1 = sb("minus1", [P, 2], F32)
        far_i = sb("far_i", [P, T], I32)
        far = sb("far", [P, T], F32)
        same_far = sb("same_far", [P, T], F32)
        any_far = sb("any_far", [P, 1], F32)
        one_c = sb("one_c", [P, 1], F32)
        long_f = sb("long_f", [1, 1], F32)
        ps_long = c.enter_context(nc.psum_tensor("ps_long", [1, 1], F32))
        dst2_i = sb("dst2_i", [P, 2, T], I32)
        dst2_l = sb("dst2_l", [P, 2, T], BF16)
        zero_b = sb("zero_b", [P, NP], BF16)
        firsts = sb("firsts", [P, 2, GT], F32)
        ld, st, zr, vs, ids, st2, fld, fs, fm = (sem(n) for n in (
            "p_load", "p_store", "p_zeroed", "p_dve", "p_ident", "p_bounds", "p_far_load", "p_far", "p_long"))
        with nc.Block() as block:
            @block.sync
            def _(sp):
                sp.dma_start(lin_s[:], a["src_lin"]).then_inc(ld, 16)
                sp.dma_start(lin_t[:], a["dst_lin"]).then_inc(ld, 16)
                sp.dma_start(src_c[:], a["src_col"]).then_inc(ld, 16)
                sp.dma_start(dst_ci[:], a["dst_col"]).then_inc(ld, 16)
                sp.dma_start(x_sb[:], a["x"].rearrange("(t p) d -> p t d", p=P)).then_inc(ld, 16)
                sp.wait_ge(fs, 1)
                flat = a["dst_lin"].rearrange("p j -> (p j)")
                sp.dma_start(far_i[0:P - 1, :], flat[SHORT:SHORT + (P - 1) * T].rearrange("(p j) -> p j", j=T)).then_inc(fld, 16)
                sp.dma_start(far_i[P - 1:P, 0:T - SHORT],
                             flat[SHORT + (P - 1) * T:EP].rearrange("(a j) -> a j", a=1)).then_inc(fld, 16)
                sp.wait_ge(vs, 9)
                for r in range(2):
                    sp.dma_start(dst2_d[r].rearrange("(p j) -> p j", p=P), dst2_l[:, r, :]).then_inc(st, 16)
                sp.dma_start(key_d.rearrange("(p j) -> p j", p=P), key_l[:]).then_inc(st, 16)
                sp.dma_start(dstf_d[1:EP + 1].rearrange("(p j) -> p j", p=P), dstf_l[:]).then_inc(st, 16)
                sp.dma_start(dstf_d[0:1].rearrange("(a j) -> a j", a=1), minus1[0:1, 0:1]).then_inc(st, 16)
                sp.dma_start(dstf_d[EP + 1:EP + 2].rearrange("(a j) -> a j", a=1), minus1[0:1, 1:2]).then_inc(st, 16)
                sp.wait_ge(st, 96)
                ends = dstf_d[1:EP + 1].rearrange("(h g k p) -> g h k p", h=2, k=GT, p=P)
                with nc.allow_non_contiguous_dma(reason="one number of each tile"):
                    for h in range(2):
                        sp.dma_start(firsts[0:GH, h, :], ends[:, h, :, 0]).then_inc(st2, 16)
                        sp.dma_start(last_id[0:GH, h, :], ends[:, h, :, P - 1]).then_inc(st2, 16)
                sp.wait_ge(st2, 64)
                sp.wait_ge(ld, 80)

            @block.scalar
            def _(act):
                act.wait_ge(vs, 1)
                with act.Fori(0, NT) as i:
                    act.dma_start(adj_rows[bass.ds(i * P, P), 0:NP], zero_b[:]).then_inc(zr, 16)
                act.dma_start(adj_rows[0:2, NP:NP + GE], zero_b[0:2, 0:GE]).then_inc(zr, 16)
                act.wait_ge(zr, 16 * (NT + 1))

            @block.tensor
            def _(pe):
                pe.wait_ge(fs, 5)
                nc.tensor.matmul(ps_long[:], any_far[:], one_c[:], start=True, stop=True).then_inc(fm, 1)

            @block.gpsimd
            def _(pool):
                nc.gpsimd.memset(ident[:], 0.0).then_inc(ids, 1)
                pool.wait_ge(ids, 1)
                nc.gpsimd.affine_select(out=ident[:], in_=ident[:], compare_op=ALU.not_equal, fill=1.0, base=0,
                                        pattern=[[-1, P]], channel_multiplier=1).then_inc(ids, 1)

            @block.vector
            def _(dve):
                s = Steps(dve, vs)
                fars = Steps(dve, fs)
                fars.did(nc.vector.memset(far_i[:], -1))
                fars.did(nc.vector.memset(one_c[:], 1.0))
                s.did(nc.vector.memset(zero_b[:], 0.0))
                s.did(nc.vector.memset(minus1[:], -1.0))
                dve.wait_ge(ld, 80)
                s.did(nc.vector.tensor_scalar(dst2_i[:, 0, :], lin_t[:], -32, None, ALU.bitwise_and))
                s.did(nc.vector.tensor_scalar(dst2_i[:, 1, :], lin_t[:], 31, None, ALU.bitwise_and))
                s.link(nc.vector.tensor_scalar(key_k[:], lin_t[:], SHIFT, TAG, ALU.logical_shift_left, ALU.bitwise_or))
                s.did(nc.vector.tensor_tensor(key_l[:], key_k[:], lin_s[:], ALU.bitwise_or))
                s.did(nc.vector.tensor_copy(dst2_l[:], dst2_i[:]))
                s.did(nc.vector.tensor_copy(dstf_l[:], lin_t[:]))
                s.did(nc.vector.tensor_copy(dst_c[:], dst_ci[:]))
                dve.wait_ge(ids, 2)
                s.did(nc.vector.tensor_copy(identb[:], ident[:]))
                dve.wait_ge(fld, 32)
                fars.link(nc.vector.tensor_copy(far[:], far_i[:]))
                fars.link(nc.vector.tensor_tensor(same_far[:], far[:], dstf_l[:], ALU.is_equal))
                fars.link(nc.vector.tensor_reduce(any_far[:], same_far[:], AX_X, ALU.max))
                dve.wait_ge(fm, 1)
                fars.link(nc.vector.tensor_scalar_min(long_f[:], ps_long[:], 1.0))
                fars.did(nc.vector.tensor_copy(long_i[:], long_f[:]))
                dve.wait_ge(st2, 64)
                s.did(nc.vector.tensor_copy(first_id[0:GH], firsts[0:GH]))

    end_phase()
    long_flag = nc.values_load(long_i[0:1, 0:1], min_val=0, max_val=1)

    def either(program):
        with nc.If(long_flag > 0):
            program(False)
        with nc.Else():
            program(True)

    with ExitStack() as c:
        def sb(name, shape, dt):
            return c.enter_context(nc.sbuf_tensor(name, shape, dt))
        key_row = sb("key_row", [P, 2, GE], I32)
        key_c = sb("key_c", [P, T], I32)
        key_ck = sb("key_ck", [P, T], I32)
        dst_k = sb("dst_k", [P, T], I32)
        earlier = sb("earlier", [P, 2 * GE - P], F32)
        junk = sb("junk", [P, GT, GE], BF16)
        tally = sb("tally", [P, 2, GT], F32)
        again = sb("again", [P, 2, GT], I32)
        slot = sb("slot", [P, 2, GT], I32)
        count = sb("count", [P, 2, GT], BF16)
        dump = sb("dump", [P, 2, GT], I32)
        zero_f = sb("zero_f", [P, 8 * GT * D], F32)
        attr = sb("g_attr", [DE + 1, RB, GE], F32)
        w1 = sb("g_w1", [DE + 1, P], F32)
        w2 = sb("g_w2", [P, D], F32)
        b2 = sb("g_b2", [1, GT, D], F32)
        b2_left = sb("g_b2left", [1, GT, D], F32)
        b2_part = sb("g_b2part", [1, 3, GT * D], BF16)
        one_r = sb("g_one", [1, P], BF16)
        hid = sb("g_hid", [P, 2, GE], F32)
        gates = sb("g_gates", [P, RB, GT * D], F32)
        ps_1 = c.enter_context(nc.psum_tensor("ps_1", [P, 2, 2, 512], F32))
        ps_e = c.enter_context(nc.psum_tensor("ps_e", [P, 2, 512], F32))
        wl, prep, h1, relued, gated, moved = (sem(n) for n in ("g_w", "g_prep", "g_h1", "g_relu", "g_gated", "g_moved"))
        attr_in = [sem(f"g_attr{b}") for b in range(RB)]
        stored = [sem(f"g_st{b}") for b in range(RB)]
        ld0, vs0 = sem("b_load0"), sem("b_dve0")
        rows = [sem("b_row0"), sem("b_row1")]
        pool0, zr2 = sem("b_pool0"), sem("b_zeroed")
        vs1, ready = sem("b_dve"), sem("b_ready")
        landed = [sem(f"b_landed{half}", keep=True) for half in range(2)]
        def build(short):
            def group(i, b):
                return i + b * GH if short else i * 2 + b

            def window(k):
                return (max(0, k * P - SHORT), min(GE, k * P + P + SHORT)) if short else (0, GE)

            with nc.Block() as block:
                @block.sync
                def _(sp):
                    sp.dma_start(dst_k[:], a["dst_col"]).then_inc(ld0, 16)
                    row = lambda n: a[n].rearrange("(a n) -> a n", a=1)
                    for half in range(2):
                        sp.dma_start(w1[0:DE, half * D:(half + 1) * D], a["L3_gnn_W1e"]).then_inc(wl, 16)
                        sp.dma_start(w1[DE:DE + 1, half * D:(half + 1) * D], row("L3_gnn_b1e")).then_inc(wl, 16)
                        sp.dma_start(w2[half * D:(half + 1) * D, :], a["L3_gnn_W2e"]).then_inc(wl, 16)
                    for k in range(GT):
                        sp.dma_start(b2[:, k, :], row("L3_gnn_b2e")).then_inc(wl, 16)
                    for b in range(2):
                        sp.dma_start(key_row[:, b, :], prefetch_row(key_d, group(0, b) * GE, GE)).then_inc(rows[b], 16)
                    with sp.Fori(1, G // 2) as i:
                        for b in range(2):
                            sp.wait_ge(ready, i * 2 + (b - 1))
                            sp.dma_start(key_row[:, b, :], prefetch_row(key_d, group(i, b) * GE, GE)).then_inc(rows[b], 16)
                    for b in range(2):
                        sp.wait_ge(rows[b], 16 * (G // 2))

                @block.scalar
                def _(act):
                    act.wait_ge(vs0, 4)
                    zrows = (EP + NP) // P
                    zv = recvz_d.rearrange("(p r) d -> p (r d)", p=P)
                    step = 8 * GT
                    n = 0
                    for r in range(0, zrows, step):
                        w = min(step, zrows - r)
                        act.dma_start(zv[:, r * D:(r + w) * D], zero_f[:, 0:w * D]).then_inc(zr2, 16)
                        n += 1

                    def attributes(g, b):
                        act.dma_start(attr[0:DE, b, :], a["attr_T"][:, bass.ds(g * GE, GE)]).then_inc(attr_in[b], 16)

                    def store(i, b, first):
                        act.wait_ge(gated, i * RB + (b + 1))
                        if not first:
                            act.wait_ge(stored[b], i * 16)
                        nc.scalar.copy(gates[:, b, :], ps_e[:, b % 2, :]).then_inc(moved, 1)
                        act.wait_ge(moved, i * RB + (b + 1))
                        act.dma_start(gate_d[bass.ds(i * RB + b, 1)].rearrange("a p f -> p (a f)"), gates[:, b, :]) \
                            .then_inc(stored[b], 16)

                    def turn(i, first, last=False):
                        for b in range(RB):
                            act.wait_ge(h1, i * RB + (b + 1))
                            if not last:
                                attributes(i * RB + (b + RB), b)
                            if not (first and b < 2):
                                act.wait_ge(gated, i * RB + (b - 1))
                            nc.scalar.activation(hid[:, b % 2, :], ps_1[:, b % 2].rearrange("p a n -> p (a n)"), ACT.Relu) \
                                .then_inc(relued, 1)
                            if not (first and b == 0):
                                store(i if b else i - 1, (b - 1) % RB, first)
                    for b in range(RB):
                        attributes(b, b)
                    turn(0, True)
                    with act.Fori(1, G // RB - 1) as i:
                        turn(i, False)
                    turn(G // RB - 1, False, True)
                    store(G // RB - 1, RB - 1, False)
                    for b in range(RB):
                        act.wait_ge(stored[b], 16 * (G // RB))
                    act.wait_ge(zr2, 16 * n)

                @block.tensor
                def _(pe):
                    pe.wait_ge(prep, 5)

                    def hidden(i, b, first):
                        pe.wait_ge(attr_in[b], i * 16 + 16)
                        if not (first and b < 2):
                            pe.wait_ge(relued, i * RB + (b - 1))
                        for half in range(2):
                            mm = nc.tensor.matmul(ps_1[:, b % 2, half, :], w1[:], attr[:, b, half * 512:(half + 1) * 512],
                                                  start=True, stop=True)
                        mm.then_inc(h1, 1)

                    def gate(i, b, first):
                        pe.wait_ge(relued, i * RB + (b + 1))
                        if not (first and b < 2):
                            pe.wait_ge(moved, i * RB + (b - 1))
                        for part in range(3):
                            nc.tensor.matmul(ps_e[:, b % 2, :], one_r[:], b2_part[:, part, :], start=part == 0, stop=False)
                        for k in range(GT):
                            mm = nc.tensor.matmul(ps_e[:, b % 2, k * D:(k + 1) * D], hid[:, b % 2, k * P:(k + 1) * P], w2[:],
                                                  start=False, stop=k == GT - 1)
                        mm.then_inc(gated, 1)

                    def turn(i, first):
                        for b in range(RB):
                            hidden(i, b, first)
                            if not (first and b == 0):
                                gate(i if b else i - 1, (b - 1) % RB, first and b > 0)
                    turns(pe, turn)
                    gate(G // RB - 1, RB - 1, False)

                @block.vector
                def _(dve):
                    s = Steps(dve, vs0)
                    dve.wait_ge(ld0, 16)
                    s.link(nc.vector.tensor_scalar(key_ck[:], dst_k[:], SHIFT, TAG, ALU.logical_shift_left, ALU.bitwise_or))
                    s.did(nc.vector.tensor_tensor(key_c[:], key_ck[:], src_c[:], ALU.bitwise_or))
                    s.did(nc.vector.memset(earlier[:], 1.0))
                    s.link(nc.vector.memset(zero_f[:], 0.0))
                    nc.vector.memset(attr[DE:DE + 1], 1.0).then_inc(prep, 1)
                    nc.vector.memset(one_r[:], 1.0).then_inc(prep, 1)
                    dve.wait_ge(wl, 16 * (6 + GT))
                    nc.vector.tensor_scalar_mul(w1[:, D:P], w1[:, D:P], -1.0).then_inc(prep, 1)
                    nc.vector.tensor_scalar_mul(w2[D:P, :], w2[D:P, :], -0.1).then_inc(prep, 1)
                    for part in range(3):
                        left = b2 if part == 0 else b2_left
                        s.link(nc.vector.tensor_copy(b2_part[:, part, :], left[:].rearrange("a k d -> a (k d)")))
                        s.link(nc.vector.tensor_sub(b2_left[:].rearrange("a k d -> a (k d)"),
                                                    left[:].rearrange("a k d -> a (k d)"), b2_part[:, part, :]))
                    dve.sem_inc(prep, 1)
                    dve.wait_ge(pool0, 2)
                    def turn(i, first):
                        t = Steps(dve, vs1, turn=i, per=5 * 2)
                        for b in range(2):
                            dve.wait_ge(rows[b], i * 16 + 16)
                            for k in range(GT):
                                lo, hi = window(k)
                                col = bass.ds(group(i, b) * GT + k, 1)
                                w = earlier[:, GE - P - k * P + lo:GE - P - k * P + hi]
                                last = nc.vector.scalar_tensor_tensor(
                                    out=junk[:, k, lo:hi], in0=key_row[:, b, lo:hi].bitcast(F32), scalar=key_c[:, col].bitcast(F32),
                                    in1=w, op0=ALU.is_equal, op1=ALU.mult, accum_out=tally[:, b, k:k + 1])
                            t.link(last)
                            t.did(nc.vector.tensor_scalar(again[:, b, :], tally[:, b, :], LESS, None, ALU.is_ge))
                            if not first:
                                if short:
                                    dve.wait_ge(landed[b], i * (16 * GT))
                                else:
                                    dve.wait_ge(landed[0], (i * 2 + (b - 1)) * 16 * GT)
                            t.did(nc.vector.tensor_copy(count[:, b, :], tally[:, b, :]))
                            t.link(nc.vector.tensor_scalar(slot[:, b, :], key_c[:, bass.ds(group(i, b) * GT, GT)], TAG - 1, None,
                                                           ALU.bitwise_and))
                            dve.nop(nofuse=True)
                            t.did(nc.vector.copy_predicated(slot[:, b, :], again[:, b, :], dump[:, b, :]))
                            t.wait()
                            dve.sem_inc(ready, 1)

                    turn(0, True)
                    with dve.Fori(1, G // 2) as i:
                        turn(i, False)

                @block.gpsimd
                def _(pool):
                    pool.wait_ge(vs0, 3)
                    nc.gpsimd.affine_select(out=earlier[:], in_=earlier[:], compare_op=ALU.is_ge, fill=1.0 + LESS,
                                            base=-(GE - P), pattern=[[1, 2 * GE - P]],
                                            channel_multiplier=-1).then_inc(pool0, 1)
                    nc.gpsimd.iota(dump[:], pattern=[[PITCH, 2], [P, GT]], base=NP, channel_multiplier=1).then_inc(pool0, 1)
                    def turn(i, first):
                        for b in range(2):
                            pool.wait_ge(ready, i * 2 + (b + 1))
                            pool.nop(nofuse=True)
                            if short and not first:
                                pool.wait_ge(landed[b], i * (16 * GT))
                                pool.nop(nofuse=True)
                            elif not short and not (first and b == 0):
                                pool.wait_ge(landed[0], (i * 2 + b) * 16 * GT)
                                pool.nop(nofuse=True)
                            for k in range(GT):
                                nc.gpsimd.indirect_dma_start(
                                    adj_d, bass.IndirectOffsetOnAxis(ap=slot[:, b, k:k + 1], axis=0),
                                    count[:, b, k:k + 1], None, compute_op=ALU.add).then_inc(landed[b if short else 0], 16)

                    turn(0, True)
                    with pool.Fori(1, G // 2) as i:
                        turn(i, False)
                    for half in range(2 if short else 1):
                        pool.wait_ge(landed[half], 16 * GT * (GH if short else G))

        either(build)
    if dbg and dbg["stop"] == "build":
        return finish_debug(nc, top, sem, dbg, {"adj": adj_rows[:, 0:NP]})


    end_phase()
    with ExitStack() as c:
        def sb(name, shape, dt):
            return c.enter_context(nc.sbuf_tensor(name, shape, dt))
        R_IN = 3
        blk = sb("blk", [P, R_IN, NB, BW], BF16)
        blkT = sb("blkT", [P, R_IN, NB, BW], BF16)
        in_part = sb("in_part", [P, NT, NBLK], F32)
        out_part = sb("out_part", [P, NT, NBLK], F32)
        psT = [c.enter_context(nc.psum_tensor(f"psT{j}", [P, BW], BF16)) for j in range(NB)]
        loaded = [sem(f"t_load{q}") for q in range(R_IN)]
        stored = [sem(f"t_store{q}") for q in range(R_IN)]
        turned, moved, summed, degs = sem("t_turned"), sem("t_moved"), sem("t_summed"), sem("t_degs")
        uses = [len(range(q, NBLK, R_IN)) for q in range(R_IN)]

        def before(C, i):
            return i * NBLK + C - R_IN + 1 if C >= R_IN else i * NBLK - NBLK + max(range(C % R_IN, NBLK, R_IN)) + 1

        with nc.Block() as block:
            @block.sync
            def _(sp):
                def turn(i, first):
                    for C in range(NBLK):
                        if not (first and C < R_IN):
                            sp.wait_ge(turned, before(C, i) * NB)
                            sp.wait_ge(summed, before(C, i))
                        sp.dma_start(blk[:, C % R_IN], adj_rows[bass.ds(i * BW, BW), C * BW:(C + 1) * BW]
                                     .rearrange("(t p) s -> p t s", p=P)).then_inc(loaded[C % R_IN], 16)
                turn(0, True)
                with sp.Fori(1, NBLK) as i:
                    turn(i, False)

            @block.tensor
            def _(pe):
                def turn(i, first):
                    for C in range(NBLK):
                        pe.wait_ge(loaded[C % R_IN], i * (16 * uses[C % R_IN]) + 16 * (C // R_IN + 1))
                        for j in range(NB):
                            if not (first and C == 0):
                                pe.wait_ge(moved, i * (NBLK * NB) + ((C - 1) * NB + j + 1))
                            for t in range(NB):
                                mm = nc.tensor.transpose(psT[j][:, t * P:(t + 1) * P],
                                                         blk[:, C % R_IN, t, j * P:(j + 1) * P], identb[:])
                            mm.then_inc(turned, 1)
                turn(0, True)
                with pe.Fori(1, NBLK) as i:
                    turn(i, False)

            @block.scalar
            def _(act):
                def turn(i, first):
                    for C in range(NBLK):
                        if not (first and C < R_IN):
                            prev = (C - R_IN) // R_IN + 1 if C >= R_IN else 0
                            act.wait_ge(stored[C % R_IN], i * (16 * uses[C % R_IN]) + 16 * prev)
                        for j in range(NB):
                            act.wait_ge(turned, i * (NBLK * NB) + (C * NB + j + 1))
                            nc.scalar.activation(blkT[:, C % R_IN, j, :], psT[j][:], ACT.Copy,
                                                 accum_out=out_part[:, C * NB + j, bass.ds(i, 1)]).then_inc(moved, 1)
                        act.wait_ge(moved, i * (NBLK * NB) + ((C + 1) * NB))
                        act.dma_start(adjT_d[C * BW:(C + 1) * BW, bass.ds(i * BW, BW)].rearrange("(t p) s -> p t s", p=P),
                                      blkT[:, C % R_IN]).then_inc(stored[C % R_IN], 16)
                turn(0, True)
                with act.Fori(1, NBLK) as i:
                    turn(i, False)
                for q in range(R_IN):
                    act.wait_ge(stored[q], 16 * uses[q] * NBLK)

            @block.vector
            def _(dve):
                with dve.Fori(0, NBLK) as i:
                    for C in range(NBLK):
                        dve.wait_ge(loaded[C % R_IN], i * (16 * uses[C % R_IN]) + 16 * (C // R_IN + 1))
                        nc.vector.tensor_reduce(in_part[:, bass.ds(i * NB, NB), C], blk[:, C % R_IN], AX_X,
                                                ALU.add).then_inc(summed, 1)
                dve.wait_ge(summed, NBLK * NBLK)
                dve.wait_ge(moved, NBLK * NBLK * NB)
                nc.vector.tensor_reduce(deg_in[:], in_part[:], AX_X, ALU.add).then_inc(degs, 1)
                nc.vector.tensor_reduce(deg_out[:], out_part[:], AX_X, ALU.add).then_inc(degs, 1)

    end_phase()
    with ExitStack() as c:
        def sb(name, shape, dt):
            return c.enter_context(nc.sbuf_tensor(name, shape, dt))
        upto = sb("upto", [P, P], F32)
        ones = sb("ones", [P, P], F32)
        tot = sb("tot", [P, NT], F32)
        cum_t = sb("cum_t", [P, NT], F32)
        cum = sb("cum", [P, NT], F32)
        first = sb("first", [P, NT], F32)
        ei = sb("ei", [P, 2, NT], I32)
        ew = sb("ew", [P, 3, 2, NT], I32)
        cl = sb("cl", [P, 2, NT], F32)
        rt = sb("rt", [P, 2, NT], F32)
        no_edge = sb("no_edge", [P, NT], I32)
        spare = sb("spare", [P, NT], I32)
        low = sb("low", [P, NT], F32)
        base = sb("base", [P, 2, NT], F32)
        base_i = sb("base_i", [P, 2, NT], I32)
        tile_k = sb("tile_k", [P, 2, NT], I32)
        ps_in = c.enter_context(nc.psum_tensor("ps_in", [P, NT], F32))
        ps_tot = c.enter_context(nc.psum_tensor("ps_tot", [P, NT], F32))
        vs, pl, mm_s, rooted = sem("n_dve"), sem("n_pool"), sem("n_pe"), sem("n_root")
        with nc.Block() as block:
            @block.gpsimd
            def _(pool):
                nc.gpsimd.memset(upto[:], 1.0).then_inc(pl, 1)
                nc.gpsimd.iota(spare[:], pattern=[[P, NT]], base=EP, channel_multiplier=1).then_inc(pl, 1)
                pool.wait_ge(pl, 2)
                nc.gpsimd.affine_select(out=upto[:], in_=upto[:], compare_op=ALU.is_ge, fill=0.0, base=0,
                                        pattern=[[1, P]], channel_multiplier=-1).then_inc(pl, 1)

            @block.tensor
            def _(pe):
                pe.wait_ge(pl, 3)
                pe.wait_ge(vs, 1)
                nc.tensor.matmul(ps_in[:], upto[:], deg_in[:], start=True, stop=True)
                nc.tensor.matmul(ps_tot[:], ones[:], deg_in[:], start=True, stop=True).then_inc(mm_s, 1)

            @block.scalar
            def _(act):
                act.wait_ge(vs, 3)
                nc.scalar.sqrt(rt[:], cl[:]).then_inc(rooted, 1)

            @block.vector
            def _(dve):
                s = Steps(dve, vs)
                s.did(nc.vector.memset(ones[:], 1.0))
                s.did(nc.vector.tensor_scalar_max(cl[:, 0, :], deg_in[:], 1.0))
                s.did(nc.vector.tensor_scalar_max(cl[:, 1, :], deg_out[:], 1.0))
                dve.wait_ge(rooted, 1)
                s.did(nc.vector.reciprocal(norm_in[:], rt[:, 0, :]))
                s.did(nc.vector.reciprocal(norm_out[:], rt[:, 1, :]))
                s.did(nc.vector.reciprocal(half_in[:], cl[:, 0, :]))
                s.link(nc.vector.reciprocal(half_out[:], cl[:, 1, :]))
                s.did(nc.vector.tensor_scalar_mul(half_in[:], half_in[:], 0.5))
                s.did(nc.vector.tensor_scalar_mul(half_out[:], half_out[:], 0.5))
                dve.wait_ge(mm_s, 1)
                s.link(nc.vector.tensor_copy(tot[:], ps_tot[:]))
                s.link(nc.vector.tensor_tensor_scan(cum_t[:], ones[:, 0:NT], tot[:], 0.0, ALU.mult, ALU.add))
                s.link(nc.vector.tensor_sub(cum_t[:], cum_t[:], tot[:]))
                s.link(nc.vector.tensor_add(cum[:], cum_t[:], ps_in[:]))
                s.link(nc.vector.tensor_sub(first[:], cum[:], deg_in[:]))
                s.did(nc.vector.tensor_copy(ei[:, 1, :], first[:]))
                s.link(nc.vector.tensor_scalar(cum[:], cum[:], -1.0, 0.0, ALU.add, ALU.max))
                s.link(nc.vector.tensor_copy(ei[:, 0, :], cum[:]))
                s.did(nc.vector.tensor_scalar(ew[:, 0], ei[:], -GE, None, ALU.bitwise_and))
                s.did(nc.vector.tensor_scalar(ew[:, 1], ei[:], P - 1, 3, ALU.bitwise_and, ALU.logical_shift_left))
                s.link(nc.vector.tensor_scalar(ew[:, 2], ei[:], 7, GT - 1, ALU.logical_shift_right, ALU.bitwise_and))
                s.link(nc.vector.tensor_tensor(ew[:, 0], ew[:, 0], ew[:, 1], ALU.bitwise_or))
                s.did(nc.vector.tensor_tensor(end_row[:], ew[:, 0, 0], ew[:, 2, 0], ALU.bitwise_or))
                s.did(nc.vector.tensor_tensor(start_row[:], ew[:, 0, 1], ew[:, 2, 1], ALU.bitwise_or))
                s.link(nc.vector.tensor_scalar(no_edge[:], deg_in[:], 0.0, None, ALU.is_equal))
                s.did(nc.vector.copy_predicated(start_row[:], no_edge[:], spare[:]))
                s.link(nc.vector.tensor_scalar(ei[:, 1, :], ei[:, 0, :], P - 1, None, ALU.bitwise_and))
                s.link(nc.vector.tensor_scalar(low[:], ei[:, 1, :], float(P - 1), None, ALU.not_equal))
                s.link(nc.vector.tensor_scalar(alive[:], deg_in[:], 0.0, None, ALU.is_gt))
                s.link(nc.vector.tensor_mul(own_end[:], low[:], alive[:]))
                s.link(nc.vector.tensor_scalar(base_i[:, 0, :], ei[:, 0, :], -P, None, ALU.bitwise_and))
                s.link(nc.vector.tensor_copy(base[:, 0, :], base_i[:, 0, :]))
                s.link(nc.vector.tensor_scalar(base[:, 1, :], base[:, 0, :], -float(P), None, ALU.add))
                for before in range(SHORT // P):
                    s.link(nc.vector.tensor_tensor(carried[:, before, :], base[:, before, :], first[:], ALU.is_gt))
                    s.link(nc.vector.tensor_mul(carried[:, before, :], carried[:, before, :], alive[:]))
                s.link(nc.vector.tensor_scalar(base[:], base[:], -1.0, 0.0, ALU.add, ALU.max))
                s.link(nc.vector.tensor_copy(base_i[:], base[:]))
                s.link(nc.vector.tensor_scalar(tile_k[:], base_i[:], 7, GT - 1, ALU.logical_shift_right, ALU.bitwise_and))
                s.link(nc.vector.tensor_scalar(carry_row[:], base_i[:], -GE, (P - 1) * GT, ALU.bitwise_and, ALU.bitwise_or))
                s.link(nc.vector.tensor_tensor(carry_row[:], carry_row[:], tile_k[:], ALU.bitwise_or))
    if dbg and dbg["stop"] == "deg":
        return finish_debug(nc, top, sem, dbg, {"adjT": adjT_d, "deg_in": deg_in[:], "deg_out": deg_out[:], "norm_in": norm_in[:],
            "end_row": end_row[:], "start_row": start_row[:], "own_end": own_end[:], "first_id": first_id[0:98], "last_id": last_id[0:98]})


    end_phase()
    def each(row):
        return row.unsqueeze(2).to_broadcast([P, NT, D])

    def along(vector):
        return vector.unsqueeze(1).to_broadcast([P, NT, D])

    def row_of(name, width=D):
        return a[name].rearrange("(a n) -> a n", a=1).to_broadcast([P, width])

    def split(s):
        for part in range(3):
            src = h_sb if part == 0 else t_sb
            s.link(nc.vector.tensor_copy(h3[:, :, part * D:(part + 1) * D], src[:]))
            if part < 2:
                s.link(nc.vector.tensor_sub(t_sb[:], src[:], h3[:, :, part * D:(part + 1) * D]))

    def norm_phase(tag, scale, with_split):
        with ExitStack() as c:
            mean = c.enter_context(nc.sbuf_tensor(f"mean{tag}", [P, NT], F32))
            var = c.enter_context(nc.sbuf_tensor(f"var{tag}", [P, NT], F32))
            std = c.enter_context(nc.sbuf_tensor(f"std{tag}", [P, NT], F32))
            rstd = c.enter_context(nc.sbuf_tensor(f"rstd{tag}", [P, NT], F32))
            vs, rooted = sem(f"ln_dve{tag}"), sem(f"ln_root{tag}")
            with nc.Block() as block:
                @block.scalar
                def _(act):
                    act.wait_ge(vs, 6)
                    nc.scalar.sqrt(std[:], var[:]).then_inc(rooted, 1)

                @block.vector
                def _(dve):
                    s = Steps(dve, vs)
                    s.link(nc.vector.tensor_reduce(mean[:], x_sb[:], AX_X, ALU.add))
                    s.link(nc.vector.tensor_scalar_mul(mean[:], mean[:], 1.0 / D))
                    s.link(nc.vector.tensor_sub(h_sb[:], x_sb[:], each(mean[:])))
                    s.link(nc.vector.tensor_mul(t_sb[:], h_sb[:], h_sb[:]))
                    s.link(nc.vector.tensor_reduce(var[:], t_sb[:], AX_X, ALU.add))
                    s.link(nc.vector.tensor_scalar(var[:], var[:], 1.0 / D, EPS, ALU.mult, ALU.add))
                    dve.wait_ge(rooted, 1)
                    s.link(nc.vector.reciprocal(rstd[:], std[:]))
                    if scale is not None:
                        s.link(nc.vector.tensor_mul(rstd[:], rstd[:], scale[:]))
                    s.link(nc.vector.tensor_scalar_max(h_sb[:], h_sb[:], 0.0))
                    s.link(nc.vector.tensor_mul(h_sb[:], h_sb[:], each(rstd[:])))
                    if with_split:
                        split(s)
        end_phase()

    sw_load = [sem(f"s_load{q}", keep=True) for q in range(4)]
    sw_used, sw_high, sw_low, sw_made, sw_taken, sw_w, sw_chain = (
        sem(n, keep=True) for n in ("s_used", "s_high", "s_low", "s_made", "s_taken", "s_weights", "s_chain"))
    sweeps = [0]

    def sweep(matrix, weight, scale, accumulate):
        n = sweeps[0]
        sweeps[0] += 1
        RING = 4
        uses = [len(range(q, NBLK, RING)) for q in range(RING)]
        tb = n * NBLK
        with ExitStack() as c:
            ring = c.enter_context(nc.sbuf_tensor(f"ring{n}", [P, RING, NB, BW], BF16))
            high = c.enter_context(nc.sbuf_tensor(f"high{n}", [P, BW], F32))
            low = c.enter_context(nc.sbuf_tensor(f"low{n}", [P, SPLIT[0]], F32))
            w2 = c.enter_context(nc.sbuf_tensor(f"w2_{n}", [P, D], F32))
            tmp = c.enter_context(nc.sbuf_tensor(f"swt{n}", [P, NB, D], F32))
            ps_h = c.enter_context(nc.psum_tensor(f"ps_h{n}", [P, 2, 512], F32))
            ps_l = c.enter_context(nc.psum_tensor(f"ps_l{n}", [P, 512], F32))
            ps_y = c.enter_context(nc.psum_tensor(f"ps_y{n}", [P, 2, 512], F32))

            def before(kb, i):
                held = kb - RING if kb >= RING else max(range(kb % RING, NBLK, RING)) - NBLK
                return i * NBLK + (tb * NBLK + held + 1)

            with nc.Block() as block:
                @block.sync
                def _(sp):
                    sp.dma_start(w2[0:D, :], a[weight]).then_inc(sw_w, 16)
                    sp.dma_start(w2[D:P, :], a[weight]).then_inc(sw_w, 16)

                    def turn(i, first):
                        for kb in range(NBLK):
                            if not (first and kb < RING):
                                sp.wait_ge(sw_used, before(kb, i))
                            sp.dma_start(ring[:, kb % RING], matrix[kb * BW:(kb + 1) * BW, bass.ds(i * BW, BW)]
                                         .rearrange("(t p) s -> p t s", p=P)).then_inc(sw_load[kb % RING], 16)
                    turn(0, True)
                    with sp.Fori(1, NBLK) as i:
                        turn(i, False)

                @block.tensor
                def _(pe):
                    pe.wait_ge(sw_w, 32 * (n + 1))
                    with pe.Fori(0, NBLK) as i:
                        pe.wait_ge(sw_high, i + (tb + 1))
                        pe.wait_ge(sw_low, i + (tb + 1))
                        for kb in range(NBLK):
                            q = kb % RING
                            pe.wait_ge(sw_load[q], i * (16 * uses[q]) + 16 * (tb * uses[q] + kb // RING + 1))
                            for t in range(NB):
                                k = kb * NB + t
                                moving = [ring[:, q, t, h * SPLIT[0]:h * SPLIT[0] + SPLIT[h]] for h in range(2)]
                                for h in range(2):
                                    nc.tensor.matmul(ps_h[:, h, 0:SPLIT[h]], h3[:, k, 0:P], moving[h], start=k == 0, stop=k == NT - 1)
                                for h in range(2):
                                    mm = nc.tensor.matmul(ps_l[h * D:(h + 1) * D, 0:SPLIT[h]], h3[:, k, P:P + D], moving[h],
                                                          start=k == 0, stop=k == NT - 1)
                            mm.then_inc(sw_used, 1)
                        pe.wait_ge(sw_high, i + (tb + 2))
                        pe.wait_ge(sw_low, i + (tb + 2))
                        pe.wait_ge(sw_taken, i + (tb + 1))
                        for j in range(NB):
                            h, col = j // 4, (j % 4) * P
                            y = ps_y[:, h, (j % 4) * D:(j % 4 + 1) * D]
                            nc.tensor.matmul(y, high[:, j * P:(j + 1) * P], w2[:], start=True, stop=False)
                            mm = nc.tensor.matmul(y, low[h * D:(h + 1) * D, col:col + P], w2[h * D:(h + 1) * D, :],
                                                  start=False, stop=True)
                        mm.then_inc(sw_made, 1)

                @block.scalar
                def _(act):
                    if n == 0:
                        act.sem_inc(sw_low, 1)
                    with act.Fori(0, NBLK) as i:
                        act.wait_ge(sw_used, i * NBLK + (tb * NBLK + NBLK))
                        nc.scalar.copy(low[0:D, :], ps_l[0:D, :])
                        nc.scalar.copy(low[D:P, 0:SPLIT[1]], ps_l[D:P, 0:SPLIT[1]]).then_inc(sw_low, 1)

                @block.vector
                def _(dve):
                    if n == 0:
                        dve.sem_inc(sw_high, 1)
                        dve.sem_inc(sw_taken, 1)
                    with dve.Fori(0, NBLK) as i:
                        dve.wait_ge(sw_used, i * NBLK + (tb * NBLK + NBLK))
                        nc.vector.tensor_copy(high[:, 0:SPLIT[0]], ps_h[:, 0, :])
                        nc.vector.tensor_copy(high[:, SPLIT[0]:BW], ps_h[:, 1, 0:SPLIT[1]]).then_inc(sw_high, 1)
                        dve.wait_ge(sw_made, i + (tb + 1))
                        for h in range(2):
                            tiles = SPLIT[h] // P
                            nodes = bass.ds(i * NB + 4 * h, tiles)
                            sc = scale[:, nodes].unsqueeze(2).to_broadcast([P, tiles, D])
                            y = ps_y[:, h, 0:tiles * D].rearrange("p (t d) -> p t d", d=D)
                            into = tmp[:, 4 * h:4 * h + tiles, :] if accumulate else y_sb[:, nodes, :]
                            ins = nc.vector.tensor_mul(into, y, sc)
                        ins.then_inc(sw_taken, 1)
                        if accumulate:
                            dve.wait_ge(sw_taken, i + (tb + 2))
                            nodes = bass.ds(i * NB, NB)
                            nc.vector.tensor_add(y_sb[:, nodes, :], y_sb[:, nodes, :], tmp[:]).then_inc(sw_chain, 1)

    def bias_phase(tag, biases, factors, work):
        with ExitStack() as c:
            rows = c.enter_context(nc.sbuf_tensor(f"rows{tag}", [P, len(biases), D], F32))
            ld, vs = sem(f"bias_load{tag}"), sem(f"bias_dve{tag}")
            with nc.Block() as block:
                @block.sync
                def _(sp):
                    for r, name in enumerate(biases):
                        sp.dma_start(rows[:, r, :], row_of(name)).then_inc(ld, 16)

                @block.vector
                def _(dve):
                    dve.wait_ge(ld, 16 * len(biases))
                    work(Steps(dve, vs), rows)
        end_phase()

    norm_phase("0", norm_out, True)
    sweep(adjT_d, "L0_gnn_W1", norm_in, False)

    def between(s, rows):
        s.link(nc.vector.tensor_add(h_sb[:], y_sb[:], along(rows[:, 0, :])))
        s.link(nc.vector.tensor_scalar_max(h_sb[:], h_sb[:], 0.0))
        s.link(nc.vector.tensor_mul(h_sb[:], h_sb[:], each(norm_out[:])))
        split(s)
    bias_phase("0a", ["L0_gnn_b1"], None, between)
    sweep(adjT_d, "L0_gnn_W2", norm_in, False)

    def close0(s, rows):
        s.link(nc.vector.tensor_add(x_sb[:], x_sb[:], y_sb[:]))
        s.link(nc.vector.tensor_add(x_sb[:], x_sb[:], along(rows[:, 0, :])))
    bias_phase("0b", ["L0_gnn_b2"], None, close0)
    if dbg and dbg["stop"] == "L0":
        return finish_debug(nc, top, sem, dbg, {"x": x_sb[:]})


    def node_product(tag, width, fill, local=(), stores=(), hidden=False, prepare=None, extra_bias=None, factor=None):
        per_bank = min(NB, 512 // width)
        banks = -(-NB // per_bank)
        with ExitStack() as c:
            def sb(name, shape, dt=F32):
                return c.enter_context(nc.sbuf_tensor(name + tag, shape, dt))
            wid = P if hidden else width
            wcat = sb("wcat", [D + 1, wid])
            hst = sb("hst", [P, NB, D])
            hT = sb("hT", [D + 1, BW])
            stage = sb("stage", [P, NB, width])
            ps_x = c.enter_context(nc.psum_tensor("ps_x" + tag, [D, 2, 512], F32))
            ps_m = c.enter_context(nc.psum_tensor("ps_m" + tag, [P, banks, 512], F32))
            if hidden:
                w2n = sb("w2n", [P, D])
                b2n = sb("b2n", [P, D])
                dps = sb("dps", [P, 1])
                hid = sb("hid", [P, 2, 512])
                act_h = sb("act_h", [P, BW])
                ps_hid = c.enter_context(nc.psum_tensor("ps_hid" + tag, [P, 2, 512], F32))
            copied, turned, moved, made, taken, stored, wl = (
                sem(f"{n}{tag}") for n in ("np_copied", "np_turned", "np_moved", "np_made", "np_taken", "np_stored", "np_w"))
            hid_made, hid_out, hid_act, prep, chain = (
                sem(f"{n}{tag}") for n in ("np_hid", "np_hidout", "np_hidact", "np_prep", "np_chain"))
            extra = prepare(c) if prepare else None
            loads = [0]
            with nc.Block() as block:
                @block.sync
                def _(sp):
                    loads[0] = 16 * fill(sp, wcat, wl, extra)
                    if hidden:
                        sp.dma_start(w2n[:], a["L3_gnn_W2n"]).then_inc(wl, 16)
                        sp.dma_start(b2n[:], row_of("L3_gnn_b2n")).then_inc(wl, 16)
                        sp.dma_start(dps[:], row_of("L3_gnn_dp_scale", 1)).then_inc(wl, 16)
                        loads[0] += 48

                    def turn(i):
                        sp.wait_ge(taken, i + 1)
                        for cols, rows in stores:
                            sp.dma_start(rows[bass.ds(i * BW, BW), :].rearrange("(t p) d -> p t d", p=P),
                                         stage[:, :, cols]).then_inc(stored, 16)
                    if stores:
                        with sp.Fori(0, NBLK) as i:
                            turn(i)
                        sp.wait_ge(stored, 16 * len(stores) * NBLK)

                @block.tensor
                def _(pe):
                    pe.wait_ge(wl, loads[0])
                    if extra is not None:
                        extra["pe"](pe, prep)

                    def turn(i, first):
                        pe.wait_ge(copied, i + 1)
                        pe.nop(nofuse=True)
                        for j in range(NB):
                            tr = nc.tensor.transpose(ps_x[:, j // 4, (j % 4) * P:(j % 4 + 1) * P], hst[:, j, :], ident[:])
                        tr.then_inc(turned, 1)
                        pe.wait_ge(moved, i * 2 + 2)
                        pe.wait_ge(prep, 2)
                        if hidden:
                            for half in range(2):
                                mm = nc.tensor.matmul(ps_hid[:, half, 0:SPLIT[half]], wcat[:],
                                                      hT[:, half * 512:half * 512 + SPLIT[half]], start=True, stop=True)
                            mm.then_inc(hid_made, 1)
                            pe.wait_ge(hid_act, i * 2 + 2)
                        if not first:
                            pe.wait_ge(taken, i)
                        for j in range(NB):
                            dst = ps_m[:, j // per_bank, (j % per_bank) * width:(j % per_bank + 1) * width]
                            if hidden:
                                lhs, rhs = act_h[:, j * P:(j + 1) * P], w2n[:]
                            else:
                                lhs, rhs = hT[:, j * P:(j + 1) * P], wcat[:]
                            mm = nc.tensor.matmul(dst, lhs, rhs, start=True, stop=True)
                        mm.then_inc(made, 1)
                    turn(0, True)
                    with pe.Fori(1, NBLK) as i:
                        turn(i, False)

                @block.scalar
                def _(act):
                    def turn(i, first):
                        act.wait_ge(turned, i + 1)
                        if not first:
                            act.wait_ge(made, i)
                        nc.scalar.copy(hT[0:D, 0:512], ps_x[:, 0, :]).then_inc(moved, 1)
                        nc.scalar.copy(hT[0:D, 512:BW], ps_x[:, 1, 0:BW - 512]).then_inc(moved, 1)
                        if hidden:
                            act.wait_ge(hid_made, i + 1)
                            for half in range(2):
                                nc.scalar.activation(hid[:, half, 0:SPLIT[half]], ps_hid[:, half, 0:SPLIT[half]], ACT.Copy,
                                                     scale=0.1).then_inc(hid_out, 1)
                    turn(0, True)
                    with act.Fori(1, NBLK) as i:
                        turn(i, False)

                @block.vector
                def _(dve):
                    nc.vector.memset(hT[D:D + 1, :], 1.0).then_inc(prep, 1)
                    if extra is not None:
                        extra["dve"](dve, prep, wl, loads[0])
                    else:
                        dve.sem_inc(prep, 1)
                    dve.wait_ge(wl, loads[0])

                    def turn(i, first):
                        nodes = bass.ds(i * NB, NB)
                        if not first:
                            dve.wait_ge(turned, i)
                        nc.vector.tensor_copy(hst[:], h_sb[:, nodes, :]).then_inc(copied, 1)
                        if hidden:
                            dve.wait_ge(hid_out, i * 2 + 2)
                            for half in range(2):
                                nc.vector.tensor_tensor(act_h[:, half * 512:half * 512 + SPLIT[half]],
                                                        ps_hid[:, half, 0:SPLIT[half]], hid[:, half, 0:SPLIT[half]],
                                                        ALU.max).then_inc(hid_act, 1)
                        dve.wait_ge(made, i + 1)
                        if stores and not first:
                            dve.wait_ge(stored, i * (16 * len(stores)))
                        ct = Steps(dve, chain, turn=i, per=banks + (2 if hidden else 0))
                        for b in range(banks):
                            w = min(per_bank, NB - b * per_bank)
                            ct.did(nc.vector.tensor_copy(
                                stage[:, b * per_bank:b * per_bank + w, :],
                                ps_m[:, b, 0:w * width].rearrange("p (j f) -> p j f", j=w)))
                        ct.wait()
                        if hidden:
                            ct.link(nc.vector.tensor_add(stage[:], stage[:], b2n[:].unsqueeze(1).to_broadcast([P, NB, D])))
                            ct.link(nc.vector.tensor_scalar(stage[:], stage[:], dps[:, 0:1], None, ALU.mult))
                        for cols, keep_in in local:
                            nc.vector.tensor_copy(keep_in[:, nodes, :], stage[:, :, cols]).then_inc(sw_chain, 1)
                        dve.nop(nofuse=True)
                        dve.sem_inc(taken, 1)
                    turn(0, True)
                    with dve.Fori(1, NBLK) as i:
                        turn(i, False)
        end_phase()

    def dst_rows(g):
        return dstf_d[1:EP + 1].rearrange("(a n) -> a n", a=1)[:, bass.ds(g * GE, GE)].to_broadcast([P, GE])

    def part_rows(table, g):
        return table[bass.ds(g * GE, GE), :].rearrange("(p k) d -> p (k d)", p=P)

    def collect(tag, finish):
        def both(short):
            (collect_short if short else collect_long)(tag + ("s" if short else "l"), finish)
        either(both)
        end_phase()

    def collect_short(tag, finish):
        with ExitStack() as c:
            rows = [c.enter_context(nc.sbuf_tensor(f"carry{n}{tag}", [P, NT, D], F32)) for n in range(SHORT // P)]
            got, vs = sem(f"c_got{tag}", keep=True), sem(f"c_dve{tag}")
            with nc.Block() as block:
                @block.gpsimd
                def _(pool):
                    for t in range(NT):
                        for into, row in [(y_sb, end_row[:, t:t + 1])] + [
                                (rows[n], carry_row[:, n, t:t + 1]) for n in range(SHORT // P)]:
                            nc.gpsimd.indirect_dma_start(into[:, t, :], None, part_d,
                                                         bass.IndirectOffsetOnAxis(ap=row, axis=0)).then_inc(got, 16)

                @block.vector
                def _(dve):
                    s = Steps(dve, vs)
                    dve.wait_ge(got, 16 * NT * (1 + SHORT // P))
                    s.link(nc.vector.tensor_mul(y_sb[:], y_sb[:], each(alive[:])))
                    for n in range(SHORT // P):
                        s.link(nc.vector.tensor_mul(rows[n][:], rows[n][:], each(carried[:, n, :])))
                        s.link(nc.vector.tensor_add(y_sb[:], y_sb[:], rows[n][:]))
                    finish(s)

                for idle in (block.tensor, block.scalar, block.sync):
                    idle(lambda eng: eng.nop(nofuse=True))

    def collect_long(tag, finish):
        with ExitStack() as c:
            def sb(name, shape, dt=F32):
                return c.enter_context(nc.sbuf_tensor(name + tag, shape, dt))
            last_row = sb("last_row", [P, 2, GT * D])
            iota_i = sb("iota_i", [P, P], I32)
            iota_f = sb("iota_f", [P, P])
            shifted = sb("shifted", [P, NT, 2 * GT])
            node0 = sb("node0", [P, NT])
            node0_i = sb("node0_i", [P, NT], I32)
            hot = sb("hot", [P, 2, 2 * GT, P])
            ps_c = c.enter_context(nc.psum_tensor("ps_c" + tag, [P, 2, 512], F32))
            got = sem(f"c_got{tag}", keep=True)
            ld, pl, hots, picked, taken, vs, chain = (
                sem(f"{n}{tag}") for n in ("c_load", "c_iota", "c_hot", "c_picked", "c_taken", "c_dve", "c_chain"))
            with nc.Block() as block:
                @block.sync
                def _(sp):
                    view = part_d.rearrange("(h g p k) d -> h g p (k d)", h=2, p=P, k=GT)
                    for h in range(2):
                        sp.dma_start(last_row[0:GH, h, :], view[h, :, P - 1, :]).then_inc(ld, 16)

                @block.gpsimd
                def _(pool):
                    nc.gpsimd.iota(iota_i[:], pattern=[[1, P]], base=0, channel_multiplier=0).then_inc(pl, 1)
                    nc.gpsimd.iota(node0_i[:], pattern=[[P, NT]], base=0, channel_multiplier=0).then_inc(pl, 1)
                    for t in range(NT):
                        nc.gpsimd.indirect_dma_start(y_sb[:, t, :], None, part_d,
                                                     bass.IndirectOffsetOnAxis(ap=end_row[:, t:t + 1], axis=0)).then_inc(got, 16)

                @block.scalar
                def _(act):
                    act.nop(nofuse=True)

                @block.tensor
                def _(pe):
                    pe.wait_ge(ld, 32)

                    def node_tile(t2, i, first):
                        pe.wait_ge(hots, i + 1)
                        if not first:
                            pe.wait_ge(taken, i - 1)
                        for q in range(2 * GT):
                            mm = nc.tensor.matmul(ps_c[:, t2, 0:D], hot[0:GH, t2, q, :],
                                                  last_row[0:GH, q // GT, (q % GT) * D:(q % GT + 1) * D],
                                                  start=q == 0, stop=q == 2 * GT - 1)
                        mm.then_inc(picked, 1)
                    for t2 in range(2):
                        node_tile(t2, t2, True)
                    with pe.Fori(2, NT - 1, 2) as i:
                        for t2 in range(2):
                            node_tile(t2, i + t2, False)
                    node_tile(0, NT - 1, False)

                @block.vector
                def _(dve):
                    s = Steps(dve, vs)
                    dve.wait_ge(pl, 2)
                    s.did(nc.vector.tensor_copy(iota_f[:], iota_i[:]))
                    s.link(nc.vector.tensor_copy(node0[:], node0_i[:]))
                    s.link(nc.vector.tensor_sub(
                        shifted[0:GH], last_id[0:GH].rearrange("p h k -> p (h k)").unsqueeze(1).to_broadcast([GH, NT, 2 * GT]),
                        node0[0:GH, :].unsqueeze(2).to_broadcast([GH, NT, 2 * GT])))
                    dve.wait_ge(got, 16 * NT)
                    s.link(nc.vector.tensor_mul(y_sb[:], y_sb[:], each(own_end[:])))

                    def node_tile(t2, i, first):
                        if not first:
                            dve.wait_ge(picked, i - 1)
                        one = iota_f[0:GH, :].unsqueeze(1).to_broadcast([GH, 2 * GT, P])
                        at = shifted[0:GH, bass.ds(i, 1), :].rearrange("p a q -> p (a q)").unsqueeze(2) \
                            .to_broadcast([GH, 2 * GT, P])
                        nc.vector.tensor_tensor(hot[0:GH, t2], one, at, ALU.is_equal).then_inc(hots, 1)

                    def take(t2, i):
                        dve.wait_ge(picked, i + 1)
                        node = y_sb[:, bass.ds(i, 1), :].rearrange("p a d -> p (a d)")
                        nc.vector.tensor_add(node, node, ps_c[:, t2, 0:D]).then_inc(taken, 1)
                    for t2 in range(2):
                        node_tile(t2, t2, True)
                    with dve.Fori(2, NT - 1, 2) as i:
                        for t2 in range(2):
                            take(t2, i + (t2 - 2))
                            node_tile(t2, i + t2, False)
                    take(0, NT - 3)
                    node_tile(0, NT - 1, False)
                    take(1, NT - 2)
                    take(0, NT - 1)
                    dve.wait_ge(taken, NT)
                    finish(s)

    norm_phase("1", None, False)

    def l1_prepare(c):
        weT = c.enter_context(nc.sbuf_tensor("weT", [D, D + 1], F32))
        ws = c.enter_context(nc.sbuf_tensor("ws", [D, D], F32))
        wsb = c.enter_context(nc.sbuf_tensor("wsb", [D + 1, D], F32))
        ps_w = c.enter_context(nc.psum_tensor("ps_w", [D + 1, D], F32))
        fused = sem("l1_fused")

        def pe(eng, prep):
            nc.tensor.matmul(ps_w[:], weT[:], ws[:], start=True, stop=True).then_inc(fused, 1)

        def dve(eng, prep, wl, loads):
            eng.wait_ge(wl, loads)
            eng.wait_ge(fused, 1)
            nc.vector.tensor_copy(both["wcat"][:, 0:D], ps_w[:]).then_inc(fused, 1)
            eng.wait_ge(fused, 2)
            nc.vector.tensor_add(both["wcat"][D:D + 1, 0:D], both["wcat"][D:D + 1, 0:D], wsb[D:D + 1, :]).then_inc(prep, 1)
        both = {"pe": pe, "dve": dve, "weT": weT, "ws": ws, "wsb": wsb}
        return both

    def l1_fill(sp, wcat, wl, extra):
        extra["wcat"] = wcat
        for dst, src in ((wcat[0:D, D:2 * D], a["L1_gnn_We_k"].rearrange("f h d -> f (h d)")),
                         (wcat[D:D + 1, D:2 * D], a["L1_gnn_We_b"]),
                         (wcat[0:D, 2 * D:3 * D], a["L1_gnn_Wr_k"].rearrange("f h d -> f (h d)")),
                         (wcat[D:D + 1, 2 * D:3 * D], a["L1_gnn_Wr_b"]),
                         (extra["weT"][:], a["L1_We_T"]),
                         (extra["ws"][:], a["L1_gnn_Ws_k"]),
                         (extra["wsb"][D:D + 1, :], a["L1_gnn_Ws_b"].rearrange("(a n) -> a n", a=1))):
            sp.dma_start(dst, src).then_inc(wl, 16)
        return 7
    node_product("n1", 3 * D, l1_fill, local=[(slice(2 * D, 3 * D), y_sb)],
                 stores=[(slice(0, 2 * D), send_d), (slice(2 * D, 3 * D), recv_d)], prepare=l1_prepare)

    with ExitStack() as c:
        tile_first = c.enter_context(nc.sbuf_tensor("tile_first", [P, 2, GT, D], F32))
        put, got, wrote = sem("z_put", keep=True), sem("z_got", keep=True), sem("z_wrote")
        with nc.Block() as block:
            @block.gpsimd
            def _(pool):
                for h in range(2):
                    for k in range(GT):
                        nc.gpsimd.indirect_dma_start(
                            tile_first[0:GH, h, k, :], None, recv_d,
                            bass.IndirectOffsetOnAxis(ap=first_id[0:GH, h, k:k + 1], axis=0)).then_inc(got, 16)
                for t in range(NT):
                    nc.gpsimd.indirect_dma_start(recvz_d, bass.IndirectOffsetOnAxis(ap=start_row[:, t:t + 1], axis=0),
                                                 y_sb[:, t, :], None).then_inc(put, 16)

            @block.sync
            def _(sp):
                sp.wait_ge(got, 16 * 2 * GT)
                sp.wait_ge(put, 16 * NT)
                view = recvz_d[0:EP, :].rearrange("(h g p k) d -> h g p (k d)", h=2, p=P, k=GT)
                for h in range(2):
                    sp.dma_start(view[h, :, 0, :], tile_first[0:GH, h].rearrange("p k d -> p (k d)")).then_inc(wrote, 16)
                sp.wait_ge(wrote, 32)

    end_phase()
    logit_scope = ExitStack()
    logit = logit_scope.enter_context(nc.sbuf_tensor("logit", [P, T], F32))
    with ExitStack() as c:
        def sb(name, shape, dt=F32):
            return c.enter_context(nc.sbuf_tensor(name, shape, dt))
        idx = sb("e_idx", [P, RB, GT], I32)
        sent = sb("sent", [P, RB, GT, 2 * D])
        drow = sb("drow", [P, RB, GE])
        zrow = sb("zrow", [P, RB, GT * D])
        same = sb("same", [P, 2, GT, P])
        pack = sb("pack", [P, 2, GT * D])
        xc, u, tt, den, qq = (sb(n, [P, 2, GT * D]) for n in ("xc", "u", "tt", "den", "qq"))
        wa2 = sb("wa2", [P, 2])
        wab = sb("wab", [P, 1])
        two = sb("two", [P, 1])
        ps_x = c.enter_context(nc.psum_tensor("ps_xt", [P, 2, 512], F32))
        ps_w = c.enter_context(nc.psum_tensor("ps_wa", [P, 2, 512], F32))
        gathered = [sem(f"a_gat{b}", keep=True) for b in range(RB)]
        rowed = [sem(f"a_row{b}") for b in range(RB)]
        stored = [sem("a_st0"), sem("a_st1")]
        wl, fetched, consts, packed, compared, summed, bent, exped, mids, logged, inverted, chain, dotted, done = (
            sem(f"a_{n}") for n in ("w", "idx", "consts", "packed", "same", "sum", "bent", "exp", "mids", "logged", "inverted",
                                    "chain", "dotted", "done"))
        with nc.Block() as block:
            @block.sync
            def _(sp):
                sp.wait_ge(consts, 1)
                for h in range(2):
                    sp.dma_start(wa2[h * D:(h + 1) * D, h:h + 1], a["L1_gnn_Wa_k"]).then_inc(wl, 16)
                sp.dma_start(wab[:], row_of("L1_gnn_Wa_b", 1)).then_inc(wl, 16)

                def turn(i, first):
                    for b in range(RB):
                        if not first:
                            sp.wait_ge(summed, i * RB + (b + 1 - RB))
                        sp.dma_start(drow[:, b, :], dst_rows(i * RB + b)).then_inc(rowed[b], 16)
                        sp.dma_start(zrow[:, b, :], part_rows(recvz_d, i * RB + b)).then_inc(rowed[b], 16)
                turns(sp, turn)

            @block.gpsimd
            def _(pool):
                def turn(i, first):
                    for b in range(RB):
                        pool.wait_ge(fetched, i * RB + (b + 1))
                        pool.nop(nofuse=True)
                        if not first:
                            pool.wait_ge(summed, i * RB + (b + 1 - RB))
                            pool.nop(nofuse=True)
                            pool.wait_ge(packed, i * RB + (b + 1 - RB))
                            pool.nop(nofuse=True)
                        for k in range(GT):
                            nc.gpsimd.indirect_dma_start(
                                sent[:, b, k, :], None, send_d,
                                bass.IndirectOffsetOnAxis(ap=idx[:, b, k:k + 1], axis=0)).then_inc(gathered[b], 16)
                turns(pool, turn)

            @block.tensor
            def _(pe):
                pe.wait_ge(consts, 3)

                def arguments(i, b, first):
                    pe.wait_ge(rowed[b], i * 32 + 32)
                    pe.wait_ge(gathered[b], i * (16 * GT) + 16 * GT)
                    pe.wait_ge(compared, i * RB + (b + 1))
                    if not (first and b < 2):
                        pe.wait_ge(mids, i * (2 * RB) + (b * 2 - 2))
                    for k in range(GT):
                        x = ps_x[k % 2 * D:k % 2 * D + D, b % 2, k // 2 * P:k // 2 * P + P]
                        nc.tensor.matmul(x, sent[:, b, k, 0:D], ident[:], start=True, stop=False)
                        mm = nc.tensor.matmul(x, zrow[:, b, k * D:(k + 1) * D], same[:, b % 2, k, :], start=False, stop=True)
                    mm.then_inc(summed, 1)

                def dots(i, b, first):
                    pe.wait_ge(chain, i * (3 * RB) + (3 * b + 3))
                    if not first:
                        pe.wait_ge(done, i * RB + (b - 1))
                    for kk in range(GT // 2):
                        mm = nc.tensor.matmul(ps_w[:, b % 2, 2 * kk:2 * kk + 2], qq[:, b % 2, kk * P:(kk + 1) * P], wa2[:],
                                              start=True, stop=True)
                    mm.then_inc(dotted, 1)

                def turn(i, first):
                    for b in range(RB):
                        arguments(i, b, first)
                        if not (first and b < 2):
                            dots(i if b >= 2 else i - 1, (b - 2) % RB, first and b < 4)
                turn(0, True)
                with pe.Fori(1, G // RB) as i:
                    turn(i, False)
                dots(G // RB - 1, RB - 2, False)
                dots(G // RB - 1, RB - 1, False)

            @block.scalar
            def _(act):
                nc.scalar.preload_act_table_set("natural_log_exp_and_others")
                act.wait_ge(consts, 3)

                def front(i, b, first):
                    h = b % 2
                    act.wait_ge(gathered[b], i * (16 * GT) + 16 * GT)
                    if not (first and b < 2):
                        act.wait_ge(stored[h], i * 32 + 16 * (b // 2))
                    nc.scalar.copy(pack[:, h, :].rearrange("p (k d) -> p k d", d=D), sent[:, b, :, D:2 * D]).then_inc(packed, 1)
                    act.wait_ge(bent, i * RB + (b + 1))
                    nc.scalar.activation(u[:, h, :], xc[:, h, :], ACT.Exp).then_inc(exped, 1)
                    act.wait_ge(packed, i * RB + (b + 1))
                    act.dma_start(emb_d[bass.ds(i * RB + b, 1)].rearrange("a p f -> p (a f)"), pack[:, h, :]) \
                        .then_inc(stored[h], 16)

                def back(i, b):
                    act.wait_ge(mids, i * (2 * RB) + (b * 2 + 1))
                    nc.scalar.activation(den[:, b % 2, :], tt[:, b % 2, :], ACT.Ln, bias=two[:, 0:1]).then_inc(logged, 1)
                    act.wait_ge(logged, i * RB + (b + 1))
                    nc.scalar.activation(den[:, b % 2, :], den[:, b % 2, :], ACT.Exp, scale=-1.0).then_inc(inverted, 1)

                def take(i, b):
                    act.wait_ge(dotted, i * RB + (b + 1))
                    nc.scalar.activation(logit[:, bass.ds((i * RB + b) * GT, GT)], ps_w[:, b % 2, 0:GT], ACT.Identity,
                                         bias=wab[:, 0:1]).then_inc(done, 1)

                def turn(i, first):
                    for b in range(RB):
                        front(i, b, first)
                        back(i, b)
                        if not (first and b < 3):
                            take(i if b >= 3 else i - 1, (b - 3) % RB)
                turns(act, turn)
                for b in range(1, RB):
                    take(G // RB - 1, b)
                for h in range(2):
                    act.wait_ge(stored[h], 16 * (G // 2))

            @block.vector
            def _(dve):
                nc.vector.memset(wa2[:], 0.0).then_inc(consts, 1)
                nc.vector.memset(two[:], 2.0).then_inc(consts, 1)
                for b in range(RB):
                    nc.vector.tensor_copy(idx[:, b, :], src_c[:, b * GT:(b + 1) * GT]).then_inc(fetched, 1)
                dve.wait_ge(wl, 48)
                nc.vector.tensor_scalar_mul(wa2[:], wa2[:], -1.0).then_inc(consts, 1)

                def compare(i, b, first):
                    dve.wait_ge(rowed[b], i * 32 + 32)
                    if not (first and b < 2):
                        dve.wait_ge(summed, i * RB + (b - 1))
                    nc.vector.tensor_tensor(
                        same[:, b % 2], drow[:, b, :].rearrange("p (k e) -> p k e", k=GT),
                        dst_c[:, bass.ds((i * RB + b) * GT, GT)].unsqueeze(2).to_broadcast([P, GT, P]),
                        ALU.is_equal).then_inc(compared, 1)

                def front(i, b, last):
                    dve.wait_ge(summed, i * RB + (b + 1))
                    nc.vector.tensor_scalar_min(xc[:, b % 2, :], ps_x[:, b % 2, :], 20.0).then_inc(bent, 1)
                    if not last:
                        nc.vector.tensor_copy(idx[:, b, :], src_c[:, bass.ds((i * RB + b) * GT + RB * GT, GT)]).then_inc(fetched, 1)

                def middle(i, b, first):
                    h = b % 2
                    dve.wait_ge(exped, i * RB + (b + 1))
                    m = Steps(dve, mids, turn=i, per=2 * RB, base=2 * b)
                    m.did(nc.vector.scalar_tensor_tensor(out=tt[:, h, :], in0=u[:, h, :], scalar=2.0, in1=u[:, h, :],
                                                         op0=ALU.add, op1=ALU.mult))
                    m.wait()
                    if not (first and b < 2):
                        dve.wait_ge(dotted, i * RB + (b - 1))
                    m.did(nc.vector.tensor_mul(qq[:, h, :], tt[:, h, :], ps_x[:, h, :]))

                def back(i, b):
                    h = b % 2
                    dve.wait_ge(inverted, i * RB + (b + 1))
                    dve.wait_ge(mids, i * (2 * RB) + (b * 2 + 2))
                    ct = Steps(dve, chain, turn=i, per=3 * RB, base=3 * b)
                    ct.link(nc.vector.scalar_tensor_tensor(out=tt[:, h, :], in0=tt[:, h, :], scalar=2.0, in1=den[:, h, :],
                                                           op0=ALU.add, op1=ALU.mult))
                    ct.link(nc.vector.scalar_tensor_tensor(out=tt[:, h, :], in0=tt[:, h, :], scalar=2.0, in1=den[:, h, :],
                                                           op0=ALU.subtract, op1=ALU.mult))
                    ct.did(nc.vector.tensor_mul(qq[:, h, :], qq[:, h, :], tt[:, h, :]))

                def turn(i, first, last):
                    for b in range(RB):
                        front(i, b, last)
                        if b + 1 < RB:
                            compare(i, b + 1, first)
                        elif not last:
                            compare(i + 1, 0, False)
                        if not (first and b == 0):
                            back(i if b else i - 1, (b - 1) % RB)
                        middle(i, b, first)
                compare(0, 0, True)
                turn(0, True, False)
                with dve.Fori(1, G // RB - 1) as i:
                    turn(i, False, False)
                turn(G // RB - 1, False, True)
                back(G // RB - 1, RB - 1)
    if dbg and dbg["stop"] == "logit":
        dbg["scope"] = logit_scope
        return finish_debug(nc, top, sem, dbg, {"logit": logit[:], "send": send_d})


    end_phase()
    NTB = -(-T // P)

    def tile_block(c0):
        return min(P, T - c0 * P)

    def lin_rows(table, c0):
        return table.rearrange("(t p) -> t p", p=P)[c0 * P:c0 * P + tile_block(c0), :]

    with ExitStack() as c:
        def sb(name, shape, dt=F32):
            return c.enter_context(nc.sbuf_tensor(name, shape, dt))
        turn_s = sb("turn_s", [P, NTB, P])
        ps_t = [c.enter_context(nc.psum_tensor(f"ps_t{q}", [P, P], F32)) for q in range(2)]
        dl, dp, dn, lin = (sb(n, [P, T]) for n in ("dl", "dp", "dn", "lin"))
        cont, nxt, is_end, gap = (sb(n, [P, T]) for n in ("cont", "nxt", "is_end", "gap"))
        run, ends_v, segmax, expo = (sb(n, [P, T]) for n in ("run", "ends_v", "segmax", "expo"))
        gate = sb("gate", [P, 3])
        row_s = sb("row_s", [1, 2, P])
        carry_r = sb("carry_r", [1, P + 1])
        carry_c = sb("carry_c", [P, 1])
        one = sb("one", [1, 1])
        ps_g = c.enter_context(nc.psum_tensor("ps_g", [1, 2, P], F32))
        ps_c1 = c.enter_context(nc.psum_tensor("ps_c1", [P, 1], F32))
        turned, moved, st, ld, vs, pe_row, pe_col, ex, wst, wld, back_t = (
            sem(n) for n in ("m_turned", "m_moved", "m_store", "m_load", "m_dve", "m_row", "m_col", "m_exp", "m_wst", "m_wld",
                             "m_back"))
        ask_row, ask_col, w_ready = sem("m_askrow"), sem("m_askcol"), sem("m_wready")
        border = [(run[:, T - 1:T], gate[:, 0:1], carry_r[:, 0:P]), (segmax[:, 0:1], gate[:, 2:3], carry_r[:, 1:P + 1]),
                  (run[:, T - 1:T], gate[:, 1:2], carry_r[:, 0:P]), (segmax[:, 0:1], gate[:, 2:3], carry_r[:, 1:P + 1])]
        with nc.Block() as block:
            @block.tensor
            def _(pe):
                for c0 in range(NTB):
                    w = tile_block(c0)
                    if c0 >= 2:
                        pe.wait_ge(moved, c0 - 1)
                    nc.tensor.transpose(ps_t[c0 % 2][0:w, :], logit[:, c0 * P:c0 * P + w], ident[:]).then_inc(turned, 1)
                for n in range(4):
                    pe.wait_ge(ask_row, n + 1)
                    nc.tensor.matmul(ps_g[:, 0, :], border[n][0], ident[:], start=True, stop=True)
                    nc.tensor.matmul(ps_g[:, 1, :], border[n][1], ident[:], start=True, stop=True).then_inc(pe_row, 1)
                    pe.wait_ge(ask_col, n + 1)
                    nc.tensor.matmul(ps_c1[:], border[n][2], one[:], start=True, stop=True).then_inc(pe_col, 1)
                pe.wait_ge(moved, NTB)
                for c0 in range(NTB):
                    w = tile_block(c0)
                    pe.wait_ge(wld, 16 * NTB)
                    if c0 >= 2:
                        pe.wait_ge(back_t, c0 - 1)
                    nc.tensor.transpose(ps_t[c0 % 2][:, 0:w], turn_s[0:w, c0, :], ident[0:w, 0:w]).then_inc(turned, 1)

            @block.sync
            def _(sp):
                for c0 in range(NTB):
                    sp.wait_ge(moved, c0 + 1)
                    sp.dma_start(lin_rows(lin_d, c0), turn_s[0:tile_block(c0), c0, :]).then_inc(st, 16)
                sp.dma_start(dl[:], dstf_d[1:EP + 1].rearrange("(p j) -> p j", p=P)).then_inc(ld, 16)
                sp.dma_start(dp[:], dstf_d[0:EP].rearrange("(p j) -> p j", p=P)).then_inc(ld, 16)
                sp.dma_start(dn[:], dstf_d[2:EP + 2].rearrange("(p j) -> p j", p=P)).then_inc(ld, 16)
                sp.wait_ge(st, 16 * NTB)
                sp.dma_start(lin[:], lin_d.rearrange("(p j) -> p j", p=P)).then_inc(ld, 16)
                sp.wait_ge(w_ready, 1)
                sp.dma_start(wgt_d.rearrange("(p j) -> p j", p=P), run[:]).then_inc(wst, 16)
                sp.wait_ge(wst, 16)
                for c0 in range(NTB):
                    sp.dma_start(turn_s[0:tile_block(c0), c0, :], lin_rows(wgt_d, c0)).then_inc(wld, 16)

            @block.scalar
            def _(act):
                for c0 in range(NTB):
                    act.wait_ge(turned, c0 + 1)
                    w = tile_block(c0)
                    nc.scalar.copy(turn_s[0:w, c0, :], ps_t[c0 % 2][0:w, :]).then_inc(moved, 1)
                act.wait_ge(ex, 1)
                nc.scalar.activation(expo[:], lin[:], ACT.Exp).then_inc(ex, 1)
                for c0 in range(NTB):
                    w = tile_block(c0)
                    act.wait_ge(turned, NTB + c0 + 1)
                    nc.scalar.copy(logit[:, c0 * P:c0 * P + w], ps_t[c0 % 2][:, 0:w]).then_inc(back_t, 1)

            @block.vector
            def _(dve):
                s = Steps(dve, vs)
                s.did(nc.vector.memset(one[:], 1.0))
                dve.wait_ge(ld, 64)
                s.did(nc.vector.tensor_tensor(cont[:], dl[:], dp[:], ALU.is_equal))
                s.link(nc.vector.tensor_tensor(nxt[:], dl[:], dn[:], ALU.is_equal))
                s.did(nc.vector.tensor_scalar(gap[:], cont[:], -1.0, BIG, ALU.add, ALU.mult))
                s.link(nc.vector.tensor_scalar(is_end[:], nxt[:], -1.0, 1.0, ALU.mult, ALU.add))
                s.did(nc.vector.tensor_reduce(gate[:, 0:1], gap[:], AX_X, ALU.min))
                s.did(nc.vector.tensor_reduce(gate[:, 1:2], cont[:], AX_X, ALU.min))
                s.link(nc.vector.tensor_reduce(gate[:, 2:3], nxt[:], AX_X, ALU.min))

                def scan(n, out, g, v, start, op0, op1, reverse):
                    def way(ap):
                        return ap[:, ::-1] if reverse else ap[:]
                    s.link(nc.vector.tensor_tensor_scan(way(out), way(g), way(v), start, op0, op1))
                    dve.sem_inc(ask_row, 1)
                    dve.wait_ge(pe_row, n + 1)
                    s.did(nc.vector.memset(carry_r[:], start))
                    s.link(nc.vector.tensor_copy(row_s[:], ps_g[:]))
                    dst = carry_r[:, P - 1::-1] if reverse else carry_r[:, 1:P + 1]
                    s.link(nc.vector.tensor_tensor_scan(dst, way(row_s[:, 1, :]), way(row_s[:, 0, :]), start, op0, op1))
                    dve.sem_inc(ask_col, 1)
                    dve.wait_ge(pe_col, n + 1)
                    s.link(nc.vector.tensor_copy(carry_c[:], ps_c1[:]))
                    s.link(nc.vector.tensor_tensor_scan(way(out), way(g), way(v), carry_c[:, 0:1], op0, op1))

                scan(0, run, gap, lin, -BIG, ALU.add, ALU.max, False)
                s.link(nc.vector.tensor_mul(ends_v[:], run[:], is_end[:]))
                scan(1, segmax, nxt, ends_v, 0.0, ALU.mult, ALU.add, True)
                s.link(nc.vector.tensor_sub(lin[:], lin[:], segmax[:]))
                dve.sem_inc(ex, 1)
                dve.wait_ge(ex, 2)
                scan(2, run, cont, expo, 0.0, ALU.mult, ALU.add, False)
                s.link(nc.vector.tensor_mul(ends_v[:], run[:], is_end[:]))
                scan(3, segmax, nxt, ends_v, 0.0, ALU.mult, ALU.add, True)
                s.link(nc.vector.reciprocal(segmax[:], segmax[:]))
                s.link(nc.vector.tensor_mul(run[:], expo[:], segmax[:]))
                dve.sem_inc(w_ready, 1)
    if dbg and dbg["stop"] == "soft":
        dbg["scope"] = logit_scope
        return finish_debug(nc, top, sem, dbg, {"logit": logit[:], "send": send_d})

    end_phase()
    with ExitStack() as c:
        def sb(name, shape, dt=F32):
            return c.enter_context(nc.sbuf_tensor(name, shape, dt))
        drow = sb("w_drow", [P, RB, GE])
        emb = sb("w_emb", [P, RB, GT * D])
        same = sb("w_same", [P, RB, GT, P])
        part = sb("w_part", [P, RB, GT * D])
        ps_p = c.enter_context(nc.psum_tensor("ps_p", [P, RB, 512], F32))
        loaded = [sem(f"w_load{b}") for b in range(RB)]
        stored = [sem(f"w_st{b}") for b in range(RB)]
        weighed, summed, moved = sem("w_weighed"), sem("w_summed"), sem("w_moved")

        with nc.Block() as block:
            @block.sync
            def _(sp):
                def turn(i, first):
                    for b in range(RB):
                        g = i * RB + b
                        if not first:
                            sp.wait_ge(summed, i * RB + (b + 1 - RB))
                        sp.dma_start(drow[:, b, :], dst_rows(g)).then_inc(loaded[b], 16)
                        sp.dma_start(emb[:, b, :], emb_d[bass.ds(g, 1)].rearrange("a p f -> p (a f)")).then_inc(loaded[b], 16)
                turns(sp, turn)

            @block.vector
            def _(dve):
                def turn(i, first):
                    for b in range(RB):
                        dve.wait_ge(loaded[b], i * 32 + 32)
                        if not first:
                            dve.wait_ge(summed, i * RB + (b + 1 - RB))
                        for k in range(GT):
                            col = bass.ds((i * RB + b) * GT + k, 1)
                            last = nc.vector.tensor_scalar(same[:, b, k, :], drow[:, b, k * P:(k + 1) * P], dst_c[:, col],
                                                           logit[:, col], ALU.is_equal, ALU.mult)
                        last.then_inc(weighed, 1)
                turns(dve, turn)

            @block.tensor
            def _(pe):
                def turn(i, first):
                    for b in range(RB):
                        pe.wait_ge(weighed, i * RB + (b + 1))
                        if not first:
                            pe.wait_ge(moved, i * RB + (b + 1 - RB))
                        for k in range(GT):
                            mm = nc.tensor.matmul(ps_p[:, b, k * D:(k + 1) * D], same[:, b, k, :], emb[:, b, k * D:(k + 1) * D],
                                                  start=True, stop=True)
                        mm.then_inc(summed, 1)
                turns(pe, turn)

            @block.scalar
            def _(act):
                def turn(i, first):
                    for b in range(RB):
                        act.wait_ge(summed, i * RB + (b + 1))
                        if not first:
                            act.wait_ge(stored[b], i * 16)
                        nc.scalar.copy(part[:, b, :], ps_p[:, b, :]).then_inc(moved, 1)
                        act.wait_ge(moved, i * RB + (b + 1))
                        act.dma_start(part_rows(part_d, i * RB + b), part[:, b, :]).then_inc(stored[b], 16)
                turns(act, turn)
                for b in range(RB):
                    act.wait_ge(stored[b], 16 * (G // RB))
    end_phase()
    logit_scope.close()

    def close1(s):
        s.link(nc.vector.tensor_add(x_sb[:], x_sb[:], y_sb[:]))
    collect("c1", close1)
    if dbg and dbg["stop"] == "L1":
        return finish_debug(nc, top, sem, dbg, {"x": x_sb[:]})

    def sage_fill(n):
        def fill(sp, wcat, wl, extra):
            sp.dma_start(wcat[0:D, :], a[f"L2_gnn_w_self{n}"]).then_inc(wl, 16)
            sp.dma_start(wcat[D:D + 1, :], a[f"L2_gnn_b_self{n}"].rearrange("(a n) -> a n", a=1)).then_inc(wl, 16)
            return 2
        return fill

    def sage(n):
        node_product(f"s{n}", D, sage_fill(n), local=[(slice(0, D), y_sb)])
        sweep(adjT_d, f"L2_gnn_w_s2d{n}", half_in, True)
        sweep(adj_rows, f"L2_gnn_w_d2s{n}", half_out, True)

    def half_biases(s, rows):
        s.link(nc.vector.tensor_add(rows[:, 0, :], rows[:, 0, :], rows[:, 1, :]))
        s.link(nc.vector.tensor_scalar_mul(rows[:, 0, :], rows[:, 0, :], 0.5))
        s.link(nc.vector.tensor_add(y_sb[:], y_sb[:], along(rows[:, 0, :])))

    def between2(s, rows):
        half_biases(s, rows)
        s.link(nc.vector.tensor_scalar_max(h_sb[:], y_sb[:], 0.0))
        split(s)

    def close2(s, rows):
        half_biases(s, rows)
        s.link(nc.vector.tensor_add(x_sb[:], x_sb[:], y_sb[:]))
    norm_phase("2", None, True)
    sage(1)
    bias_phase("2a", ["L2_gnn_b_s2d1", "L2_gnn_b_d2s1"], None, between2)
    sage(2)
    bias_phase("2b", ["L2_gnn_b_s2d2", "L2_gnn_b_d2s2"], None, close2)
    if dbg and dbg["stop"] == "L2":
        return finish_debug(nc, top, sem, dbg, {"x": x_sb[:]})

    norm_phase("3", None, False)

    def hidden_fill(sp, wcat, wl, extra):
        sp.dma_start(wcat[0:D, :], a["L3_gnn_W1n"]).then_inc(wl, 16)
        sp.dma_start(wcat[D:D + 1, :], a["L3_gnn_b1n"].rearrange("(a n) -> a n", a=1)).then_inc(wl, 16)
        return 2
    node_product("n3", D, hidden_fill, stores=[(slice(0, D), xt_d)], hidden=True)

    with ExitStack() as c:
        def sb(name, shape, dt=F32):
            return c.enter_context(nc.sbuf_tensor(name, shape, dt))
        idx = sb("x_idx", [P, RB, GT], I32)
        xg = sb("x_rows", [P, RB, GT, D])
        dst2 = sb("x_dst2", [2, RB, GE], BF16)
        ones2 = sb("x_ones2", [2, P], BF16)
        gates = sb("x_gates", [P, RB, GT * D])
        same = sb("x_same", [P, RB, GT, P])
        msg = sb("x_msg", [P, RB, GT * D])
        part = sb("x_part", [P, RB, GT * D])
        ps_d = c.enter_context(nc.psum_tensor("ps_d3", [P, 2, 2, 512], F32))
        ps_p = c.enter_context(nc.psum_tensor("ps_p3", [P, RB, 512], F32))
        gathered = [sem(f"x_gat{b}", keep=True) for b in range(RB)]
        rowed = [sem(f"x_row{b}") for b in range(RB)]
        loaded = [sem(f"x_load{b}") for b in range(RB)]
        stored = [sem(f"x_st{b}") for b in range(RB)]
        const, spread, fetched, compared, msgs, summed, moved = (
            sem(n) for n in ("x_const", "x_spread", "x_idx_s", "x_same_s", "x_msgs", "x_sum", "x_moved"))
        with nc.Block() as block:
            @block.sync
            def _(sp):
                def turn(i, first):
                    for b in range(RB):
                        g = i * RB + b
                        if not first:
                            sp.wait_ge(compared, i * RB + (b + 1 - RB))
                        sp.dma_start(dst2[:, b, :], dst2_d[:, bass.ds(g * GE, GE)]).then_inc(rowed[b], 16)
                        if not first:
                            sp.wait_ge(msgs, i * RB + (b + 1 - RB))
                        sp.dma_start(gates[:, b, :], gate_d[bass.ds(g, 1)].rearrange("a p f -> p (a f)")).then_inc(loaded[b], 16)
                turns(sp, turn)

            @block.gpsimd
            def _(pool):
                def turn(i, first):
                    for b in range(RB):
                        pool.wait_ge(fetched, i * RB + (b + 1))
                        pool.nop(nofuse=True)
                        if not first:
                            pool.wait_ge(msgs, i * RB + (b + 1 - RB))
                            pool.nop(nofuse=True)
                        for k in range(GT):
                            nc.gpsimd.indirect_dma_start(
                                xg[:, b, k, :], None, xt_d,
                                bass.IndirectOffsetOnAxis(ap=idx[:, b, k:k + 1], axis=0)).then_inc(gathered[b], 16)
                turns(pool, turn)

            @block.vector
            def _(dve):
                nc.vector.memset(ones2[:], 1.0).then_inc(const, 1)
                for b in range(RB):
                    nc.vector.tensor_copy(idx[:, b, :], src_c[:, b * GT:(b + 1) * GT]).then_inc(fetched, 1)

                def turn(i, first, last=False):
                    for b in range(RB):
                        g = i * RB + b
                        dve.wait_ge(spread, i * RB + (b + 1))
                        if not first:
                            dve.wait_ge(summed, i * RB + (b + 1 - RB))
                        nc.vector.tensor_tensor(
                            same[:, b], ps_d[:, b % 2].rearrange("p h (k e) -> p (h k) e", e=P),
                            dst_c[:, bass.ds(g * GT, GT)].unsqueeze(2).to_broadcast([P, GT, P]),
                            ALU.is_equal).then_inc(compared, 1)
                        dve.wait_ge(gathered[b], i * (16 * GT) + 16 * GT)
                        if not last:
                            nc.vector.tensor_copy(idx[:, b, :], src_c[:, bass.ds((g + RB) * GT, GT)]).then_inc(fetched, 1)
                        dve.wait_ge(loaded[b], i * 16 + 16)
                        nc.vector.tensor_mul(msg[:, b, :], gates[:, b, :], xg[:, b].rearrange("p k d -> p (k d)")) \
                            .then_inc(msgs, 1)
                turn(0, True)
                with dve.Fori(1, G // RB - 1) as i:
                    turn(i, False)
                turn(G // RB - 1, False, True)

            @block.tensor
            def _(pe):
                pe.wait_ge(const, 1)

                def spread_dst(i, b, first):
                    pe.wait_ge(rowed[b], i * 16 + 16)
                    if not (first and b < 2):
                        pe.wait_ge(compared, i * RB + (b - 1))
                    for half in range(2):
                        mm = nc.tensor.matmul(ps_d[:, b % 2, half, :], ones2[:], dst2[:, b, half * 512:(half + 1) * 512],
                                              start=True, stop=True)
                    mm.then_inc(spread, 1)

                def sums(i, b, first):
                    pe.wait_ge(msgs, i * RB + (b + 1))
                    pe.wait_ge(compared, i * RB + (b + 1))
                    if not first:
                        pe.wait_ge(moved, i * RB + (b + 1 - RB))
                    for k in range(GT):
                        mm = nc.tensor.matmul(ps_p[:, b, k * D:(k + 1) * D], same[:, b, k, :], msg[:, b, k * D:(k + 1) * D],
                                              start=True, stop=True)
                    mm.then_inc(summed, 1)

                def turn(i, first):
                    for b in range(RB):
                        spread_dst(i, b, first)
                        if not (first and b == 0):
                            sums(i if b else i - 1, (b - 1) % RB, first)
                turns(pe, turn)
                sums(G // RB - 1, RB - 1, False)

            @block.scalar
            def _(act):
                def turn(i, first):
                    for b in range(RB):
                        act.wait_ge(summed, i * RB + (b + 1))
                        if not first:
                            act.wait_ge(stored[b], i * 16)
                        nc.scalar.copy(part[:, b, :], ps_p[:, b, :]).then_inc(moved, 1)
                        act.wait_ge(moved, i * RB + (b + 1))
                        act.dma_start(part_rows(part_d, i * RB + b), part[:, b, :]).then_inc(stored[b], 16)
                turns(act, turn)
                for b in range(RB):
                    act.wait_ge(stored[b], 16 * (G // RB))

    end_phase()
    with ExitStack() as c:
        rows = c.enter_context(nc.sbuf_tensor("rows3", [P, 2, D], F32))
        res = c.enter_context(nc.sbuf_tensor("res3", [P, 1], F32))
        mean, var, std, rstd = (c.enter_context(nc.sbuf_tensor(n, [P, NT], F32)) for n in ("mean4", "var4", "std4", "rstd4"))
        wl = sem("f_w", keep=True)
        with nc.Block() as block:
            @block.sync
            def _(sp):
                sp.dma_start(rows[:, 0, :], row_of("L3_gnn_gamma")).then_inc(wl, 16)
                sp.dma_start(rows[:, 1, :], row_of("L3_gnn_beta")).then_inc(wl, 16)
                sp.dma_start(res[:], row_of("L3_gnn_res_w", 1)).then_inc(wl, 16)
                sp.wait_ge(wl, 48)
        def close3(s):
            s.link(nc.vector.scalar_tensor_tensor(out=h_sb[:].rearrange("p t d -> p (t d)"),
                                                  in0=y_sb[:].rearrange("p t d -> p (t d)"), scalar=res[:, 0:1],
                                                  in1=h_sb[:].rearrange("p t d -> p (t d)"), op0=ALU.mult, op1=ALU.add))
            s.link(nc.vector.tensor_reduce(mean[:], h_sb[:], AX_X, ALU.add))
            s.link(nc.vector.tensor_scalar_mul(mean[:], mean[:], 1.0 / D))
            s.link(nc.vector.tensor_sub(h_sb[:], h_sb[:], each(mean[:])))
            s.link(nc.vector.tensor_mul(t_sb[:], h_sb[:], h_sb[:]))
            s.link(nc.vector.tensor_reduce(var[:], t_sb[:], AX_X, ALU.add))
            s.link(nc.vector.tensor_scalar(var[:], var[:], 1.0 / D, EPS, ALU.mult, ALU.add))
        collect("c3", close3)
        done, vs, rooted = sem("f_done"), sem("f_dve"), sem("f_root")
        full = N_NODES // P
        with nc.Block() as block:
            @block.scalar
            def _(act):
                nc.scalar.sqrt(std[:], var[:]).then_inc(rooted, 1)

            @block.vector
            def _(dve):
                s = Steps(dve, vs)
                dve.wait_ge(rooted, 1)
                s.link(nc.vector.reciprocal(rstd[:], std[:]))
                s.link(nc.vector.tensor_mul(h_sb[:], h_sb[:], each(rstd[:])))
                s.link(nc.vector.tensor_mul(h_sb[:], h_sb[:], along(rows[:, 0, :])))
                s.link(nc.vector.tensor_add(h_sb[:], h_sb[:], along(rows[:, 1, :])))
                s.link(nc.vector.tensor_add(x_sb[:], x_sb[:], h_sb[:]))
                dve.sem_inc(done, 1)

            @block.sync
            def _(sp):
                if out is not None:
                    sp.wait_ge(done, 1)
                    sp.dma_start(out[0:full * P, :].rearrange("(t p) d -> p t d", p=P), x_sb[:, 0:full, :]).then_inc(wl, 16)
                    sp.dma_start(out[full * P:N_NODES, :], x_sb[0:N_NODES - full * P, full, :]).then_inc(wl, 16)
                    sp.wait_ge(wl, 48 + 32)
    if dbg and dbg["stop"] == "L3":
        return finish_debug(nc, top, sem, dbg, {"x": x_sb[:]})
    passing["scope"].close()
    top.close()


def finish_debug(nc, top, sem, dbg, what):
    s = sem("dbg", keep=True)
    with nc.Block() as block:
        @block.sync
        def _(sp):
            n = 0
            for name, src in what.items():
                if name in dbg["aps"]:
                    sp.dma_start(dbg["aps"][name], src).then_inc(s, 16)
                    n += 16
            sp.wait_ge(s, n)
    if "scope" in dbg:
        dbg["scope"].close()
    top.close()


def layout(inputs):
    import numpy as np

    arrays = {k: np.ascontiguousarray(v) for k, v in inputs.items() if k.startswith("L")}
    x = np.zeros((NP, D), np.float32)
    x[:N_NODES] = inputs["x"]
    arrays["x"] = x
    order = np.arange(EP - E_EDGES, dtype=np.int32)
    pad = order % (NP - N_NODES) + N_NODES
    pad_dst = order * (NP - N_NODES) // (EP - E_EDGES) + N_NODES
    src = np.concatenate([np.asarray(inputs["src"]), pad])
    dst = np.concatenate([np.asarray(inputs["dst"]), pad_dst])
    for name, v in (("src", src), ("dst", dst)):
        arrays[f"{name}_lin"] = v.reshape(P, T)
        arrays[f"{name}_col"] = np.ascontiguousarray(v.reshape(T, P).T)
    attr = np.zeros((DE, EP), np.float32)
    attr[:, :E_EDGES] = np.asarray(inputs["edge_attr_32"]).T
    arrays["attr_T"] = attr
    arrays["L1_We_T"] = np.ascontiguousarray(
        np.concatenate([np.asarray(inputs["L1_gnn_We_k"]).reshape(D, D), np.asarray(inputs["L1_gnn_We_b"])]).T)
    return arrays


def kernel(**inputs):
    import concourse.bacc as _bacc
    from concourse.bass_utils import run_bass_kernel_spmd as _run

    nc = _bacc.Bacc("TRN2", target_bir_lowering=False, num_devices=1)
    arrays, aps = {}, {}
    for name, v in layout(inputs).items():
        arrays[f"in_{name}_dram"] = v
        aps[name] = nc.dram_tensor(f"in_{name}_dram", v.shape, mybir.dt.from_np(v.dtype), kind="ExternalInput").ap()
    out = nc.dram_tensor("out_dram", (N_NODES, D), F32, kind="ExternalOutput").ap()
    build_program(nc, aps, out, None)
    r = _run(nc, [arrays], core_ids=[0])
    return r.results[0]["out_dram"]
```

```python
from contextlib import ExitStack

import concourse.bass as bass
from concourse import mybir

ALU = mybir.AluOpType
ACT = mybir.ActivationFunctionType
AX_X = mybir.AxisListType.X
F32 = mybir.dt.float32
BF16 = mybir.dt.bfloat16
I32 = mybir.dt.int32

P = 128
N_NODES, D, E_EDGES, DE = 6250, 64, 200000, 32
NT = 49
NP = NT * P
NB = 7
NBLK = NT // NB
BW = NB * P
SPLIT = (4 * P, (NB - 4) * P)
GT = 8
GE = GT * P
G = -(-E_EDGES // GE)
EP = G * GE
T = G * GT
GH = G // 2
SHIFT = 13
PITCH = 1 << SHIFT
TAG = 0x40000000
LESS = 2048.0
SHORT = P
EPS = 1e-5
BIG = 1e30
RB = 4
assert G % RB == 0
assert SHORT <= P and SHORT <= 256
assert NP >= N_NODES and G % 2 == 0 and GE + NP <= PITCH and LESS > GE


class Steps:

    def __init__(self, eng, sem, base=0, turn=0, per=0):
        self.eng, self.sem, self.base, self.turn, self.per, self.n = eng, sem, base, turn, per, 0

    def did(self, instruction, by=1):
        instruction.then_inc(self.sem, by)
        self.n += by

    def wait(self):
        self.eng.wait_ge(self.sem, self.turn * self.per + self.base + self.n)

    def link(self, instruction):
        self.did(instruction)
        self.wait()


def prefetch_row(dram, row, width):
    return dram.rearrange("(a n) -> a n", a=1)[:, bass.ds(row, width)].to_broadcast([P, width])


def build_program(nc, a, out):
    top = ExitStack()

    passing = {"scope": ExitStack(), "numbers": []}

    def sem(name, keep=False):
        if keep:
            return top.enter_context(nc.semaphore(name))
        handle = passing["scope"].enter_context(nc.semaphore(name))
        passing["numbers"].append(handle)
        return handle

    def end_phase():
        numbers = sorted(h.num for h in passing["numbers"])
        while numbers:
            n = 1
            while n < len(numbers) and numbers[n] == numbers[0] + n:
                n += 1
            nc.gpsimd.sem_clear(range(numbers[0], numbers[0] + n))
            numbers = numbers[n:]
        nc.all_engine_barrier()
        passing["scope"].close()
        passing["scope"], passing["numbers"] = ExitStack(), []

    def turns(eng, turn):
        turn(0, True)
        with eng.Fori(1, G // RB) as i:
            turn(i, False)

    def dram(name, shape, dt):
        return nc.dram_tensor(name, shape, dt).ap()

    key_d = dram("key_d", (EP,), I32)
    dst2_d = dram("dst2_d", (2, EP), BF16)
    dstf_d = dram("dstf_d", (EP + 2,), F32)
    adj_d = dram("adj_d", (NP * PITCH, 1), BF16)
    adjT_d = dram("adjT_d", (NP, NP), BF16)
    adj_rows = adj_d.rearrange("(d s) o -> d (s o)", s=PITCH)
    wide_d = dram("wide_d", (NP * PITCH, 1), F32)
    wideT_d = dram("wideT_d", (NP, NP), F32)
    wide_rows = wide_d.rearrange("(d s) o -> d (s o)", s=PITCH)
    send_d = dram("send_d", (NP, 2 * D), F32)
    recv_d = dram("recv_d", (NP, D), F32)
    recvz_d = dram("recvz_d", (EP + NP, D), F32)
    emb_d = dram("emb_d", (G, P, GT * D), F32)
    part_d = dram("part_d", (EP, D), F32)
    gate_d = dram("gate_d", (G, P, GT * D), F32)
    xt_d = dram("xt_d", (NP, D), F32)
    lin_d = dram("lin_d", (EP,), F32)
    wgt_d = dram("wgt_d", (EP,), F32)

    def keep(name, shape, dt):
        return top.enter_context(nc.sbuf_tensor(name, shape, dt))

    x_sb = keep("x_sb", [P, NT, D], F32)
    y_sb = keep("y_sb", [P, NT, D], F32)
    h_sb = keep("h_sb", [P, NT, D], F32)
    t_sb = keep("t_sb", [P, NT, D], F32)
    h3 = keep("h3", [P, NT, 3 * D], BF16)
    src_c = keep("src_c", [P, T], I32)
    dst_c = keep("dst_c", [P, T], F32)
    ident = keep("ident", [P, P], F32)
    identb = keep("identb", [P, P], BF16)
    deg_in = keep("deg_in", [P, NT], F32)
    deg_out = keep("deg_out", [P, NT], F32)
    norm_in = keep("norm_in", [P, NT], F32)
    norm_out = keep("norm_out", [P, NT], F32)
    half_in = keep("half_in", [P, NT], F32)
    half_out = keep("half_out", [P, NT], F32)
    end_row = keep("end_row", [P, NT], I32)
    start_row = keep("start_row", [P, NT], I32)
    own_end = keep("own_end", [P, NT], F32)
    alive = keep("alive", [P, NT], F32)
    carry_row = keep("carry_row", [P, NT], I32)
    carried = keep("carried", [P, NT], F32)
    long_i = keep("long_i", [1, 1], I32)
    first_id = keep("first_id", [P, 2, GT], I32)
    last_id = keep("last_id", [P, 2, GT], F32)

    with ExitStack() as c:
        def sb(name, shape, dt):
            return c.enter_context(nc.sbuf_tensor(name, shape, dt))
        dst_ci = sb("dst_ci", [P, T], I32)
        lin_s = sb("lin_s", [P, T], I32)
        lin_t = sb("lin_t", [P, T], I32)
        key_l = sb("key_l", [P, T], I32)
        key_k = sb("key_k", [P, T], I32)
        dstf_l = sb("dstf_l", [P, T], F32)
        minus1 = sb("minus1", [P, 2], F32)
        far_i = sb("far_i", [P, T], I32)
        far = sb("far", [P, T], F32)
        same_far = sb("same_far", [P, T], F32)
        any_far = sb("any_far", [P, 1], F32)
        one_c = sb("one_c", [P, 1], F32)
        long_f = sb("long_f", [1, 1], F32)
        ps_long = c.enter_context(nc.psum_tensor("ps_long", [1, 1], F32))
        dst2_i = sb("dst2_i", [P, 2, T], I32)
        dst2_l = sb("dst2_l", [P, 2, T], BF16)
        zero_b = sb("zero_b", [P, NP], BF16)
        firsts = sb("firsts", [P, 2, GT], F32)
        ld, st, zr, vs, ids, st2, fld, fs, fm = (sem(n) for n in (
            "p_load", "p_store", "p_zeroed", "p_dve", "p_ident", "p_bounds", "p_far_load", "p_far", "p_long"))
        with nc.Block() as block:
            @block.sync
            def _(sp):
                sp.dma_start(lin_s[:], a["src_lin"]).then_inc(ld, 16)
                sp.dma_start(lin_t[:], a["dst_lin"]).then_inc(ld, 16)
                sp.dma_start(src_c[:], a["src_col"]).then_inc(ld, 16)
                sp.dma_start(dst_ci[:], a["dst_col"]).then_inc(ld, 16)
                sp.dma_start(x_sb[:], a["x"].rearrange("(t p) d -> p t d", p=P)).then_inc(ld, 16)
                sp.wait_ge(fs, 1)
                flat = a["dst_lin"].rearrange("p j -> (p j)")
                sp.dma_start(far_i[0:P - 1, :], flat[SHORT:SHORT + (P - 1) * T].rearrange("(p j) -> p j", j=T)).then_inc(fld, 16)
                sp.dma_start(far_i[P - 1:P, 0:T - SHORT],
                             flat[SHORT + (P - 1) * T:EP].rearrange("(a j) -> a j", a=1)).then_inc(fld, 16)
                sp.wait_ge(vs, 9)
                for r in range(2):
                    sp.dma_start(dst2_d[r].rearrange("(p j) -> p j", p=P), dst2_l[:, r, :]).then_inc(st, 16)
                sp.dma_start(key_d.rearrange("(p j) -> p j", p=P), key_l[:]).then_inc(st, 16)
                sp.dma_start(dstf_d[1:EP + 1].rearrange("(p j) -> p j", p=P), dstf_l[:]).then_inc(st, 16)
                sp.dma_start(dstf_d[0:1].rearrange("(a j) -> a j", a=1), minus1[0:1, 0:1]).then_inc(st, 16)
                sp.dma_start(dstf_d[EP + 1:EP + 2].rearrange("(a j) -> a j", a=1), minus1[0:1, 1:2]).then_inc(st, 16)
                sp.wait_ge(st, 96)
                ends = dstf_d[1:EP + 1].rearrange("(h g k p) -> g h k p", h=2, k=GT, p=P)
                with nc.allow_non_contiguous_dma(reason="one number of each tile"):
                    for h in range(2):
                        sp.dma_start(firsts[0:GH, h, :], ends[:, h, :, 0]).then_inc(st2, 16)
                        sp.dma_start(last_id[0:GH, h, :], ends[:, h, :, P - 1]).then_inc(st2, 16)
                sp.wait_ge(st2, 64)
                sp.wait_ge(ld, 80)

            @block.scalar
            def _(act):
                act.wait_ge(vs, 1)
                with act.Fori(0, NT) as i:
                    act.dma_start(adj_rows[bass.ds(i * P, P), 0:NP], zero_b[:]).then_inc(zr, 16)
                act.dma_start(adj_rows[0:2, NP:NP + GE], zero_b[0:2, 0:GE]).then_inc(zr, 16)
                act.wait_ge(zr, 16 * (NT + 1))

            @block.tensor
            def _(pe):
                pe.wait_ge(fs, 5)
                nc.tensor.matmul(ps_long[:], any_far[:], one_c[:], start=True, stop=True).then_inc(fm, 1)

            @block.gpsimd
            def _(pool):
                nc.gpsimd.memset(ident[:], 0.0).then_inc(ids, 1)
                pool.wait_ge(ids, 1)
                nc.gpsimd.affine_select(out=ident[:], in_=ident[:], compare_op=ALU.not_equal, fill=1.0, base=0,
                                        pattern=[[-1, P]], channel_multiplier=1).then_inc(ids, 1)

            @block.vector
            def _(dve):
                s = Steps(dve, vs)
                fars = Steps(dve, fs)
                fars.did(nc.vector.memset(far_i[:], -1))
                fars.did(nc.vector.memset(one_c[:], 1.0))
                s.did(nc.vector.memset(zero_b[:], 0.0))
                s.did(nc.vector.memset(minus1[:], -1.0))
                dve.wait_ge(ld, 80)
                s.did(nc.vector.tensor_scalar(dst2_i[:, 0, :], lin_t[:], -32, None, ALU.bitwise_and))
                s.did(nc.vector.tensor_scalar(dst2_i[:, 1, :], lin_t[:], 31, None, ALU.bitwise_and))
                s.link(nc.vector.tensor_scalar(key_k[:], lin_t[:], SHIFT, TAG, ALU.logical_shift_left, ALU.bitwise_or))
                s.did(nc.vector.tensor_tensor(key_l[:], key_k[:], lin_s[:], ALU.bitwise_or))
                s.did(nc.vector.tensor_copy(dst2_l[:], dst2_i[:]))
                s.did(nc.vector.tensor_copy(dstf_l[:], lin_t[:]))
                s.did(nc.vector.tensor_copy(dst_c[:], dst_ci[:]))
                dve.wait_ge(ids, 2)
                s.did(nc.vector.tensor_copy(identb[:], ident[:]))
                dve.wait_ge(fld, 32)
                fars.link(nc.vector.tensor_copy(far[:], far_i[:]))
                fars.link(nc.vector.tensor_tensor(same_far[:], far[:], dstf_l[:], ALU.is_equal))
                fars.link(nc.vector.tensor_reduce(any_far[:], same_far[:], AX_X, ALU.max))
                dve.wait_ge(fm, 1)
                fars.link(nc.vector.tensor_scalar_min(long_f[:], ps_long[:], 1.0))
                fars.did(nc.vector.tensor_copy(long_i[:], long_f[:]))
                dve.wait_ge(st2, 64)
                s.did(nc.vector.tensor_copy(first_id[0:GH], firsts[0:GH]))

    end_phase()
    long_flag = nc.values_load(long_i[0:1, 0:1], min_val=0, max_val=1)

    def idle(block, *engines):
        for name in engines:
            {"sync": block.sync, "scalar": block.scalar, "vector": block.vector, "tensor": block.tensor,
             "gpsimd": block.gpsimd}[name](lambda eng: eng.nop(nofuse=True))

    def either(program):
        with nc.If(long_flag > 0):
            program(False)
        with nc.Else():
            program(True)

    with ExitStack() as c:
        def sb(name, shape, dt):
            return c.enter_context(nc.sbuf_tensor(name, shape, dt))
        key_row = sb("key_row", [P, 2, GE], I32)
        key_c = sb("key_c", [P, T], I32)
        key_ck = sb("key_ck", [P, T], I32)
        dst_k = sb("dst_k", [P, T], I32)
        earlier = sb("earlier", [P, 2 * GE - P], F32)
        junk = sb("junk", [P, GT, GE], BF16)
        tally = sb("tally", [P, 2, GT], F32)
        again = sb("again", [P, 2, GT], I32)
        slot = sb("slot", [P, 2, GT], I32)
        count_b = sb("count_b", [P, 2, GT], BF16)
        count_f = sb("count_f", [P, 2, GT], F32)
        dump = sb("dump", [P, 2, GT], I32)
        zero_f = sb("zero_f", [P, 8 * GT * D], F32)
        attr = sb("g_attr", [DE + 1, RB, GE], F32)
        w1 = sb("g_w1", [DE + 1, P], F32)
        w2 = sb("g_w2", [P, D], F32)
        b2 = sb("g_b2", [1, GT, D], F32)
        b2_left = sb("g_b2left", [1, GT, D], F32)
        b2_part = sb("g_b2part", [1, 3, GT * D], BF16)
        one_r = sb("g_one", [1, P], BF16)
        hid = sb("g_hid", [P, 2, GE], F32)
        gates = sb("g_gates", [P, RB, GT * D], F32)
        ps_1 = c.enter_context(nc.psum_tensor("ps_1", [P, 2, 2, 512], F32))
        ps_e = c.enter_context(nc.psum_tensor("ps_e", [P, 2, 512], F32))
        ps_hist = c.enter_context(nc.psum_tensor("ps_hist", [P, NT], F32))
        iota_i = sb("src_iota_i", [P, P], I32)
        iota_f = sb("src_iota_f", [P, P], F32)
        src_split_i = y_sb[:].rearrange("p t d -> p (t d)").bitcast(I32).rearrange("p (a t) -> p a t", a=2)
        src_split = t_sb[:].rearrange("p t d -> p (t d)").rearrange("p (a t) -> p a t", a=2)
        hot_flat = h3[:].rearrange("p t d -> p (t d)")
        hot_lo = hot_flat[:, 0:2 * GE].rearrange("p (b k e) -> p b k e", b=2, k=GT)
        hot_hi = hot_flat[:, 2 * GE:2 * GE + 2 * GT * NT].rearrange("p (b k e) -> p b k e", b=2, k=GT)
        hots, hots_used, split_s = sem("b_hots"), sem("b_hots_used"), sem("b_split")
        wl, prep, h1, relued, gated, moved = (sem(n) for n in ("g_w", "g_prep", "g_h1", "g_relu", "g_gated", "g_moved"))
        attr_in = [sem(f"g_attr{b}") for b in range(RB)]
        stored = [sem(f"g_st{b}") for b in range(RB)]
        ld0, vs0 = sem("b_load0"), sem("b_dve0")
        rows = [sem("b_row0"), sem("b_row1")]
        pool0, zr2 = sem("b_pool0"), sem("b_zeroed")
        vs1, ready = sem("b_dve"), sem("b_ready")
        landed = [sem(f"b_landed{half}", keep=True) for half in range(2)]
        def build(short):
            table, count = (adj_d, count_b) if short else (wide_d, count_f)

            def group(i, b):
                return i + b * GH if short else i * 2 + b

            def window(k):
                return (max(0, k * P - SHORT), min(GE, k * P + P + SHORT)) if short else (0, GE)

            with nc.Block() as block:
                @block.sync
                def _(sp):
                    sp.dma_start(dst_k[:], a["dst_col"]).then_inc(ld0, 16)
                    row = lambda n: a[n].rearrange("(a n) -> a n", a=1)
                    for half in range(2):
                        sp.dma_start(w1[0:DE, half * D:(half + 1) * D], a["L3_gnn_W1e"]).then_inc(wl, 16)
                        sp.dma_start(w1[DE:DE + 1, half * D:(half + 1) * D], row("L3_gnn_b1e")).then_inc(wl, 16)
                        sp.dma_start(w2[half * D:(half + 1) * D, :], a["L3_gnn_W2e"]).then_inc(wl, 16)
                    for k in range(GT):
                        sp.dma_start(b2[:, k, :], row("L3_gnn_b2e")).then_inc(wl, 16)
                    for b in range(2):
                        sp.dma_start(key_row[:, b, :], prefetch_row(key_d, group(0, b) * GE, GE)).then_inc(rows[b], 16)
                    with sp.Fori(1, G // 2) as i:
                        for b in range(2):
                            sp.wait_ge(ready, i * 2 + (b - 1))
                            sp.dma_start(key_row[:, b, :], prefetch_row(key_d, group(i, b) * GE, GE)).then_inc(rows[b], 16)
                    for b in range(2):
                        sp.wait_ge(rows[b], 16 * (G // 2))

                @block.scalar
                def _(act):
                    act.wait_ge(vs0, 4)
                    zrows = (EP + NP) // P
                    zv = recvz_d.rearrange("(p r) d -> p (r d)", p=P)
                    step = 8 * GT
                    n = 0
                    for r in range(0, zrows, step):
                        w = min(step, zrows - r)
                        act.dma_start(zv[:, r * D:(r + w) * D], zero_f[:, 0:w * D]).then_inc(zr2, 16)
                        n += 1

                    def attributes(g, b):
                        act.dma_start(attr[0:DE, b, :], a["attr_T"][:, bass.ds(g * GE, GE)]).then_inc(attr_in[b], 16)

                    def store(i, b, first):
                        act.wait_ge(gated, i * RB + (b + 1))
                        if not first:
                            act.wait_ge(stored[b], i * 16)
                        nc.scalar.copy(gates[:, b, :], ps_e[:, b % 2, :]).then_inc(moved, 1)
                        act.wait_ge(moved, i * RB + (b + 1))
                        act.dma_start(gate_d[bass.ds(i * RB + b, 1)].rearrange("a p f -> p (a f)"), gates[:, b, :]) \
                            .then_inc(stored[b], 16)

                    def turn(i, first, last=False):
                        for b in range(RB):
                            act.wait_ge(h1, i * RB + (b + 1))
                            if not last:
                                attributes(i * RB + (b + RB), b)
                            if not (first and b < 2):
                                act.wait_ge(gated, i * RB + (b - 1))
                            nc.scalar.activation(hid[:, b % 2, :], ps_1[:, b % 2].rearrange("p a n -> p (a n)"), ACT.Relu) \
                                .then_inc(relued, 1)
                            if not (first and b == 0):
                                store(i if b else i - 1, (b - 1) % RB, first)
                    for b in range(RB):
                        attributes(b, b)
                    turn(0, True)
                    with act.Fori(1, G // RB - 1) as i:
                        turn(i, False)
                    turn(G // RB - 1, False, True)
                    store(G // RB - 1, RB - 1, False)
                    for b in range(RB):
                        act.wait_ge(stored[b], 16 * (G // RB))
                    act.wait_ge(zr2, 16 * n)

                @block.tensor
                def _(pe):
                    pe.wait_ge(prep, 5)

                    def hidden(i, b, first):
                        pe.wait_ge(attr_in[b], i * 16 + 16)
                        if not (first and b < 2):
                            pe.wait_ge(relued, i * RB + (b - 1))
                        for half in range(2):
                            mm = nc.tensor.matmul(ps_1[:, b % 2, half, :], w1[:], attr[:, b, half * 512:(half + 1) * 512],
                                                  start=True, stop=True)
                        mm.then_inc(h1, 1)

                    def gate(i, b, first):
                        pe.wait_ge(relued, i * RB + (b + 1))
                        if not (first and b < 2):
                            pe.wait_ge(moved, i * RB + (b - 1))
                        for part in range(3):
                            nc.tensor.matmul(ps_e[:, b % 2, :], one_r[:], b2_part[:, part, :], start=part == 0, stop=False)
                        for k in range(GT):
                            mm = nc.tensor.matmul(ps_e[:, b % 2, k * D:(k + 1) * D], hid[:, b % 2, k * P:(k + 1) * P], w2[:],
                                                  start=False, stop=k == GT - 1)
                        mm.then_inc(gated, 1)

                    def histogram(i, b, first, last):
                        pe.wait_ge(hots, i * RB + (b + 1))
                        for k in range(GT):
                            mm = nc.tensor.matmul(ps_hist[:], hot_lo[:, b % 2, k, :], hot_hi[:, b % 2, k, :],
                                                  start=first and b == k == 0, stop=last and b == RB - 1 and k == GT - 1)
                        mm.then_inc(hots_used, 1)

                    def turn(i, first, last=False):
                        for b in range(RB):
                            hidden(i, b, first)
                            if short:
                                histogram(i, b, first, last)
                            if not (first and b == 0):
                                gate(i if b else i - 1, (b - 1) % RB, first and b > 0)
                    turn(0, True)
                    with pe.Fori(1, G // RB - 1) as i:
                        turn(i, False)
                    turn(G // RB - 1, False, True)
                    gate(G // RB - 1, RB - 1, False)

                @block.vector
                def _(dve):
                    s = Steps(dve, vs0)
                    dve.wait_ge(ld0, 16)
                    s.link(nc.vector.tensor_scalar(key_ck[:], dst_k[:], SHIFT, TAG, ALU.logical_shift_left, ALU.bitwise_or))
                    s.did(nc.vector.tensor_tensor(key_c[:], key_ck[:], src_c[:], ALU.bitwise_or))
                    s.did(nc.vector.memset(earlier[:], 1.0))
                    s.link(nc.vector.memset(zero_f[:], 0.0))
                    nc.vector.memset(attr[DE:DE + 1], 1.0).then_inc(prep, 1)
                    nc.vector.memset(one_r[:], 1.0).then_inc(prep, 1)
                    dve.wait_ge(wl, 16 * (6 + GT))
                    nc.vector.tensor_scalar_mul(w1[:, D:P], w1[:, D:P], -1.0).then_inc(prep, 1)
                    nc.vector.tensor_scalar_mul(w2[D:P, :], w2[D:P, :], -0.1).then_inc(prep, 1)
                    for part in range(3):
                        left = b2 if part == 0 else b2_left
                        s.link(nc.vector.tensor_copy(b2_part[:, part, :], left[:].rearrange("a k d -> a (k d)")))
                        s.link(nc.vector.tensor_sub(b2_left[:].rearrange("a k d -> a (k d)"),
                                                    left[:].rearrange("a k d -> a (k d)"), b2_part[:, part, :]))
                    dve.sem_inc(prep, 1)
                    if short:
                        dve.wait_ge(pool0, 3)
                        ss = Steps(dve, split_s)
                        ss.did(nc.vector.tensor_copy(iota_f[:], iota_i[:]))
                        ss.did(nc.vector.tensor_scalar(src_split_i[:, 0, :], src_c[:], P - 1, None, ALU.bitwise_and))
                        ss.link(nc.vector.tensor_scalar(src_split_i[:, 1, :], src_c[:], 7, NP - 1, ALU.logical_shift_right,
                                                        ALU.bitwise_and))
                        ss.link(nc.vector.tensor_copy(src_split[:], src_split_i[:]))
                    dve.wait_ge(pool0, 3)
                    def turn(i, first):
                        t = Steps(dve, vs1, turn=i, per=5 * 2)
                        for b in range(2):
                            dve.wait_ge(rows[b], i * 16 + 16)
                            for k in range(GT):
                                lo, hi = window(k)
                                col = bass.ds(group(i, b) * GT + k, 1)
                                w = earlier[:, GE - P - k * P + lo:GE - P - k * P + hi]
                                last = nc.vector.scalar_tensor_tensor(
                                    out=junk[:, k, lo:hi], in0=key_row[:, b, lo:hi].bitcast(F32), scalar=key_c[:, col].bitcast(F32),
                                    in1=w, op0=ALU.is_equal, op1=ALU.mult, accum_out=tally[:, b, k:k + 1])
                            t.link(last)
                            t.did(nc.vector.tensor_scalar(again[:, b, :], tally[:, b, :], LESS, None, ALU.is_ge))
                            if not first:
                                if short:
                                    dve.wait_ge(landed[b], i * (16 * GT))
                                else:
                                    dve.wait_ge(landed[0], (i * 2 + (b - 1)) * 16 * GT)
                            t.did(nc.vector.tensor_copy(count[:, b, :], tally[:, b, :]))
                            t.link(nc.vector.tensor_scalar(slot[:, b, :], key_c[:, bass.ds(group(i, b) * GT, GT)], TAG - 1, None,
                                                           ALU.bitwise_and))
                            dve.nop(nofuse=True)
                            t.did(nc.vector.copy_predicated(slot[:, b, :], again[:, b, :], dump[:, b, :]))
                            t.wait()
                            dve.sem_inc(ready, 1)
                            if short:
                                if not first:
                                    dve.wait_ge(hots_used, i * 2 + (b - 1))
                                cols = bass.ds(group(i, b) * GT, GT)
                                for into, part, width in ((hot_lo, 0, P), (hot_hi, 1, NT)):
                                    hot = nc.vector.tensor_tensor(
                                        into[:, b], iota_f[:, 0:width].unsqueeze(1).to_broadcast([P, GT, width]),
                                        src_split[:, part, cols].unsqueeze(2).to_broadcast([P, GT, width]), ALU.is_equal)
                                hot.then_inc(hots, 1)

                    turn(0, True)
                    with dve.Fori(1, G // 2) as i:
                        turn(i, False)
                    if short:
                        dve.wait_ge(hots_used, G)
                        nc.vector.tensor_copy(deg_out[:], ps_hist[:]).then_inc(split_s, 1)

                @block.gpsimd
                def _(pool):
                    pool.wait_ge(vs0, 3)
                    nc.gpsimd.affine_select(out=earlier[:], in_=earlier[:], compare_op=ALU.is_ge, fill=1.0 + LESS,
                                            base=-(GE - P), pattern=[[1, 2 * GE - P]],
                                            channel_multiplier=-1).then_inc(pool0, 1)
                    nc.gpsimd.iota(iota_i[:], pattern=[[1, P]], base=0, channel_multiplier=0).then_inc(pool0, 1)
                    nc.gpsimd.iota(dump[:], pattern=[[PITCH, 2], [P, GT]], base=NP, channel_multiplier=1).then_inc(pool0, 1)
                    def turn(i, first):
                        for b in range(2):
                            pool.wait_ge(ready, i * 2 + (b + 1))
                            pool.nop(nofuse=True)
                            if short and not first:
                                pool.wait_ge(landed[b], i * (16 * GT))
                                pool.nop(nofuse=True)
                            elif not short and not (first and b == 0):
                                pool.wait_ge(landed[0], (i * 2 + b) * 16 * GT)
                                pool.nop(nofuse=True)
                            for k in range(GT):
                                nc.gpsimd.indirect_dma_start(
                                    table, bass.IndirectOffsetOnAxis(ap=slot[:, b, k:k + 1], axis=0),
                                    count[:, b, k:k + 1], None, compute_op=ALU.add).then_inc(landed[b if short else 0], 16)

                    turn(0, True)
                    with pool.Fori(1, G // 2) as i:
                        turn(i, False)
                    for half in range(2 if short else 1):
                        pool.wait_ge(landed[half], 16 * GT * (GH if short else G))

        def zero_wide():
            zeroed, blank = sem("wz_zeroed"), sem("wz_blank")
            step = GE * 4
            with nc.Block() as block:
                @block.vector
                def _(dve):
                    nc.vector.memset(zero_f[:], 0.0).then_inc(blank, 1)

                @block.sync
                def _(sp):
                    sp.wait_ge(blank, 1)
                    with sp.Fori(0, NT) as i:
                        for c0 in range(0, NP, step):
                            w = min(step, NP - c0)
                            sp.dma_start(wide_rows[bass.ds(i * P, P), c0:c0 + w], zero_f[:, 0:w]).then_inc(zeroed, 16)
                    sp.dma_start(wide_rows[0:2, NP:NP + GE], zero_f[0:2, 0:GE]).then_inc(zeroed, 16)
                    sp.wait_ge(zeroed, 16 * (NT * len(range(0, NP, step)) + 1))
                idle(block, "scalar", "tensor", "gpsimd")

        def zero_and_build(short):
            if not short:
                zero_wide()
            build(short)
        either(zero_and_build)

    end_phase()
    def transpose_wide():
        with ExitStack() as c:
            def sb(name, shape, dt):
                return c.enter_context(nc.sbuf_tensor(name, shape, dt))
            rows = sb("wt_rows", [P, NP], F32)
            cols = sb("wt_cols", [P, NT, P], F32)
            out_part = sb("wt_out", [P, NT, NT], F32)
            ps = [c.enter_context(nc.psum_tensor(f"wt_ps{q}", [P, P], F32)) for q in range(2)]
            loaded, stored, turned, moved, degs = (sem(n) for n in ("wt_load", "wt_store", "wt_turned", "wt_moved", "wt_degs"))
            with nc.Block() as block:
                @block.sync
                def _(sp):
                    def turn(i, first):
                        if not first:
                            sp.wait_ge(degs, i * 2)
                            sp.nop(nofuse=True)
                            sp.wait_ge(turned, i * NT)
                            sp.nop(nofuse=True)
                        sp.dma_start(rows[:], wide_rows[bass.ds(i * P, P), 0:NP]).then_inc(loaded, 16)
                        sp.wait_ge(degs, i * 2 + 2)
                        sp.nop(nofuse=True)
                        sp.dma_start(wideT_d[:, bass.ds(i * P, P)].rearrange("(t p) s -> p t s", p=P), cols[:]) \
                            .then_inc(stored, 16)
                    turn(0, True)
                    with sp.Fori(1, NT) as i:
                        turn(i, False)
                    sp.wait_ge(stored, 16 * NT)

                @block.tensor
                def _(pe):
                    def turn(i, first):
                        pe.wait_ge(loaded, i * 16 + 16)
                        for t in range(NT):
                            if not (first and t < 2):
                                pe.wait_ge(moved, i * NT + (t - 1))
                            nc.tensor.transpose(ps[t % 2][:], rows[:, t * P:(t + 1) * P], ident[:]).then_inc(turned, 1)
                            if t == NT - 1:
                                pe.wait_ge(moved, i * NT + NT)
                    turn(0, True)
                    with pe.Fori(1, NT) as i:
                        turn(i, False)

                @block.scalar
                def _(act):
                    def turn(i, first):
                        if not first:
                            act.wait_ge(stored, i * 16)
                        for t in range(NT):
                            act.wait_ge(turned, i * NT + (t + 1))
                            nc.scalar.copy(cols[:, t, :], ps[t % 2][:]).then_inc(moved, 1)
                    turn(0, True)
                    with act.Fori(1, NT) as i:
                        turn(i, False)

                @block.vector
                def _(dve):
                    with dve.Fori(0, NT) as i:
                        dve.wait_ge(loaded, i * 16 + 16)
                        nc.vector.tensor_reduce(deg_in[:, bass.ds(i, 1)], rows[:], AX_X, ALU.add).then_inc(degs, 1)
                        dve.wait_ge(moved, i * NT + NT)
                        nc.vector.tensor_reduce(out_part[:, :, bass.ds(i, 1)].rearrange("p t o -> p (t o)"), cols[:], AX_X,
                                                ALU.add).then_inc(degs, 1)
                    dve.wait_ge(degs, 2 * NT)
                    nc.vector.tensor_reduce(deg_out[:], out_part[:], AX_X, ALU.add).then_inc(degs, 1)
                idle(block, "gpsimd")

    with nc.If(long_flag > 0):
        transpose_wide()

    end_phase()
    with ExitStack() as c:
        clipped = c.enter_context(nc.sbuf_tensor("o_clipped", [P, NT], F32))
        root = c.enter_context(nc.sbuf_tensor("o_root", [P, NT], F32))
        vs, rooted = sem("o_dve"), sem("o_root_s")
        with nc.Block() as block:
            @block.scalar
            def _(act):
                act.wait_ge(vs, 1)
                nc.scalar.sqrt(root[:], clipped[:]).then_inc(rooted, 1)

            @block.vector
            def _(dve):
                nc.vector.tensor_scalar_max(clipped[:], deg_out[:], 1.0).then_inc(vs, 1)
                dve.wait_ge(rooted, 1)
                nc.vector.reciprocal(norm_out[:], root[:]).then_inc(vs, 1)

    end_phase()
    def each(row):
        return row.unsqueeze(2).to_broadcast([P, NT, D])

    def along(vector):
        return vector.unsqueeze(1).to_broadcast([P, NT, D])

    def row_of(name, width=D):
        return a[name].rearrange("(a n) -> a n", a=1).to_broadcast([P, width])

    def split(s):
        for part in range(3):
            src = h_sb if part == 0 else t_sb
            s.link(nc.vector.tensor_copy(h3[:, :, part * D:(part + 1) * D], src[:]))
            if part < 2:
                s.link(nc.vector.tensor_sub(t_sb[:], src[:], h3[:, :, part * D:(part + 1) * D]))

    def norm_phase(tag, scale, with_split):
        with ExitStack() as c:
            mean = c.enter_context(nc.sbuf_tensor(f"mean{tag}", [P, NT], F32))
            var = c.enter_context(nc.sbuf_tensor(f"var{tag}", [P, NT], F32))
            std = c.enter_context(nc.sbuf_tensor(f"std{tag}", [P, NT], F32))
            rstd = c.enter_context(nc.sbuf_tensor(f"rstd{tag}", [P, NT], F32))
            vs, rooted = sem(f"ln_dve{tag}"), sem(f"ln_root{tag}")
            with nc.Block() as block:
                @block.scalar
                def _(act):
                    act.wait_ge(vs, 6)
                    nc.scalar.sqrt(std[:], var[:]).then_inc(rooted, 1)

                @block.vector
                def _(dve):
                    s = Steps(dve, vs)
                    s.link(nc.vector.tensor_reduce(mean[:], x_sb[:], AX_X, ALU.add))
                    s.link(nc.vector.tensor_scalar_mul(mean[:], mean[:], 1.0 / D))
                    s.link(nc.vector.tensor_sub(h_sb[:], x_sb[:], each(mean[:])))
                    s.link(nc.vector.tensor_mul(t_sb[:], h_sb[:], h_sb[:]))
                    s.link(nc.vector.tensor_reduce(var[:], t_sb[:], AX_X, ALU.add))
                    s.link(nc.vector.tensor_scalar(var[:], var[:], 1.0 / D, EPS, ALU.mult, ALU.add))
                    dve.wait_ge(rooted, 1)
                    s.link(nc.vector.reciprocal(rstd[:], std[:]))
                    if scale is not None:
                        s.link(nc.vector.tensor_mul(rstd[:], rstd[:], scale[:]))
                    s.link(nc.vector.tensor_scalar_max(h_sb[:], h_sb[:], 0.0))
                    s.link(nc.vector.tensor_mul(h_sb[:], h_sb[:], each(rstd[:])))
                    if with_split:
                        split(s)
        end_phase()

    sw_load = [sem(f"s_load{q}", keep=True) for q in range(4)]
    sw_used, sw_high, sw_low, sw_made, sw_taken, sw_w, sw_chain = (
        sem(n, keep=True) for n in ("s_used", "s_high", "s_low", "s_made", "s_taken", "s_weights", "s_chain"))
    sweeps = [0]

    def sweep(in_edges, weight, scale, accumulate):
        n = sweeps[0]
        sweeps[0] += 1

        def program(short):
            if short:
                sweep_short(n, adjT_d if in_edges else adj_rows, weight, scale, accumulate)
            else:
                sweep_wide(n, wideT_d if in_edges else wide_rows, weight, scale, accumulate)
        either(program)

    def sweep_wide(n, matrix, weight, scale, accumulate):
        with ExitStack() as c:
            blk = c.enter_context(nc.sbuf_tensor(f"ws_blk{n}", [P, NT, P], F32))
            sums = c.enter_context(nc.sbuf_tensor(f"ws_sums{n}", [D, P], F32))
            w = c.enter_context(nc.sbuf_tensor(f"ws_w{n}", [D, D], F32))
            got = c.enter_context(nc.sbuf_tensor(f"ws_got{n}", [P, D], F32))
            ps_s = c.enter_context(nc.psum_tensor(f"ws_ps{n}", [D, P], F32))
            ps_o = c.enter_context(nc.psum_tensor(f"ws_po{n}", [P, D], F32))
            wl, loaded, swept, copied, made, scaled, taken = (
                sem(f"ws_{x}{n}") for x in ("wl", "loaded", "swept", "copied", "made", "scaled", "taken"))
            with nc.Block() as block:
                @block.sync
                def _(sp):
                    sp.dma_start(w[:], a[weight]).then_inc(wl, 16)

                    def turn(i, first):
                        if not first:
                            sp.wait_ge(swept, i)
                            sp.nop(nofuse=True)
                        sp.dma_start(blk[:], matrix[0:NP, bass.ds(i * P, P)].rearrange("(t p) s -> p t s", p=P)) \
                            .then_inc(loaded, 16)
                    turn(0, True)
                    with sp.Fori(1, NT) as i:
                        turn(i, False)

                @block.tensor
                def _(pe):
                    pe.wait_ge(wl, 16)
                    with pe.Fori(0, NT) as i:
                        pe.wait_ge(loaded, i * 16 + 16)
                        for k in range(NT):
                            mm = nc.tensor.matmul(ps_s[:], h_sb[:, k, :], blk[:, k, :], start=k == 0, stop=k == NT - 1)
                        mm.then_inc(swept, 1)
                        pe.wait_ge(copied, i + 1)
                        nc.tensor.matmul(ps_o[:], sums[:], w[:], start=True, stop=True).then_inc(made, 1)

                @block.scalar
                def _(act):
                    def turn(i, first):
                        act.wait_ge(swept, i + 1)
                        if not first:
                            act.wait_ge(taken, i)
                        nc.scalar.copy(sums[:], ps_s[:]).then_inc(copied, 1)
                    turn(0, True)
                    with act.Fori(1, NT) as i:
                        turn(i, False)

                @block.vector
                def _(dve):
                    with dve.Fori(0, NT) as i:
                        dve.wait_ge(made, i + 1)
                        if scale is None:
                            nc.vector.tensor_copy(got[:], ps_o[:]).then_inc(scaled, 1)
                        else:
                            nc.vector.tensor_mul(got[:], ps_o[:], scale[:, bass.ds(i, 1)].to_broadcast([P, D])).then_inc(scaled, 1)
                        dve.wait_ge(scaled, i + 1)
                        node = y_sb[:, bass.ds(i, 1), :].rearrange("p a d -> p (a d)")
                        if accumulate:
                            nc.vector.tensor_add(node, node, got[:]).then_inc(taken, 1)
                        else:
                            nc.vector.tensor_copy(node, got[:]).then_inc(taken, 1)
                        dve.wait_ge(taken, i + 1)
                idle(block, "gpsimd")

    def sweep_short(n, matrix, weight, scale, accumulate):
        RING = 4
        uses = [len(range(q, NBLK, RING)) for q in range(RING)]
        tb = n * NBLK
        with ExitStack() as c:
            ring = c.enter_context(nc.sbuf_tensor(f"ring{n}", [P, RING, NB, BW], BF16))
            high = c.enter_context(nc.sbuf_tensor(f"high{n}", [P, BW], F32))
            low = c.enter_context(nc.sbuf_tensor(f"low{n}", [P, SPLIT[0]], F32))
            w2 = c.enter_context(nc.sbuf_tensor(f"w2_{n}", [P, D], F32))
            tmp = c.enter_context(nc.sbuf_tensor(f"swt{n}", [P, NB, D], F32))
            ps_h = c.enter_context(nc.psum_tensor(f"ps_h{n}", [P, 2, 512], F32))
            ps_l = c.enter_context(nc.psum_tensor(f"ps_l{n}", [P, 512], F32))
            ps_y = c.enter_context(nc.psum_tensor(f"ps_y{n}", [P, 2, 512], F32))

            def before(kb, i):
                held = kb - RING if kb >= RING else max(range(kb % RING, NBLK, RING)) - NBLK
                return i * NBLK + (tb * NBLK + held + 1)

            with nc.Block() as block:
                @block.sync
                def _(sp):
                    sp.dma_start(w2[0:D, :], a[weight]).then_inc(sw_w, 16)
                    sp.dma_start(w2[D:P, :], a[weight]).then_inc(sw_w, 16)

                    def turn(i, first):
                        for kb in range(NBLK):
                            if not (first and kb < RING):
                                sp.wait_ge(sw_used, before(kb, i))
                            sp.dma_start(ring[:, kb % RING], matrix[kb * BW:(kb + 1) * BW, bass.ds(i * BW, BW)]
                                         .rearrange("(t p) s -> p t s", p=P)).then_inc(sw_load[kb % RING], 16)
                    turn(0, True)
                    with sp.Fori(1, NBLK) as i:
                        turn(i, False)

                @block.tensor
                def _(pe):
                    pe.wait_ge(sw_w, 32 * (n + 1))

                    def swept(i, kb):
                        q = kb % RING
                        pe.wait_ge(sw_load[q], i * (16 * uses[q]) + 16 * (tb * uses[q] + kb // RING + 1))
                        for t in range(NB):
                            k = kb * NB + t
                            moving = [ring[:, q, t, h * SPLIT[0]:h * SPLIT[0] + SPLIT[h]] for h in range(2)]
                            for h in range(2):
                                nc.tensor.matmul(ps_h[:, h, 0:SPLIT[h]], h3[:, k, 0:P], moving[h], start=k == 0, stop=k == NT - 1)
                            for h in range(2):
                                mm = nc.tensor.matmul(ps_l[h * D:(h + 1) * D, 0:SPLIT[h]], h3[:, k, P:P + D], moving[h],
                                                      start=k == 0, stop=k == NT - 1)
                        mm.then_inc(sw_used, 1)

                    def product(i):
                        pe.wait_ge(sw_taken, i + (tb + 1))
                        for j in range(NB):
                            h, col = j // 4, (j % 4) * P
                            y = ps_y[:, h, (j % 4) * D:(j % 4 + 1) * D]
                            nc.tensor.matmul(y, high[:, j * P:(j + 1) * P], w2[:], start=True, stop=False)
                            mm = nc.tensor.matmul(y, low[h * D:(h + 1) * D, col:col + P], w2[h * D:(h + 1) * D, :],
                                                  start=False, stop=True)
                        mm.then_inc(sw_made, 1)

                    def turn(i, first):
                        pe.wait_ge(sw_high, i + (tb + 1))
                        pe.wait_ge(sw_low, i + (tb + 1))
                        swept(i, 0)
                        if not first:
                            product(i - 1)
                        for kb in range(1, NBLK):
                            swept(i, kb)
                    turn(0, True)
                    with pe.Fori(1, NBLK) as i:
                        turn(i, False)
                    pe.wait_ge(sw_high, tb + NBLK + 1)
                    pe.wait_ge(sw_low, tb + NBLK + 1)
                    product(NBLK - 1)

                @block.scalar
                def _(act):
                    if n == 0:
                        act.sem_inc(sw_low, 1)
                    with act.Fori(0, NBLK) as i:
                        act.wait_ge(sw_used, i * NBLK + (tb * NBLK + NBLK))
                        nc.scalar.copy(low[0:D, :], ps_l[0:D, :])
                        nc.scalar.copy(low[D:P, 0:SPLIT[1]], ps_l[D:P, 0:SPLIT[1]]).then_inc(sw_low, 1)

                @block.vector
                def _(dve):
                    if n == 0:
                        dve.sem_inc(sw_high, 1)
                        dve.sem_inc(sw_taken, 1)
                    with dve.Fori(0, NBLK) as i:
                        dve.wait_ge(sw_used, i * NBLK + (tb * NBLK + NBLK))
                        nc.vector.tensor_copy(high[:, 0:SPLIT[0]], ps_h[:, 0, :])
                        nc.vector.tensor_copy(high[:, SPLIT[0]:BW], ps_h[:, 1, 0:SPLIT[1]]).then_inc(sw_high, 1)
                        dve.wait_ge(sw_made, i + (tb + 1))
                        for h in range(2):
                            tiles = SPLIT[h] // P
                            nodes = bass.ds(i * NB + 4 * h, tiles)
                            sc = scale[:, nodes].unsqueeze(2).to_broadcast([P, tiles, D])
                            y = ps_y[:, h, 0:tiles * D].rearrange("p (t d) -> p t d", d=D)
                            into = tmp[:, 4 * h:4 * h + tiles, :] if accumulate else y_sb[:, nodes, :]
                            ins = nc.vector.tensor_mul(into, y, sc)
                        ins.then_inc(sw_taken, 1)
                        if accumulate:
                            dve.wait_ge(sw_taken, i + (tb + 2))
                            nodes = bass.ds(i * NB, NB)
                            nc.vector.tensor_add(y_sb[:, nodes, :], y_sb[:, nodes, :], tmp[:]).then_inc(sw_chain, 1)
                idle(block, "gpsimd")

    def transpose_and_sweep():
        with ExitStack() as c:
            def sb(name, shape, dt=F32):
                return c.enter_context(nc.sbuf_tensor(name, shape, dt))
            R = 3
            blk = sb("blk", [P, R, NB, BW], BF16)
            blkT = sb("blkT", [P, R, NB, BW], BF16)
            in_part = sb("in_part", [P, NT, NBLK])
            high, low, w2 = sb("t_high", [P, BW]), sb("t_low", [P, SPLIT[0]]), sb("t_w2", [P, D])
            TB = 3
            psT = [c.enter_context(nc.psum_tensor(f"psT{q}", [P, BW], BF16)) for q in range(TB)]
            ps_h = c.enter_context(nc.psum_tensor("t_ps_h", [P, 2, 512], F32))
            ps_l = c.enter_context(nc.psum_tensor("t_ps_l", [P, 512], F32))
            ps_y = c.enter_context(nc.psum_tensor("t_ps_y", [P, 2, 512], F32))
            loaded = [sem(f"t_load{q}") for q in range(R)]
            stored = [sem(f"t_store{q}") for q in range(R)]
            wl, turned, moved, summed, used, highs, lows, made, taken, degs = (
                sem(f"t_{n}") for n in ("w", "turned", "moved", "summed", "used", "high", "low", "made", "taken", "degs"))
            slot = [C % R for C in range(NBLK - 1)] + [(NBLK - 3) % R]
            holders = [[C for C in range(NBLK) if slot[C] == q] for q in range(R)]

            def fresh(C):
                return holders[slot[C]][0] == C

            def before(C, i):
                earlier = [c for c in holders[slot[C]] if c < C]
                return i * NBLK + (earlier[-1] + 1 if earlier else holders[slot[C]][-1] + 1 - NBLK)

            def times(C, i):
                return i * len(holders[slot[C]]) + holders[slot[C]].index(C)

            with nc.Block() as block:
                @block.sync
                def _(sp):
                    sp.dma_start(w2[0:D, :], a["L0_gnn_W1"]).then_inc(wl, 16)
                    sp.dma_start(w2[D:P, :], a["L0_gnn_W1"]).then_inc(wl, 16)

                    def turn(i, first):
                        for C in range(NBLK):
                            if not (first and fresh(C)):
                                sp.wait_ge(turned, before(C, i) * NB)
                                sp.wait_ge(summed, before(C, i))
                            sp.dma_start(blk[:, slot[C]], adj_rows[bass.ds(i * BW, BW), C * BW:(C + 1) * BW]
                                         .rearrange("(t p) s -> p t s", p=P)).then_inc(loaded[slot[C]], 16)
                    turn(0, True)
                    with sp.Fori(1, NBLK) as i:
                        turn(i, False)

                @block.tensor
                def _(pe):
                    pe.wait_ge(wl, 32)

                    def turn_block(i, C, first):
                        pe.wait_ge(loaded[slot[C]], times(C, i) * 16 + 16)
                        for j in range(NB):
                            n = C * NB + j
                            if not (first and n < TB):
                                held = n - TB if n >= TB else max(range(n, NBLK * NB, TB)) - NBLK * NB
                                pe.wait_ge(moved, i * (NBLK * NB) + (held + 1))
                            for t in range(NB):
                                mm = nc.tensor.transpose(psT[n % TB][:, t * P:(t + 1) * P],
                                                         blk[:, slot[C], t, j * P:(j + 1) * P], identb[:])
                            mm.then_inc(turned, 1)

                    def swept(i, C):
                        pe.wait_ge(moved, i * (NBLK * NB) + (C + 1) * NB)
                        if C == 0:
                            pe.wait_ge(highs, i + 1)
                            pe.wait_ge(lows, i + 1)
                        for t in range(NB):
                            k = C * NB + t
                            moving = [blkT[:, slot[C], t, h * SPLIT[0]:h * SPLIT[0] + SPLIT[h]] for h in range(2)]
                            for h in range(2):
                                nc.tensor.matmul(ps_h[:, h, 0:SPLIT[h]], h3[:, k, 0:P], moving[h], start=k == 0, stop=k == NT - 1)
                            for h in range(2):
                                mm = nc.tensor.matmul(ps_l[h * D:(h + 1) * D, 0:SPLIT[h]], h3[:, k, P:P + D], moving[h],
                                                      start=k == 0, stop=k == NT - 1)
                        mm.then_inc(used, 1)

                    def product(i):
                        pe.wait_ge(taken, i + 1)
                        for j in range(NB):
                            h, col = j // 4, (j % 4) * P
                            y = ps_y[:, h, (j % 4) * D:(j % 4 + 1) * D]
                            nc.tensor.matmul(y, high[:, j * P:(j + 1) * P], w2[:], start=True, stop=False)
                            mm = nc.tensor.matmul(y, low[h * D:(h + 1) * D, col:col + P], w2[h * D:(h + 1) * D, :],
                                                  start=False, stop=True)
                        mm.then_inc(made, 1)

                    def turn(i, first):
                        for C in range(NBLK):
                            turn_block(i, C, first)
                            if not (first and C == 0):
                                swept(i if C else i - 1, (C - 1) % NBLK)
                            if C == 1 and not first:
                                product(i - 1)
                    turn(0, True)
                    with pe.Fori(1, NBLK) as i:
                        turn(i, False)
                    swept(NBLK - 1, NBLK - 1)
                    pe.wait_ge(highs, NBLK + 1)
                    pe.wait_ge(lows, NBLK + 1)
                    product(NBLK - 1)

                @block.scalar
                def _(act):
                    act.sem_inc(lows, 1)

                    def take_low(i):
                        act.wait_ge(used, i * NBLK + NBLK)
                        nc.scalar.copy(low[0:D, :], ps_l[0:D, :])
                        nc.scalar.copy(low[D:P, 0:SPLIT[1]], ps_l[D:P, 0:SPLIT[1]]).then_inc(lows, 1)

                    def turn(i, first):
                        for C in range(NBLK):
                            if not (first and fresh(C)):
                                act.wait_ge(stored[slot[C]], times(C, i) * 16)
                                act.wait_ge(used, before(C, i))
                            for j in range(NB):
                                act.wait_ge(turned, i * (NBLK * NB) + (C * NB + j + 1))
                                nc.scalar.copy(blkT[:, slot[C], j, :], psT[(C * NB + j) % TB][:]).then_inc(moved, 1)
                            act.wait_ge(moved, i * (NBLK * NB) + ((C + 1) * NB))
                            act.dma_start(adjT_d[C * BW:(C + 1) * BW, bass.ds(i * BW, BW)].rearrange("(t p) s -> p t s", p=P),
                                          blkT[:, slot[C]]).then_inc(stored[slot[C]], 16)
                            if C == 0 and not first:
                                take_low(i - 1)
                    turn(0, True)
                    with act.Fori(1, NBLK) as i:
                        turn(i, False)
                    take_low(NBLK - 1)
                    for q in range(R):
                        act.wait_ge(stored[q], 16 * len(holders[q]) * NBLK)

                @block.vector
                def _(dve):
                    dve.sem_inc(highs, 1)
                    dve.sem_inc(taken, 1)

                    def take_high(i):
                        dve.wait_ge(used, i * NBLK + NBLK)
                        nc.vector.tensor_copy(high[:, 0:SPLIT[0]], ps_h[:, 0, :])
                        nc.vector.tensor_copy(high[:, SPLIT[0]:BW], ps_h[:, 1, 0:SPLIT[1]]).then_inc(highs, 1)

                    def take_product(i):
                        dve.wait_ge(made, i + 1)
                        for h in range(2):
                            tiles = SPLIT[h] // P
                            ins = nc.vector.tensor_copy(y_sb[:, bass.ds(i * NB + 4 * h, tiles), :],
                                                        ps_y[:, h, 0:tiles * D].rearrange("p (t d) -> p t d", d=D))
                        ins.then_inc(taken, 1)

                    def turn(i, first):
                        for C in range(NBLK):
                            dve.wait_ge(loaded[slot[C]], times(C, i) * 16 + 16)
                            nc.vector.tensor_reduce(in_part[:, bass.ds(i * NB, NB), C], blk[:, slot[C]], AX_X,
                                                    ALU.add).then_inc(summed, 1)
                            if C == 0 and not first:
                                take_high(i - 1)
                            if C == 3 and not first:
                                take_product(i - 1)
                    turn(0, True)
                    with dve.Fori(1, NBLK) as i:
                        turn(i, False)
                    take_high(NBLK - 1)
                    take_product(NBLK - 1)
                    dve.wait_ge(summed, NBLK * NBLK)
                    nc.vector.tensor_reduce(deg_in[:], in_part[:], AX_X, ALU.add).then_inc(degs, 1)
                idle(block, "gpsimd")

    def bias_phase(tag, biases, work):
        with ExitStack() as c:
            rows = c.enter_context(nc.sbuf_tensor(f"rows{tag}", [P, len(biases), D], F32))
            ld, vs = sem(f"bias_load{tag}"), sem(f"bias_dve{tag}")
            with nc.Block() as block:
                @block.sync
                def _(sp):
                    for r, name in enumerate(biases):
                        sp.dma_start(rows[:, r, :], row_of(name)).then_inc(ld, 16)

                @block.vector
                def _(dve):
                    dve.wait_ge(ld, 16 * len(biases))
                    work(Steps(dve, vs), rows)
        end_phase()

    norm_phase("0", norm_out, True)
    either(lambda short: transpose_and_sweep() if short else sweep_wide("first", wideT_d, "L0_gnn_W1", None, False))
    end_phase()
    with ExitStack() as c:
        def sb(name, shape, dt):
            return c.enter_context(nc.sbuf_tensor(name, shape, dt))
        upto = sb("upto", [P, P], F32)
        ones = sb("ones", [P, P], F32)
        tot = sb("tot", [P, NT], F32)
        cum_t = sb("cum_t", [P, NT], F32)
        cum = sb("cum", [P, NT], F32)
        first = sb("first", [P, NT], F32)
        ei = sb("ei", [P, 2, NT], I32)
        ew = sb("ew", [P, 3, 2, NT], I32)
        cl = sb("cl", [P, 2, NT], F32)
        rt = sb("rt", [P, NT], F32)
        no_edge = sb("no_edge", [P, NT], I32)
        spare = sb("spare", [P, NT], I32)
        low = sb("low", [P, NT], F32)
        base = sb("base", [P, NT], F32)
        base_i = sb("base_i", [P, NT], I32)
        tile_k = sb("tile_k", [P, NT], I32)
        ps_in = c.enter_context(nc.psum_tensor("ps_in", [P, NT], F32))
        ps_tot = c.enter_context(nc.psum_tensor("ps_tot", [P, NT], F32))
        vs, pl, mm_s, rooted = sem("n_dve"), sem("n_pool"), sem("n_pe"), sem("n_root")
        with nc.Block() as block:
            @block.gpsimd
            def _(pool):
                nc.gpsimd.memset(upto[:], 1.0).then_inc(pl, 1)
                nc.gpsimd.iota(spare[:], pattern=[[P, NT]], base=EP, channel_multiplier=1).then_inc(pl, 1)
                pool.wait_ge(pl, 2)
                nc.gpsimd.affine_select(out=upto[:], in_=upto[:], compare_op=ALU.is_ge, fill=0.0, base=0,
                                        pattern=[[1, P]], channel_multiplier=-1).then_inc(pl, 1)

            @block.tensor
            def _(pe):
                pe.wait_ge(pl, 3)
                pe.wait_ge(vs, 1)
                nc.tensor.matmul(ps_in[:], upto[:], deg_in[:], start=True, stop=True)
                nc.tensor.matmul(ps_tot[:], ones[:], deg_in[:], start=True, stop=True).then_inc(mm_s, 1)

            @block.scalar
            def _(act):
                act.wait_ge(vs, 3)
                nc.scalar.sqrt(rt[:], cl[:, 0, :]).then_inc(rooted, 1)

            @block.vector
            def _(dve):
                s = Steps(dve, vs)
                s.did(nc.vector.memset(ones[:], 1.0))
                s.did(nc.vector.tensor_scalar_max(cl[:, 0, :], deg_in[:], 1.0))
                s.did(nc.vector.tensor_scalar_max(cl[:, 1, :], deg_out[:], 1.0))
                dve.wait_ge(rooted, 1)
                s.did(nc.vector.reciprocal(norm_in[:], rt[:]))
                s.did(nc.vector.reciprocal(half_in[:], cl[:, 0, :]))
                s.link(nc.vector.reciprocal(half_out[:], cl[:, 1, :]))
                s.did(nc.vector.tensor_scalar_mul(half_in[:], half_in[:], 0.5))
                s.did(nc.vector.tensor_scalar_mul(half_out[:], half_out[:], 0.5))
                dve.wait_ge(mm_s, 1)
                s.link(nc.vector.tensor_copy(tot[:], ps_tot[:]))
                s.link(nc.vector.tensor_tensor_scan(cum_t[:], ones[:, 0:NT], tot[:], 0.0, ALU.mult, ALU.add))
                s.link(nc.vector.tensor_sub(cum_t[:], cum_t[:], tot[:]))
                s.link(nc.vector.tensor_add(cum[:], cum_t[:], ps_in[:]))
                s.link(nc.vector.tensor_sub(first[:], cum[:], deg_in[:]))
                s.did(nc.vector.tensor_copy(ei[:, 1, :], first[:]))
                s.link(nc.vector.tensor_scalar(cum[:], cum[:], -1.0, 0.0, ALU.add, ALU.max))
                s.link(nc.vector.tensor_copy(ei[:, 0, :], cum[:]))
                s.did(nc.vector.tensor_scalar(ew[:, 0], ei[:], -GE, None, ALU.bitwise_and))
                s.did(nc.vector.tensor_scalar(ew[:, 1], ei[:], P - 1, 3, ALU.bitwise_and, ALU.logical_shift_left))
                s.link(nc.vector.tensor_scalar(ew[:, 2], ei[:], 7, GT - 1, ALU.logical_shift_right, ALU.bitwise_and))
                s.link(nc.vector.tensor_tensor(ew[:, 0], ew[:, 0], ew[:, 1], ALU.bitwise_or))
                s.did(nc.vector.tensor_tensor(end_row[:], ew[:, 0, 0], ew[:, 2, 0], ALU.bitwise_or))
                s.did(nc.vector.tensor_tensor(start_row[:], ew[:, 0, 1], ew[:, 2, 1], ALU.bitwise_or))
                s.link(nc.vector.tensor_scalar(no_edge[:], deg_in[:], 0.0, None, ALU.is_equal))
                s.did(nc.vector.copy_predicated(start_row[:], no_edge[:], spare[:]))
                s.link(nc.vector.tensor_scalar(ei[:, 1, :], ei[:, 0, :], P - 1, None, ALU.bitwise_and))
                s.link(nc.vector.tensor_scalar(low[:], ei[:, 1, :], float(P - 1), None, ALU.not_equal))
                s.link(nc.vector.tensor_scalar(alive[:], deg_in[:], 0.0, None, ALU.is_gt))
                s.link(nc.vector.tensor_mul(own_end[:], low[:], alive[:]))
                s.link(nc.vector.tensor_scalar(base_i[:], ei[:, 0, :], -P, None, ALU.bitwise_and))
                s.link(nc.vector.tensor_copy(base[:], base_i[:]))
                s.link(nc.vector.tensor_tensor(carried[:], base[:], first[:], ALU.is_gt))
                s.link(nc.vector.tensor_mul(carried[:], carried[:], alive[:]))
                s.link(nc.vector.tensor_scalar(base[:], base[:], -1.0, 0.0, ALU.add, ALU.max))
                s.link(nc.vector.tensor_copy(base_i[:], base[:]))
                s.link(nc.vector.tensor_scalar(tile_k[:], base_i[:], 7, GT - 1, ALU.logical_shift_right, ALU.bitwise_and))
                s.link(nc.vector.tensor_scalar(carry_row[:], base_i[:], -GE, (P - 1) * GT, ALU.bitwise_and, ALU.bitwise_or))
                s.link(nc.vector.tensor_tensor(carry_row[:], carry_row[:], tile_k[:], ALU.bitwise_or))

    end_phase()

    def between(s, rows):
        s.link(nc.vector.tensor_mul(y_sb[:], y_sb[:], each(norm_in[:])))
        s.link(nc.vector.tensor_add(h_sb[:], y_sb[:], along(rows[:, 0, :])))
        s.link(nc.vector.tensor_scalar_max(h_sb[:], h_sb[:], 0.0))
        s.link(nc.vector.tensor_mul(h_sb[:], h_sb[:], each(norm_out[:])))
        split(s)
    bias_phase("0a", ["L0_gnn_b1"], between)
    sweep(True, "L0_gnn_W2", norm_in, False)

    def close0(s, rows):
        s.link(nc.vector.tensor_add(x_sb[:], x_sb[:], y_sb[:]))
        s.link(nc.vector.tensor_add(x_sb[:], x_sb[:], along(rows[:, 0, :])))
    bias_phase("0b", ["L0_gnn_b2"], close0)

    def node_product(tag, width, fill, local=(), stores=(), hidden=False, prepare=None):
        per_bank = min(NB, 512 // width)
        banks = -(-NB // per_bank)
        with ExitStack() as c:
            def sb(name, shape, dt=F32):
                return c.enter_context(nc.sbuf_tensor(name + tag, shape, dt))
            wid = P if hidden else width
            wcat = sb("wcat", [D + 1, wid])
            hst = sb("hst", [P, NB, D])
            hT = sb("hT", [D + 1, BW])
            stage = sb("stage", [P, NB, width])
            ps_x = c.enter_context(nc.psum_tensor("ps_x" + tag, [D, 2, 512], F32))
            ps_m = c.enter_context(nc.psum_tensor("ps_m" + tag, [P, banks, 512], F32))
            if hidden:
                w2n = sb("w2n", [P, D])
                b2n = sb("b2n", [P, D])
                dps = sb("dps", [P, 1])
                hid = sb("hid", [P, 2, 512])
                act_h = sb("act_h", [P, BW])
                ps_hid = c.enter_context(nc.psum_tensor("ps_hid" + tag, [P, 2, 512], F32))
            copied, turned, moved, made, taken, stored, wl = (
                sem(f"{n}{tag}") for n in ("np_copied", "np_turned", "np_moved", "np_made", "np_taken", "np_stored", "np_w"))
            hid_made, hid_out, hid_act, prep, chain = (
                sem(f"{n}{tag}") for n in ("np_hid", "np_hidout", "np_hidact", "np_prep", "np_chain"))
            extra = prepare(c) if prepare else None
            loads = [0]
            with nc.Block() as block:
                @block.sync
                def _(sp):
                    loads[0] = 16 * fill(sp, wcat, wl, extra)
                    if hidden:
                        sp.dma_start(w2n[:], a["L3_gnn_W2n"]).then_inc(wl, 16)
                        sp.dma_start(b2n[:], row_of("L3_gnn_b2n")).then_inc(wl, 16)
                        sp.dma_start(dps[:], row_of("L3_gnn_dp_scale", 1)).then_inc(wl, 16)
                        loads[0] += 48

                    def turn(i):
                        sp.wait_ge(taken, i + 1)
                        for cols, rows in stores:
                            sp.dma_start(rows[bass.ds(i * BW, BW), :].rearrange("(t p) d -> p t d", p=P),
                                         stage[:, :, cols]).then_inc(stored, 16)
                    if stores:
                        with sp.Fori(0, NBLK) as i:
                            turn(i)
                        sp.wait_ge(stored, 16 * len(stores) * NBLK)

                @block.tensor
                def _(pe):
                    pe.wait_ge(wl, loads[0])
                    if extra is not None:
                        extra["pe"](pe, prep)

                    def turn(i, first):
                        pe.wait_ge(copied, i + 1)
                        pe.nop(nofuse=True)
                        for j in range(NB):
                            tr = nc.tensor.transpose(ps_x[:, j // 4, (j % 4) * P:(j % 4 + 1) * P], hst[:, j, :], ident[:])
                        tr.then_inc(turned, 1)
                        pe.wait_ge(moved, i * 2 + 2)
                        pe.wait_ge(prep, 2)
                        if hidden:
                            for half in range(2):
                                mm = nc.tensor.matmul(ps_hid[:, half, 0:SPLIT[half]], wcat[:],
                                                      hT[:, half * 512:half * 512 + SPLIT[half]], start=True, stop=True)
                            mm.then_inc(hid_made, 1)
                            pe.wait_ge(hid_act, i * 2 + 2)
                        if not first:
                            pe.wait_ge(taken, i)
                        for j in range(NB):
                            dst = ps_m[:, j // per_bank, (j % per_bank) * width:(j % per_bank + 1) * width]
                            if hidden:
                                lhs, rhs = act_h[:, j * P:(j + 1) * P], w2n[:]
                            else:
                                lhs, rhs = hT[:, j * P:(j + 1) * P], wcat[:]
                            mm = nc.tensor.matmul(dst, lhs, rhs, start=True, stop=True)
                        mm.then_inc(made, 1)
                    turn(0, True)
                    with pe.Fori(1, NBLK) as i:
                        turn(i, False)

                @block.scalar
                def _(act):
                    def turn(i, first):
                        act.wait_ge(turned, i + 1)
                        if not first:
                            act.wait_ge(made, i)
                        nc.scalar.copy(hT[0:D, 0:512], ps_x[:, 0, :]).then_inc(moved, 1)
                        nc.scalar.copy(hT[0:D, 512:BW], ps_x[:, 1, 0:BW - 512]).then_inc(moved, 1)
                        if hidden:
                            act.wait_ge(hid_made, i + 1)
                            for half in range(2):
                                nc.scalar.activation(hid[:, half, 0:SPLIT[half]], ps_hid[:, half, 0:SPLIT[half]], ACT.Copy,
                                                     scale=0.1).then_inc(hid_out, 1)
                    turn(0, True)
                    with act.Fori(1, NBLK) as i:
                        turn(i, False)

                @block.vector
                def _(dve):
                    nc.vector.memset(hT[D:D + 1, :], 1.0).then_inc(prep, 1)
                    if extra is not None:
                        extra["dve"](dve, prep, wl, loads[0])
                    else:
                        dve.sem_inc(prep, 1)
                    dve.wait_ge(wl, loads[0])

                    def turn(i, first):
                        nodes = bass.ds(i * NB, NB)
                        if not first:
                            dve.wait_ge(turned, i)
                        nc.vector.tensor_copy(hst[:], h_sb[:, nodes, :]).then_inc(copied, 1)
                        if hidden:
                            dve.wait_ge(hid_out, i * 2 + 2)
                            for half in range(2):
                                nc.vector.tensor_tensor(act_h[:, half * 512:half * 512 + SPLIT[half]],
                                                        ps_hid[:, half, 0:SPLIT[half]], hid[:, half, 0:SPLIT[half]],
                                                        ALU.max).then_inc(hid_act, 1)
                        dve.wait_ge(made, i + 1)
                        if stores and not first:
                            dve.wait_ge(stored, i * (16 * len(stores)))
                        ct = Steps(dve, chain, turn=i, per=banks + (2 if hidden else 0))
                        for b in range(banks):
                            w = min(per_bank, NB - b * per_bank)
                            ct.did(nc.vector.tensor_copy(
                                stage[:, b * per_bank:b * per_bank + w, :],
                                ps_m[:, b, 0:w * width].rearrange("p (j f) -> p j f", j=w)))
                        ct.wait()
                        if hidden:
                            ct.link(nc.vector.tensor_add(stage[:], stage[:], b2n[:].unsqueeze(1).to_broadcast([P, NB, D])))
                            ct.link(nc.vector.tensor_scalar(stage[:], stage[:], dps[:, 0:1], None, ALU.mult))
                        for cols, keep_in in local:
                            nc.vector.tensor_copy(keep_in[:, nodes, :], stage[:, :, cols]).then_inc(sw_chain, 1)
                        dve.nop(nofuse=True)
                        dve.sem_inc(taken, 1)
                    turn(0, True)
                    with dve.Fori(1, NBLK) as i:
                        turn(i, False)
        end_phase()

    def dst_rows(g):
        return dstf_d[1:EP + 1].rearrange("(a n) -> a n", a=1)[:, bass.ds(g * GE, GE)].to_broadcast([P, GE])

    def part_rows(table, g):
        return table[bass.ds(g * GE, GE), :].rearrange("(p k) d -> p (k d)", p=P)

    def collect(tag, finish):
        def both(short):
            (collect_short if short else collect_long)(tag + ("s" if short else "l"), finish)
        either(both)
        end_phase()

    def collect_short(tag, finish):
        with ExitStack() as c:
            carry = c.enter_context(nc.sbuf_tensor(f"carry{tag}", [P, NT, D], F32))
            got, vs = sem(f"c_got{tag}", keep=True), sem(f"c_dve{tag}")
            with nc.Block() as block:
                @block.gpsimd
                def _(pool):
                    for t in range(NT):
                        for into, row in ((y_sb, end_row[:, t:t + 1]), (carry, carry_row[:, t:t + 1])):
                            nc.gpsimd.indirect_dma_start(into[:, t, :], None, part_d,
                                                         bass.IndirectOffsetOnAxis(ap=row, axis=0)).then_inc(got, 16)

                @block.vector
                def _(dve):
                    s = Steps(dve, vs)
                    dve.wait_ge(got, 16 * NT * 2)
                    s.link(nc.vector.tensor_mul(y_sb[:], y_sb[:], each(alive[:])))
                    s.link(nc.vector.tensor_mul(carry[:], carry[:], each(carried[:])))
                    s.link(nc.vector.tensor_add(y_sb[:], y_sb[:], carry[:]))
                    finish(s)

                idle(block, "tensor", "scalar", "sync")

    def collect_long(tag, finish):
        with ExitStack() as c:
            def sb(name, shape, dt=F32):
                return c.enter_context(nc.sbuf_tensor(name + tag, shape, dt))
            last_row = sb("last_row", [P, 2, GT * D])
            iota_i = sb("iota_i", [P, P], I32)
            iota_f = sb("iota_f", [P, P])
            shifted = sb("shifted", [P, NT, 2 * GT])
            node0 = sb("node0", [P, NT])
            node0_i = sb("node0_i", [P, NT], I32)
            hot = sb("hot", [P, 2, 2 * GT, P])
            ps_c = c.enter_context(nc.psum_tensor("ps_c" + tag, [P, 2, 512], F32))
            got = sem(f"c_got{tag}", keep=True)
            ld, pl, hots, picked, taken, vs, chain = (
                sem(f"{n}{tag}") for n in ("c_load", "c_iota", "c_hot", "c_picked", "c_taken", "c_dve", "c_chain"))
            with nc.Block() as block:
                @block.sync
                def _(sp):
                    view = part_d.rearrange("(h g p k) d -> h g p (k d)", h=2, p=P, k=GT)
                    for h in range(2):
                        sp.dma_start(last_row[0:GH, h, :], view[h, :, P - 1, :]).then_inc(ld, 16)

                @block.gpsimd
                def _(pool):
                    nc.gpsimd.iota(iota_i[:], pattern=[[1, P]], base=0, channel_multiplier=0).then_inc(pl, 1)
                    nc.gpsimd.iota(node0_i[:], pattern=[[P, NT]], base=0, channel_multiplier=0).then_inc(pl, 1)
                    for t in range(NT):
                        nc.gpsimd.indirect_dma_start(y_sb[:, t, :], None, part_d,
                                                     bass.IndirectOffsetOnAxis(ap=end_row[:, t:t + 1], axis=0)).then_inc(got, 16)

                idle(block, "scalar")

                @block.tensor
                def _(pe):
                    pe.wait_ge(ld, 32)

                    def node_tile(t2, i, first):
                        pe.wait_ge(hots, i + 1)
                        if not first:
                            pe.wait_ge(taken, i - 1)
                        for q in range(2 * GT):
                            mm = nc.tensor.matmul(ps_c[:, t2, 0:D], hot[0:GH, t2, q, :],
                                                  last_row[0:GH, q // GT, (q % GT) * D:(q % GT + 1) * D],
                                                  start=q == 0, stop=q == 2 * GT - 1)
                        mm.then_inc(picked, 1)
                    for t2 in range(2):
                        node_tile(t2, t2, True)
                    with pe.Fori(2, NT - 1, 2) as i:
                        for t2 in range(2):
                            node_tile(t2, i + t2, False)
                    node_tile(0, NT - 1, False)

                @block.vector
                def _(dve):
                    s = Steps(dve, vs)
                    dve.wait_ge(pl, 2)
                    s.did(nc.vector.tensor_copy(iota_f[:], iota_i[:]))
                    s.link(nc.vector.tensor_copy(node0[:], node0_i[:]))
                    s.link(nc.vector.tensor_sub(
                        shifted[0:GH], last_id[0:GH].rearrange("p h k -> p (h k)").unsqueeze(1).to_broadcast([GH, NT, 2 * GT]),
                        node0[0:GH, :].unsqueeze(2).to_broadcast([GH, NT, 2 * GT])))
                    dve.wait_ge(got, 16 * NT)
                    s.link(nc.vector.tensor_mul(y_sb[:], y_sb[:], each(own_end[:])))

                    def node_tile(t2, i, first):
                        if not first:
                            dve.wait_ge(picked, i - 1)
                        one = iota_f[0:GH, :].unsqueeze(1).to_broadcast([GH, 2 * GT, P])
                        at = shifted[0:GH, bass.ds(i, 1), :].rearrange("p a q -> p (a q)").unsqueeze(2) \
                            .to_broadcast([GH, 2 * GT, P])
                        nc.vector.tensor_tensor(hot[0:GH, t2], one, at, ALU.is_equal).then_inc(hots, 1)

                    def take(t2, i):
                        dve.wait_ge(picked, i + 1)
                        node = y_sb[:, bass.ds(i, 1), :].rearrange("p a d -> p (a d)")
                        nc.vector.tensor_add(node, node, ps_c[:, t2, 0:D]).then_inc(taken, 1)
                    for t2 in range(2):
                        node_tile(t2, t2, True)
                    with dve.Fori(2, NT - 1, 2) as i:
                        for t2 in range(2):
                            take(t2, i + (t2 - 2))
                            node_tile(t2, i + t2, False)
                    take(0, NT - 3)
                    node_tile(0, NT - 1, False)
                    take(1, NT - 2)
                    take(0, NT - 1)
                    dve.wait_ge(taken, NT)
                    finish(s)

    norm_phase("1", None, False)

    def l1_prepare(c):
        weT = c.enter_context(nc.sbuf_tensor("weT", [D, D + 1], F32))
        ws = c.enter_context(nc.sbuf_tensor("ws", [D, D], F32))
        wsb = c.enter_context(nc.sbuf_tensor("wsb", [D + 1, D], F32))
        ps_w = c.enter_context(nc.psum_tensor("ps_w", [D + 1, D], F32))
        fused = sem("l1_fused")

        def pe(eng, prep):
            nc.tensor.matmul(ps_w[:], weT[:], ws[:], start=True, stop=True).then_inc(fused, 1)

        def dve(eng, prep, wl, loads):
            eng.wait_ge(wl, loads)
            eng.wait_ge(fused, 1)
            nc.vector.tensor_copy(both["wcat"][:, 0:D], ps_w[:]).then_inc(fused, 1)
            eng.wait_ge(fused, 2)
            nc.vector.tensor_add(both["wcat"][D:D + 1, 0:D], both["wcat"][D:D + 1, 0:D], wsb[D:D + 1, :]).then_inc(prep, 1)
        both = {"pe": pe, "dve": dve, "weT": weT, "ws": ws, "wsb": wsb}
        return both

    def l1_fill(sp, wcat, wl, extra):
        extra["wcat"] = wcat
        for dst, src in ((wcat[0:D, D:2 * D], a["L1_gnn_We_k"].rearrange("f h d -> f (h d)")),
                         (wcat[D:D + 1, D:2 * D], a["L1_gnn_We_b"]),
                         (wcat[0:D, 2 * D:3 * D], a["L1_gnn_Wr_k"].rearrange("f h d -> f (h d)")),
                         (wcat[D:D + 1, 2 * D:3 * D], a["L1_gnn_Wr_b"]),
                         (extra["weT"][:], a["L1_We_T"]),
                         (extra["ws"][:], a["L1_gnn_Ws_k"]),
                         (extra["wsb"][D:D + 1, :], a["L1_gnn_Ws_b"].rearrange("(a n) -> a n", a=1))):
            sp.dma_start(dst, src).then_inc(wl, 16)
        return 7
    node_product("n1", 3 * D, l1_fill, local=[(slice(2 * D, 3 * D), y_sb)],
                 stores=[(slice(0, 2 * D), send_d), (slice(2 * D, 3 * D), recv_d)], prepare=l1_prepare)

    with ExitStack() as c:
        tile_first = c.enter_context(nc.sbuf_tensor("tile_first", [P, 2, GT, D], F32))
        put, got, wrote = sem("z_put", keep=True), sem("z_got", keep=True), sem("z_wrote")
        with nc.Block() as block:
            @block.gpsimd
            def _(pool):
                for h in range(2):
                    for k in range(GT):
                        nc.gpsimd.indirect_dma_start(
                            tile_first[0:GH, h, k, :], None, recv_d,
                            bass.IndirectOffsetOnAxis(ap=first_id[0:GH, h, k:k + 1], axis=0)).then_inc(got, 16)
                for t in range(NT):
                    nc.gpsimd.indirect_dma_start(recvz_d, bass.IndirectOffsetOnAxis(ap=start_row[:, t:t + 1], axis=0),
                                                 y_sb[:, t, :], None).then_inc(put, 16)

            @block.sync
            def _(sp):
                sp.wait_ge(got, 16 * 2 * GT)
                sp.wait_ge(put, 16 * NT)
                view = recvz_d[0:EP, :].rearrange("(h g p k) d -> h g p (k d)", h=2, p=P, k=GT)
                for h in range(2):
                    sp.dma_start(view[h, :, 0, :], tile_first[0:GH, h].rearrange("p k d -> p (k d)")).then_inc(wrote, 16)
                sp.wait_ge(wrote, 32)

    end_phase()
    logit_scope = ExitStack()
    logit = logit_scope.enter_context(nc.sbuf_tensor("logit", [P, T], F32))
    with ExitStack() as c:
        def sb(name, shape, dt=F32):
            return c.enter_context(nc.sbuf_tensor(name, shape, dt))
        idx = sb("e_idx", [P, RB, GT], I32)
        sent = sb("sent", [P, RB, GT, 2 * D])
        drow = sb("drow", [P, RB, GE])
        zrow = sb("zrow", [P, RB, GT * D])
        same = sb("same", [P, 2, GT, P])
        pack = sb("pack", [P, 2, GT * D])
        xc, u, tt, den, qq = (sb(n, [P, 2, GT * D]) for n in ("xc", "u", "tt", "den", "qq"))
        wa2 = sb("wa2", [P, 2])
        wab = sb("wab", [P, 1])
        two = sb("two", [P, 1])
        ps_x = c.enter_context(nc.psum_tensor("ps_xt", [P, 2, 512], F32))
        ps_w = c.enter_context(nc.psum_tensor("ps_wa", [P, 2, 512], F32))
        gathered = [sem(f"a_gat{b}", keep=True) for b in range(RB)]
        rowed = [sem(f"a_row{b}") for b in range(RB)]
        stored = [sem("a_st0"), sem("a_st1")]
        wl, fetched, consts, packed, compared, summed, bent, exped, mids, logged, inverted, chain, dotted, done = (
            sem(f"a_{n}") for n in ("w", "idx", "consts", "packed", "same", "sum", "bent", "exp", "mids", "logged", "inverted",
                                    "chain", "dotted", "done"))
        with nc.Block() as block:
            @block.sync
            def _(sp):
                sp.wait_ge(consts, 1)
                for h in range(2):
                    sp.dma_start(wa2[h * D:(h + 1) * D, h:h + 1], a["L1_gnn_Wa_k"]).then_inc(wl, 16)
                sp.dma_start(wab[:], row_of("L1_gnn_Wa_b", 1)).then_inc(wl, 16)

                def turn(i, first):
                    for b in range(RB):
                        if not first:
                            sp.wait_ge(summed, i * RB + (b + 1 - RB))
                        sp.dma_start(drow[:, b, :], dst_rows(i * RB + b)).then_inc(rowed[b], 16)
                        sp.dma_start(zrow[:, b, :], part_rows(recvz_d, i * RB + b)).then_inc(rowed[b], 16)
                turns(sp, turn)

            @block.gpsimd
            def _(pool):
                def turn(i, first):
                    for b in range(RB):
                        pool.wait_ge(fetched, i * RB + (b + 1))
                        pool.nop(nofuse=True)
                        if not first:
                            pool.wait_ge(summed, i * RB + (b + 1 - RB))
                            pool.nop(nofuse=True)
                            pool.wait_ge(packed, i * RB + (b + 1 - RB))
                            pool.nop(nofuse=True)
                        for k in range(GT):
                            nc.gpsimd.indirect_dma_start(
                                sent[:, b, k, :], None, send_d,
                                bass.IndirectOffsetOnAxis(ap=idx[:, b, k:k + 1], axis=0)).then_inc(gathered[b], 16)
                turns(pool, turn)

            @block.tensor
            def _(pe):
                pe.wait_ge(consts, 3)

                def arguments(i, b, first):
                    pe.wait_ge(rowed[b], i * 32 + 32)
                    pe.wait_ge(gathered[b], i * (16 * GT) + 16 * GT)
                    pe.wait_ge(compared, i * RB + (b + 1))
                    if not (first and b < 2):
                        pe.wait_ge(mids, i * (2 * RB) + (b * 2 - 2))
                    for k in range(GT):
                        x = ps_x[k % 2 * D:k % 2 * D + D, b % 2, k // 2 * P:k // 2 * P + P]
                        nc.tensor.matmul(x, sent[:, b, k, 0:D], ident[:], start=True, stop=False)
                        mm = nc.tensor.matmul(x, zrow[:, b, k * D:(k + 1) * D], same[:, b % 2, k, :], start=False, stop=True)
                    mm.then_inc(summed, 1)

                def dots(i, b, first):
                    pe.wait_ge(chain, i * (3 * RB) + (3 * b + 3))
                    if not first:
                        pe.wait_ge(done, i * RB + (b - 1))
                    for kk in range(GT // 2):
                        mm = nc.tensor.matmul(ps_w[:, b % 2, 2 * kk:2 * kk + 2], qq[:, b % 2, kk * P:(kk + 1) * P], wa2[:],
                                              start=True, stop=True)
                    mm.then_inc(dotted, 1)

                def turn(i, first):
                    for b in range(RB):
                        arguments(i, b, first)
                        if not (first and b < 2):
                            dots(i if b >= 2 else i - 1, (b - 2) % RB, first and b < 4)
                turn(0, True)
                with pe.Fori(1, G // RB) as i:
                    turn(i, False)
                dots(G // RB - 1, RB - 2, False)
                dots(G // RB - 1, RB - 1, False)

            @block.scalar
            def _(act):
                nc.scalar.preload_act_table_set("natural_log_exp_and_others")
                act.wait_ge(consts, 3)

                def front(i, b, first):
                    h = b % 2
                    act.wait_ge(gathered[b], i * (16 * GT) + 16 * GT)
                    if not (first and b < 2):
                        act.wait_ge(stored[h], i * 32 + 16 * (b // 2))
                    nc.scalar.copy(pack[:, h, :].rearrange("p (k d) -> p k d", d=D), sent[:, b, :, D:2 * D]).then_inc(packed, 1)
                    act.wait_ge(bent, i * RB + (b + 1))
                    nc.scalar.activation(u[:, h, :], xc[:, h, :], ACT.Exp).then_inc(exped, 1)
                    act.wait_ge(packed, i * RB + (b + 1))
                    act.dma_start(emb_d[bass.ds(i * RB + b, 1)].rearrange("a p f -> p (a f)"), pack[:, h, :]) \
                        .then_inc(stored[h], 16)

                def back(i, b):
                    act.wait_ge(mids, i * (2 * RB) + (b * 2 + 1))
                    nc.scalar.activation(den[:, b % 2, :], tt[:, b % 2, :], ACT.Ln, bias=two[:, 0:1]).then_inc(logged, 1)
                    act.wait_ge(logged, i * RB + (b + 1))
                    nc.scalar.activation(den[:, b % 2, :], den[:, b % 2, :], ACT.Exp, scale=-1.0).then_inc(inverted, 1)

                def take(i, b):
                    act.wait_ge(dotted, i * RB + (b + 1))
                    nc.scalar.activation(logit[:, bass.ds((i * RB + b) * GT, GT)], ps_w[:, b % 2, 0:GT], ACT.Identity,
                                         bias=wab[:, 0:1]).then_inc(done, 1)

                def turn(i, first):
                    for b in range(RB):
                        front(i, b, first)
                        back(i, b)
                        if not (first and b < 3):
                            take(i if b >= 3 else i - 1, (b - 3) % RB)
                turns(act, turn)
                for b in range(1, RB):
                    take(G // RB - 1, b)
                for h in range(2):
                    act.wait_ge(stored[h], 16 * (G // 2))

            @block.vector
            def _(dve):
                nc.vector.memset(wa2[:], 0.0).then_inc(consts, 1)
                nc.vector.memset(two[:], 2.0).then_inc(consts, 1)
                for b in range(RB):
                    nc.vector.tensor_copy(idx[:, b, :], src_c[:, b * GT:(b + 1) * GT]).then_inc(fetched, 1)
                dve.wait_ge(wl, 48)
                nc.vector.tensor_scalar_mul(wa2[:], wa2[:], -1.0).then_inc(consts, 1)

                def compare(i, b, first):
                    dve.wait_ge(rowed[b], i * 32 + 32)
                    if not (first and b < 2):
                        dve.wait_ge(summed, i * RB + (b - 1))
                    nc.vector.tensor_tensor(
                        same[:, b % 2], drow[:, b, :].rearrange("p (k e) -> p k e", k=GT),
                        dst_c[:, bass.ds((i * RB + b) * GT, GT)].unsqueeze(2).to_broadcast([P, GT, P]),
                        ALU.is_equal).then_inc(compared, 1)

                def front(i, b, last):
                    dve.wait_ge(summed, i * RB + (b + 1))
                    nc.vector.tensor_scalar_min(xc[:, b % 2, :], ps_x[:, b % 2, :], 20.0).then_inc(bent, 1)
                    if not last:
                        nc.vector.tensor_copy(idx[:, b, :], src_c[:, bass.ds((i * RB + b) * GT + RB * GT, GT)]).then_inc(fetched, 1)

                def middle(i, b, first):
                    h = b % 2
                    dve.wait_ge(exped, i * RB + (b + 1))
                    m = Steps(dve, mids, turn=i, per=2 * RB, base=2 * b)
                    m.did(nc.vector.scalar_tensor_tensor(out=tt[:, h, :], in0=u[:, h, :], scalar=2.0, in1=u[:, h, :],
                                                         op0=ALU.add, op1=ALU.mult))
                    m.wait()
                    if not (first and b < 2):
                        dve.wait_ge(dotted, i * RB + (b - 1))
                    m.did(nc.vector.tensor_mul(qq[:, h, :], tt[:, h, :], ps_x[:, h, :]))

                def back(i, b):
                    h = b % 2
                    dve.wait_ge(inverted, i * RB + (b + 1))
                    dve.wait_ge(mids, i * (2 * RB) + (b * 2 + 2))
                    ct = Steps(dve, chain, turn=i, per=3 * RB, base=3 * b)
                    ct.link(nc.vector.scalar_tensor_tensor(out=tt[:, h, :], in0=tt[:, h, :], scalar=2.0, in1=den[:, h, :],
                                                           op0=ALU.add, op1=ALU.mult))
                    ct.link(nc.vector.scalar_tensor_tensor(out=tt[:, h, :], in0=tt[:, h, :], scalar=2.0, in1=den[:, h, :],
                                                           op0=ALU.subtract, op1=ALU.mult))
                    ct.did(nc.vector.tensor_mul(qq[:, h, :], qq[:, h, :], tt[:, h, :]))

                def turn(i, first, last):
                    for b in range(RB):
                        front(i, b, last)
                        if b + 1 < RB:
                            compare(i, b + 1, first)
                        elif not last:
                            compare(i + 1, 0, False)
                        if not (first and b == 0):
                            back(i if b else i - 1, (b - 1) % RB)
                        middle(i, b, first)
                compare(0, 0, True)
                turn(0, True, False)
                with dve.Fori(1, G // RB - 1) as i:
                    turn(i, False, False)
                turn(G // RB - 1, False, True)
                back(G // RB - 1, RB - 1)

    end_phase()
    NTB = -(-T // P)

    def tile_block(c0):
        return min(P, T - c0 * P)

    def lin_rows(table, c0):
        return table.rearrange("(t p) -> t p", p=P)[c0 * P:c0 * P + tile_block(c0), :]

    with ExitStack() as c:
        def sb(name, shape, dt=F32):
            return c.enter_context(nc.sbuf_tensor(name, shape, dt))
        turn_s = sb("turn_s", [P, NTB, P])
        ps_t = [c.enter_context(nc.psum_tensor(f"ps_t{q}", [P, P], F32)) for q in range(2)]
        dl, dp, dn, lin = (sb(n, [P, T]) for n in ("dl", "dp", "dn", "lin"))
        cont, nxt, is_end, gap = (sb(n, [P, T]) for n in ("cont", "nxt", "is_end", "gap"))
        run, ends_v, segmax, expo = (sb(n, [P, T]) for n in ("run", "ends_v", "segmax", "expo"))
        gate = sb("gate", [P, 3])
        row_s = sb("row_s", [1, 2, P])
        carry_r = sb("carry_r", [1, P + 1])
        carry_c = sb("carry_c", [P, 1])
        one = sb("one", [1, 1])
        ps_g = c.enter_context(nc.psum_tensor("ps_g", [1, 2, P], F32))
        ps_c1 = c.enter_context(nc.psum_tensor("ps_c1", [P, 1], F32))
        turned, moved, st, ld, vs, pe_row, pe_col, ex, wst, wld, back_t = (
            sem(n) for n in ("m_turned", "m_moved", "m_store", "m_load", "m_dve", "m_row", "m_col", "m_exp", "m_wst", "m_wld",
                             "m_back"))
        ask_row, ask_col, w_ready = sem("m_askrow"), sem("m_askcol"), sem("m_wready")
        border = [(run[:, T - 1:T], gate[:, 0:1], carry_r[:, 0:P]), (segmax[:, 0:1], gate[:, 2:3], carry_r[:, 1:P + 1]),
                  (run[:, T - 1:T], gate[:, 1:2], carry_r[:, 0:P]), (segmax[:, 0:1], gate[:, 2:3], carry_r[:, 1:P + 1])]
        with nc.Block() as block:
            @block.tensor
            def _(pe):
                for c0 in range(NTB):
                    w = tile_block(c0)
                    if c0 >= 2:
                        pe.wait_ge(moved, c0 - 1)
                    nc.tensor.transpose(ps_t[c0 % 2][0:w, :], logit[:, c0 * P:c0 * P + w], ident[:]).then_inc(turned, 1)
                for n in range(4):
                    pe.wait_ge(ask_row, n + 1)
                    nc.tensor.matmul(ps_g[:, 0, :], border[n][0], ident[:], start=True, stop=True)
                    nc.tensor.matmul(ps_g[:, 1, :], border[n][1], ident[:], start=True, stop=True).then_inc(pe_row, 1)
                    pe.wait_ge(ask_col, n + 1)
                    nc.tensor.matmul(ps_c1[:], border[n][2], one[:], start=True, stop=True).then_inc(pe_col, 1)
                pe.wait_ge(moved, NTB)
                for c0 in range(NTB):
                    w = tile_block(c0)
                    pe.wait_ge(wld, 16 * NTB)
                    if c0 >= 2:
                        pe.wait_ge(back_t, c0 - 1)
                    nc.tensor.transpose(ps_t[c0 % 2][:, 0:w], turn_s[0:w, c0, :], ident[0:w, 0:w]).then_inc(turned, 1)

            @block.sync
            def _(sp):
                for c0 in range(NTB):
                    sp.wait_ge(moved, c0 + 1)
                    sp.dma_start(lin_rows(lin_d, c0), turn_s[0:tile_block(c0), c0, :]).then_inc(st, 16)
                sp.dma_start(dl[:], dstf_d[1:EP + 1].rearrange("(p j) -> p j", p=P)).then_inc(ld, 16)
                sp.dma_start(dp[:], dstf_d[0:EP].rearrange("(p j) -> p j", p=P)).then_inc(ld, 16)
                sp.dma_start(dn[:], dstf_d[2:EP + 2].rearrange("(p j) -> p j", p=P)).then_inc(ld, 16)
                sp.wait_ge(st, 16 * NTB)
                sp.dma_start(lin[:], lin_d.rearrange("(p j) -> p j", p=P)).then_inc(ld, 16)
                sp.wait_ge(w_ready, 1)
                sp.dma_start(wgt_d.rearrange("(p j) -> p j", p=P), run[:]).then_inc(wst, 16)
                sp.wait_ge(wst, 16)
                for c0 in range(NTB):
                    sp.dma_start(turn_s[0:tile_block(c0), c0, :], lin_rows(wgt_d, c0)).then_inc(wld, 16)

            @block.scalar
            def _(act):
                for c0 in range(NTB):
                    act.wait_ge(turned, c0 + 1)
                    w = tile_block(c0)
                    nc.scalar.copy(turn_s[0:w, c0, :], ps_t[c0 % 2][0:w, :]).then_inc(moved, 1)
                act.wait_ge(ex, 1)
                nc.scalar.activation(expo[:], lin[:], ACT.Exp).then_inc(ex, 1)
                for c0 in range(NTB):
                    w = tile_block(c0)
                    act.wait_ge(turned, NTB + c0 + 1)
                    nc.scalar.copy(logit[:, c0 * P:c0 * P + w], ps_t[c0 % 2][:, 0:w]).then_inc(back_t, 1)

            @block.vector
            def _(dve):
                s = Steps(dve, vs)
                s.did(nc.vector.memset(one[:], 1.0))
                dve.wait_ge(ld, 64)
                s.did(nc.vector.tensor_tensor(cont[:], dl[:], dp[:], ALU.is_equal))
                s.link(nc.vector.tensor_tensor(nxt[:], dl[:], dn[:], ALU.is_equal))
                s.did(nc.vector.tensor_scalar(gap[:], cont[:], -1.0, BIG, ALU.add, ALU.mult))
                s.link(nc.vector.tensor_scalar(is_end[:], nxt[:], -1.0, 1.0, ALU.mult, ALU.add))
                s.did(nc.vector.tensor_reduce(gate[:, 0:1], gap[:], AX_X, ALU.min))
                s.did(nc.vector.tensor_reduce(gate[:, 1:2], cont[:], AX_X, ALU.min))
                s.link(nc.vector.tensor_reduce(gate[:, 2:3], nxt[:], AX_X, ALU.min))

                def scan(n, out, g, v, start, op0, op1, reverse):
                    def way(ap):
                        return ap[:, ::-1] if reverse else ap[:]
                    s.link(nc.vector.tensor_tensor_scan(way(out), way(g), way(v), start, op0, op1))
                    dve.sem_inc(ask_row, 1)
                    dve.wait_ge(pe_row, n + 1)
                    s.did(nc.vector.memset(carry_r[:], start))
                    s.link(nc.vector.tensor_copy(row_s[:], ps_g[:]))
                    dst = carry_r[:, P - 1::-1] if reverse else carry_r[:, 1:P + 1]
                    s.link(nc.vector.tensor_tensor_scan(dst, way(row_s[:, 1, :]), way(row_s[:, 0, :]), start, op0, op1))
                    dve.sem_inc(ask_col, 1)
                    dve.wait_ge(pe_col, n + 1)
                    s.link(nc.vector.tensor_copy(carry_c[:], ps_c1[:]))
                    s.link(nc.vector.tensor_tensor_scan(way(out), way(g), way(v), carry_c[:, 0:1], op0, op1))

                scan(0, run, gap, lin, -BIG, ALU.add, ALU.max, False)
                s.link(nc.vector.tensor_mul(ends_v[:], run[:], is_end[:]))
                scan(1, segmax, nxt, ends_v, 0.0, ALU.mult, ALU.add, True)
                s.link(nc.vector.tensor_sub(lin[:], lin[:], segmax[:]))
                dve.sem_inc(ex, 1)
                dve.wait_ge(ex, 2)
                scan(2, run, cont, expo, 0.0, ALU.mult, ALU.add, False)
                s.link(nc.vector.tensor_mul(ends_v[:], run[:], is_end[:]))
                scan(3, segmax, nxt, ends_v, 0.0, ALU.mult, ALU.add, True)
                s.link(nc.vector.reciprocal(segmax[:], segmax[:]))
                s.link(nc.vector.tensor_mul(run[:], expo[:], segmax[:]))
                dve.sem_inc(w_ready, 1)

    end_phase()
    with ExitStack() as c:
        def sb(name, shape, dt=F32):
            return c.enter_context(nc.sbuf_tensor(name, shape, dt))
        drow = sb("w_drow", [P, RB, GE])
        emb = sb("w_emb", [P, RB, GT * D])
        same = sb("w_same", [P, RB, GT, P])
        part = sb("w_part", [P, RB, GT * D])
        ps_p = c.enter_context(nc.psum_tensor("ps_p", [P, RB, 512], F32))
        loaded = [sem(f"w_load{b}") for b in range(RB)]
        stored = [sem(f"w_st{b}") for b in range(RB)]
        weighed, summed, moved = sem("w_weighed"), sem("w_summed"), sem("w_moved")

        with nc.Block() as block:
            @block.sync
            def _(sp):
                def turn(i, first):
                    for b in range(RB):
                        g = i * RB + b
                        if not first:
                            sp.wait_ge(summed, i * RB + (b + 1 - RB))
                        sp.dma_start(drow[:, b, :], dst_rows(g)).then_inc(loaded[b], 16)
                        sp.dma_start(emb[:, b, :], emb_d[bass.ds(g, 1)].rearrange("a p f -> p (a f)")).then_inc(loaded[b], 16)
                turns(sp, turn)

            @block.vector
            def _(dve):
                def turn(i, first):
                    for b in range(RB):
                        dve.wait_ge(loaded[b], i * 32 + 32)
                        if not first:
                            dve.wait_ge(summed, i * RB + (b + 1 - RB))
                        for k in range(GT):
                            col = bass.ds((i * RB + b) * GT + k, 1)
                            last = nc.vector.tensor_scalar(same[:, b, k, :], drow[:, b, k * P:(k + 1) * P], dst_c[:, col],
                                                           logit[:, col], ALU.is_equal, ALU.mult)
                        last.then_inc(weighed, 1)
                turns(dve, turn)

            @block.tensor
            def _(pe):
                def turn(i, first):
                    for b in range(RB):
                        pe.wait_ge(weighed, i * RB + (b + 1))
                        if not first:
                            pe.wait_ge(moved, i * RB + (b + 1 - RB))
                        for k in range(GT):
                            mm = nc.tensor.matmul(ps_p[:, b, k * D:(k + 1) * D], same[:, b, k, :], emb[:, b, k * D:(k + 1) * D],
                                                  start=True, stop=True)
                        mm.then_inc(summed, 1)
                turns(pe, turn)

            @block.scalar
            def _(act):
                def turn(i, first):
                    for b in range(RB):
                        act.wait_ge(summed, i * RB + (b + 1))
                        if not first:
                            act.wait_ge(stored[b], i * 16)
                        nc.scalar.copy(part[:, b, :], ps_p[:, b, :]).then_inc(moved, 1)
                        act.wait_ge(moved, i * RB + (b + 1))
                        act.dma_start(part_rows(part_d, i * RB + b), part[:, b, :]).then_inc(stored[b], 16)
                turns(act, turn)
                for b in range(RB):
                    act.wait_ge(stored[b], 16 * (G // RB))
    end_phase()
    logit_scope.close()

    def close1(s):
        s.link(nc.vector.tensor_add(x_sb[:], x_sb[:], y_sb[:]))
    collect("c1", close1)

    def sage_fill(n):
        def fill(sp, wcat, wl, extra):
            sp.dma_start(wcat[0:D, :], a[f"L2_gnn_w_self{n}"]).then_inc(wl, 16)
            sp.dma_start(wcat[D:D + 1, :], a[f"L2_gnn_b_self{n}"].rearrange("(a n) -> a n", a=1)).then_inc(wl, 16)
            return 2
        return fill

    def sage(n):
        node_product(f"s{n}", D, sage_fill(n), local=[(slice(0, D), y_sb)])
        sweep(True, f"L2_gnn_w_s2d{n}", half_in, True)
        sweep(False, f"L2_gnn_w_d2s{n}", half_out, True)

    def half_biases(s, rows):
        s.link(nc.vector.tensor_add(rows[:, 0, :], rows[:, 0, :], rows[:, 1, :]))
        s.link(nc.vector.tensor_scalar_mul(rows[:, 0, :], rows[:, 0, :], 0.5))
        s.link(nc.vector.tensor_add(y_sb[:], y_sb[:], along(rows[:, 0, :])))

    def between2(s, rows):
        half_biases(s, rows)
        s.link(nc.vector.tensor_scalar_max(h_sb[:], y_sb[:], 0.0))
        split(s)

    def close2(s, rows):
        half_biases(s, rows)
        s.link(nc.vector.tensor_add(x_sb[:], x_sb[:], y_sb[:]))
    norm_phase("2", None, True)
    sage(1)
    bias_phase("2a", ["L2_gnn_b_s2d1", "L2_gnn_b_d2s1"], between2)
    sage(2)
    bias_phase("2b", ["L2_gnn_b_s2d2", "L2_gnn_b_d2s2"], close2)

    norm_phase("3", None, False)

    def hidden_fill(sp, wcat, wl, extra):
        sp.dma_start(wcat[0:D, :], a["L3_gnn_W1n"]).then_inc(wl, 16)
        sp.dma_start(wcat[D:D + 1, :], a["L3_gnn_b1n"].rearrange("(a n) -> a n", a=1)).then_inc(wl, 16)
        return 2
    node_product("n3", D, hidden_fill, stores=[(slice(0, D), xt_d)], hidden=True)

    with ExitStack() as c:
        def sb(name, shape, dt=F32):
            return c.enter_context(nc.sbuf_tensor(name, shape, dt))
        idx = sb("x_idx", [P, RB, GT], I32)
        xg = sb("x_rows", [P, RB, GT, D])
        dst2 = sb("x_dst2", [2, RB, GE], BF16)
        ones2 = sb("x_ones2", [2, P], BF16)
        gates = sb("x_gates", [P, RB, GT * D])
        same = sb("x_same", [P, RB, GT, P])
        msg = sb("x_msg", [P, RB, GT * D])
        part = sb("x_part", [P, RB, GT * D])
        ps_d = c.enter_context(nc.psum_tensor("ps_d3", [P, 2, 2, 512], F32))
        ps_p = c.enter_context(nc.psum_tensor("ps_p3", [P, RB, 512], F32))
        gathered = [sem(f"x_gat{b}", keep=True) for b in range(RB)]
        rowed = [sem(f"x_row{b}") for b in range(RB)]
        loaded = [sem(f"x_load{b}") for b in range(RB)]
        stored = [sem(f"x_st{b}") for b in range(RB)]
        const, spread, fetched, compared, msgs, summed, moved = (
            sem(n) for n in ("x_const", "x_spread", "x_idx_s", "x_same_s", "x_msgs", "x_sum", "x_moved"))
        with nc.Block() as block:
            @block.sync
            def _(sp):
                def turn(i, first):
                    for b in range(RB):
                        g = i * RB + b
                        if not first:
                            sp.wait_ge(compared, i * RB + (b + 1 - RB))
                        sp.dma_start(dst2[:, b, :], dst2_d[:, bass.ds(g * GE, GE)]).then_inc(rowed[b], 16)
                        if not first:
                            sp.wait_ge(msgs, i * RB + (b + 1 - RB))
                        sp.dma_start(gates[:, b, :], gate_d[bass.ds(g, 1)].rearrange("a p f -> p (a f)")).then_inc(loaded[b], 16)
                turns(sp, turn)

            @block.gpsimd
            def _(pool):
                def turn(i, first):
                    for b in range(RB):
                        pool.wait_ge(fetched, i * RB + (b + 1))
                        pool.nop(nofuse=True)
                        if not first:
                            pool.wait_ge(msgs, i * RB + (b + 1 - RB))
                            pool.nop(nofuse=True)
                        for k in range(GT):
                            nc.gpsimd.indirect_dma_start(
                                xg[:, b, k, :], None, xt_d,
                                bass.IndirectOffsetOnAxis(ap=idx[:, b, k:k + 1], axis=0)).then_inc(gathered[b], 16)
                turns(pool, turn)

            @block.vector
            def _(dve):
                nc.vector.memset(ones2[:], 1.0).then_inc(const, 1)
                for b in range(RB):
                    nc.vector.tensor_copy(idx[:, b, :], src_c[:, b * GT:(b + 1) * GT]).then_inc(fetched, 1)

                def turn(i, first, last=False):
                    for b in range(RB):
                        g = i * RB + b
                        dve.wait_ge(spread, i * RB + (b + 1))
                        if not first:
                            dve.wait_ge(summed, i * RB + (b + 1 - RB))
                        nc.vector.tensor_tensor(
                            same[:, b], ps_d[:, b % 2].rearrange("p h (k e) -> p (h k) e", e=P),
                            dst_c[:, bass.ds(g * GT, GT)].unsqueeze(2).to_broadcast([P, GT, P]),
                            ALU.is_equal).then_inc(compared, 1)
                        dve.wait_ge(gathered[b], i * (16 * GT) + 16 * GT)
                        if not last:
                            nc.vector.tensor_copy(idx[:, b, :], src_c[:, bass.ds((g + RB) * GT, GT)]).then_inc(fetched, 1)
                        dve.wait_ge(loaded[b], i * 16 + 16)
                        nc.vector.tensor_mul(msg[:, b, :], gates[:, b, :], xg[:, b].rearrange("p k d -> p (k d)")) \
                            .then_inc(msgs, 1)
                turn(0, True)
                with dve.Fori(1, G // RB - 1) as i:
                    turn(i, False)
                turn(G // RB - 1, False, True)

            @block.tensor
            def _(pe):
                pe.wait_ge(const, 1)

                def spread_dst(i, b, first):
                    pe.wait_ge(rowed[b], i * 16 + 16)
                    if not (first and b < 2):
                        pe.wait_ge(compared, i * RB + (b - 1))
                    for half in range(2):
                        mm = nc.tensor.matmul(ps_d[:, b % 2, half, :], ones2[:], dst2[:, b, half * 512:(half + 1) * 512],
                                              start=True, stop=True)
                    mm.then_inc(spread, 1)

                def sums(i, b, first):
                    pe.wait_ge(msgs, i * RB + (b + 1))
                    pe.wait_ge(compared, i * RB + (b + 1))
                    if not first:
                        pe.wait_ge(moved, i * RB + (b + 1 - RB))
                    for k in range(GT):
                        mm = nc.tensor.matmul(ps_p[:, b, k * D:(k + 1) * D], same[:, b, k, :], msg[:, b, k * D:(k + 1) * D],
                                              start=True, stop=True)
                    mm.then_inc(summed, 1)

                def turn(i, first):
                    for b in range(RB):
                        spread_dst(i, b, first)
                        if not (first and b == 0):
                            sums(i if b else i - 1, (b - 1) % RB, first)
                turns(pe, turn)
                sums(G // RB - 1, RB - 1, False)

            @block.scalar
            def _(act):
                def turn(i, first):
                    for b in range(RB):
                        act.wait_ge(summed, i * RB + (b + 1))
                        if not first:
                            act.wait_ge(stored[b], i * 16)
                        nc.scalar.copy(part[:, b, :], ps_p[:, b, :]).then_inc(moved, 1)
                        act.wait_ge(moved, i * RB + (b + 1))
                        act.dma_start(part_rows(part_d, i * RB + b), part[:, b, :]).then_inc(stored[b], 16)
                turns(act, turn)
                for b in range(RB):
                    act.wait_ge(stored[b], 16 * (G // RB))

    end_phase()
    with ExitStack() as c:
        rows = c.enter_context(nc.sbuf_tensor("rows3", [P, 2, D], F32))
        res = c.enter_context(nc.sbuf_tensor("res3", [P, 1], F32))
        mean, var, std, rstd = (c.enter_context(nc.sbuf_tensor(n, [P, NT], F32)) for n in ("mean4", "var4", "std4", "rstd4"))
        wl = sem("f_w", keep=True)
        with nc.Block() as block:
            @block.sync
            def _(sp):
                sp.dma_start(rows[:, 0, :], row_of("L3_gnn_gamma")).then_inc(wl, 16)
                sp.dma_start(rows[:, 1, :], row_of("L3_gnn_beta")).then_inc(wl, 16)
                sp.dma_start(res[:], row_of("L3_gnn_res_w", 1)).then_inc(wl, 16)
                sp.wait_ge(wl, 48)
        def close3(s):
            s.link(nc.vector.scalar_tensor_tensor(out=h_sb[:].rearrange("p t d -> p (t d)"),
                                                  in0=y_sb[:].rearrange("p t d -> p (t d)"), scalar=res[:, 0:1],
                                                  in1=h_sb[:].rearrange("p t d -> p (t d)"), op0=ALU.mult, op1=ALU.add))
            s.link(nc.vector.tensor_reduce(mean[:], h_sb[:], AX_X, ALU.add))
            s.link(nc.vector.tensor_scalar_mul(mean[:], mean[:], 1.0 / D))
            s.link(nc.vector.tensor_sub(h_sb[:], h_sb[:], each(mean[:])))
            s.link(nc.vector.tensor_mul(t_sb[:], h_sb[:], h_sb[:]))
            s.link(nc.vector.tensor_reduce(var[:], t_sb[:], AX_X, ALU.add))
            s.link(nc.vector.tensor_scalar(var[:], var[:], 1.0 / D, EPS, ALU.mult, ALU.add))
        collect("c3", close3)
        done, vs, rooted = sem("f_done"), sem("f_dve"), sem("f_root")
        full = N_NODES // P
        with nc.Block() as block:
            @block.scalar
            def _(act):
                nc.scalar.sqrt(std[:], var[:]).then_inc(rooted, 1)

            @block.vector
            def _(dve):
                s = Steps(dve, vs)
                dve.wait_ge(rooted, 1)
                s.link(nc.vector.reciprocal(rstd[:], std[:]))
                s.link(nc.vector.tensor_mul(h_sb[:], h_sb[:], each(rstd[:])))
                s.link(nc.vector.tensor_mul(h_sb[:], h_sb[:], along(rows[:, 0, :])))
                s.link(nc.vector.tensor_add(h_sb[:], h_sb[:], along(rows[:, 1, :])))
                s.link(nc.vector.tensor_add(x_sb[:], x_sb[:], h_sb[:]))
                dve.sem_inc(done, 1)

            @block.sync
            def _(sp):
                sp.wait_ge(done, 1)
                sp.dma_start(out[0:full * P, :].rearrange("(t p) d -> p t d", p=P), x_sb[:, 0:full, :]).then_inc(wl, 16)
                sp.dma_start(out[full * P:N_NODES, :], x_sb[0:N_NODES - full * P, full, :]).then_inc(wl, 16)
                sp.wait_ge(wl, 48 + 32)
    passing["scope"].close()
    top.close()


def layout(inputs):
    import numpy as np

    arrays = {k: np.ascontiguousarray(v) for k, v in inputs.items() if k.startswith("L")}
    x = np.zeros((NP, D), np.float32)
    x[:N_NODES] = inputs["x"]
    arrays["x"] = x
    order = np.arange(EP - E_EDGES, dtype=np.int32)
    pad = order % (NP - N_NODES) + N_NODES
    pad_dst = order * (NP - N_NODES) // (EP - E_EDGES) + N_NODES
    src = np.concatenate([np.asarray(inputs["src"]), pad])
    dst = np.concatenate([np.asarray(inputs["dst"]), pad_dst])
    for name, v in (("src", src), ("dst", dst)):
        arrays[f"{name}_lin"] = v.reshape(P, T)
        arrays[f"{name}_col"] = np.ascontiguousarray(v.reshape(T, P).T)
    attr = np.zeros((DE, EP), np.float32)
    attr[:, :E_EDGES] = np.asarray(inputs["edge_attr_32"]).T
    arrays["attr_T"] = attr
    arrays["L1_We_T"] = np.ascontiguousarray(
        np.concatenate([np.asarray(inputs["L1_gnn_We_k"]).reshape(D, D), np.asarray(inputs["L1_gnn_We_b"])]).T)
    return arrays


def kernel(**inputs):
    import concourse.bacc as _bacc
    from concourse.bass_utils import run_bass_kernel_spmd as _run

    nc = _bacc.Bacc("TRN2", target_bir_lowering=False, num_devices=1)
    arrays, aps = {}, {}
    for name, v in layout(inputs).items():
        arrays[f"in_{name}_dram"] = v
        aps[name] = nc.dram_tensor(f"in_{name}_dram", v.shape, mybir.dt.from_np(v.dtype), kind="ExternalInput").ap()
    out = nc.dram_tensor("out_dram", (N_NODES, D), F32, kind="ExternalOutput").ap()
    build_program(nc, aps, out)
    r = _run(nc, [arrays], core_ids=[0])
    return r.results[0]["out_dram"]
```
